# Optimizing a Trainium2 kernel written in Bass

```python
import numpy as np
import jax
import jax.numpy as jnp

def _softmax(x, axis=-1):
    return jax.nn.softmax(x, axis=axis)

def _gelu(x):
    return jax.nn.gelu(x, approximate=True)

def _silu(x):
    return jax.nn.silu(x)

def _sigmoid(x):
    return jax.nn.sigmoid(x)

def _layernorm(x, axis=-1, eps=1e-05):
    m = jnp.mean(x, axis=axis, keepdims=True)
    v = jnp.var(x, axis=axis, keepdims=True)
    return (x - m) / jnp.sqrt(v + eps)

def _scatter_add(tgt, idx, src, axis=0):
    return tgt.at[idx].add(src)

def _segment_sum(src, seg, n):
    return jax.ops.segment_sum(src, seg, n)
kernel_name = 'mk_decoder_preln_d1_seqx_r8_eb07d1'

def setup_inputs(seed: int=0):
    np.random.seed(seed)
    _w = jnp.asarray

    def _rec_inputs():
        import jax
        import jax.numpy as jnp
        _rk = jax.random.key(seed)
        x = -0.0002928 + 1 * jax.random.normal(jax.random.fold_in(_rk, 1), (4, 256, 256), jnp.float32)
        _lenS = 256 - jax.random.randint(jax.random.fold_in(_rk, 7), (4,), 0, max(1, 256 // 4) + 1, jnp.int32)
        _lenS2 = 512 - jax.random.randint(jax.random.fold_in(_rk, 8), (4,), 0, max(1, 512 // 4) + 1, jnp.int32)
        _ctx_2048P = jax.random.normal(jax.random.fold_in(_rk, 11), (4, 16, 256), jnp.float32)
        _ctx_2048c = jax.random.dirichlet(jax.random.fold_in(_rk, 511), 0.3 * jnp.ones((16,), jnp.float32), (4, 512))
        _ctx_2048t = jnp.einsum('bsk,bkd->bsd', _ctx_2048c, _ctx_2048P)
        _ctx_2048t = _ctx_2048t * jax.lax.rsqrt(jnp.mean(jnp.square(_ctx_2048t)) + 1e-12) * 0.953939
        ctx_2048 = 4.13588e-05 + 0.999923 * (_ctx_2048t + 0.3 * jax.random.normal(jax.random.fold_in(_rk, 611), (4, 512, 256), jnp.float32))
        _validS = jnp.arange(256)[None, :] < _lenS[:, None]
        _validS2 = jnp.arange(512)[None, :] < _lenS2[:, None]
        _causal = jnp.tril(jnp.ones((256, 256), dtype=bool))
        mask_1xSxS2_ff0 = jnp.where(jnp.ones((1, 256, 512), dtype=bool), 0.0, -1000000000.0).astype(jnp.float32)
        return (x, ctx_2048, mask_1xSxS2_ff0)
    x, ctx_2048, mask_1xSxS2_ff0 = _rec_inputs()

    def _L0_attn_setup():
        import jax, jax.numpy as jnp
        import numpy as np
        B, T, D_MODEL, N_HEAD, D_C = (2, 256, 256, 16, 64)
        D_HEAD = D_MODEL // N_HEAD
        D_ROPE = D_C // N_HEAD

        def _rope(x):
            t, d = (x.shape[2], x.shape[-1])
            freqs = 10000.0 ** (-(jnp.arange(0, d, 2, dtype=jnp.float32) / d))
            theta = jnp.arange(t, dtype=jnp.float32)[:, None] * freqs[None, :]
            cos, sin = (jnp.cos(theta), jnp.sin(theta))
            x1, x2 = (x[..., ::2], x[..., 1::2])
            return jnp.concatenate([x1 * cos - x2 * sin, x1 * sin + x2 * cos], axis=-1)

        def _heads(x):
            b, t, _ = x.shape
            return x.reshape(b, t, N_HEAD, -1).transpose(0, 2, 1, 3)
        key = jax.random.key(seed)
        ks = jax.random.split(key, 16)
        s = 0.02
        return {'x': jax.random.normal(ks[0], (B, T, D_MODEL), jnp.float32), 'W_DKV': jax.random.normal(ks[1], (D_MODEL, D_C), jnp.float32) * s, 'b_DKV': jnp.zeros((D_C,), jnp.float32), 'W_UK': jax.random.normal(ks[2], (D_C, D_MODEL), jnp.float32) * s, 'b_UK': jnp.zeros((D_MODEL,), jnp.float32), 'W_UV': jax.random.normal(ks[3], (D_C, D_MODEL), jnp.float32) * s, 'b_UV': jnp.zeros((D_MODEL,), jnp.float32), 'W_DQ': jax.random.normal(ks[4], (D_MODEL, D_C), jnp.float32) * s, 'b_DQ': jnp.zeros((D_C,), jnp.float32), 'W_UQ': jax.random.normal(ks[5], (D_C, D_MODEL), jnp.float32) * s, 'b_UQ': jnp.zeros((D_MODEL,), jnp.float32), 'W_QR': jax.random.normal(ks[6], (D_C, D_C), jnp.float32) * s, 'b_QR': jnp.zeros((D_C,), jnp.float32), 'W_KR': jax.random.normal(ks[7], (D_MODEL, D_C), jnp.float32) * s, 'b_KR': jnp.zeros((D_C,), jnp.float32)}
    _L0_attn_all = _L0_attn_setup()
    _L0_attn_in = {k: v for k, v in _L0_attn_all.items() if k in ('W_DKV', 'b_DKV', 'W_UK', 'b_UK', 'W_UV', 'b_UV', 'W_DQ', 'b_DQ', 'W_UQ', 'b_UQ', 'W_QR', 'b_QR', 'W_KR', 'b_KR')}
    del _L0_attn_all

    def _L0_xattn_setup():
        import jax, jax.numpy as jnp
        import numpy as np
        H = 256
        NH = 16
        NKV = 4
        HD = 128
        GROUPS = NH // NKV
        EPS = 1e-06
        B, S, SE = (1, 256, 512)

        def _rmsnorm(x, w, eps=EPS):
            xf = x.astype(jnp.float32)
            var = jnp.mean(xf * xf, axis=-1, keepdims=True)
            return (xf * jax.lax.rsqrt(var + eps)).astype(x.dtype) * w
        key = jax.random.key(seed)
        ks = jax.random.split(key, 12)
        sc = 0.02
        return {'hidden_states': jax.random.normal(ks[0], (B, S, H), jnp.float32), 'encoder_hidden_states': jax.random.normal(ks[1], (B, SE, H), jnp.float32), 'attention_mask': jnp.zeros((B, S, SE), jnp.float32), 'Wq': jax.random.normal(ks[2], (H, NH * HD), jnp.float32) * sc, 'bq': jax.random.normal(ks[3], (NH * HD,), jnp.float32) * sc, 'Wk': jax.random.normal(ks[4], (H, NKV * HD), jnp.float32) * sc, 'bk': jax.random.normal(ks[5], (NKV * HD,), jnp.float32) * sc, 'Wv': jax.random.normal(ks[6], (H, NKV * HD), jnp.float32) * sc, 'bv': jax.random.normal(ks[7], (NKV * HD,), jnp.float32) * sc, 'Wo': jax.random.normal(ks[8], (NH * HD, H), jnp.float32) * sc, 'qn_w': jnp.ones((HD,), jnp.float32), 'kn_w': jnp.ones((HD,), jnp.float32)}
    _L0_xattn_all = _L0_xattn_setup()
    _L0_xattn_in = {k: v for k, v in _L0_xattn_all.items() if k in ('Wq', 'bq', 'Wk', 'bk', 'Wv', 'bv', 'Wo', 'qn_w', 'kn_w')}
    del _L0_xattn_all

    def _L0_ffn_setup():
        import jax, jax.numpy as jnp
        import numpy as np
        DIM = 256
        INTER = 176
        N_ROUTED = 15
        TOPK = 2
        SHARED_INTER = 176

        def _swiglu(x, wa, wb, wo):
            return jax.nn.silu(x @ wa.T) * (x @ wb.T) @ wo.T
        key = jax.random.key(seed)
        ks = jax.random.split(key, 8)
        s = 0.02
        return {'x': jax.random.normal(ks[0], (2, 256, DIM), dtype=jnp.float32), 'gate_w': jax.random.normal(ks[1], (N_ROUTED, DIM), dtype=jnp.float32) * s, 'w1': jax.random.normal(ks[2], (N_ROUTED, INTER, DIM), dtype=jnp.float32) * s, 'w3': jax.random.normal(ks[3], (N_ROUTED, INTER, DIM), dtype=jnp.float32) * s, 'w2': jax.random.normal(ks[4], (N_ROUTED, DIM, INTER), dtype=jnp.float32) * s, 'sw1': jax.random.normal(ks[5], (SHARED_INTER, DIM), dtype=jnp.float32) * s, 'sw3': jax.random.normal(ks[6], (SHARED_INTER, DIM), dtype=jnp.float32) * s, 'sw2': jax.random.normal(ks[7], (DIM, SHARED_INTER), dtype=jnp.float32) * s}
    _L0_ffn_all = _L0_ffn_setup()
    _L0_ffn_in = {k: v for k, v in _L0_ffn_all.items() if k in ('gate_w', 'w1', 'w2', 'w3', 'sw1', 'sw2', 'sw3')}
    del _L0_ffn_all
    return {'x': x, 'ctx_2048': ctx_2048, 'mask_1xSxS2_ff0': mask_1xSxS2_ff0, 'L0_attn_W_DKV': _L0_attn_in['W_DKV'], 'L0_attn_b_DKV': _L0_attn_in['b_DKV'], 'L0_attn_W_UK': _L0_attn_in['W_UK'], 'L0_attn_b_UK': _L0_attn_in['b_UK'], 'L0_attn_W_UV': _L0_attn_in['W_UV'], 'L0_attn_b_UV': _L0_attn_in['b_UV'], 'L0_attn_W_DQ': _L0_attn_in['W_DQ'], 'L0_attn_b_DQ': _L0_attn_in['b_DQ'], 'L0_attn_W_UQ': _L0_attn_in['W_UQ'], 'L0_attn_b_UQ': _L0_attn_in['b_UQ'], 'L0_attn_W_QR': _L0_attn_in['W_QR'], 'L0_attn_b_QR': _L0_attn_in['b_QR'], 'L0_attn_W_KR': _L0_attn_in['W_KR'], 'L0_attn_b_KR': _L0_attn_in['b_KR'], 'L0_xattn_Wq': _L0_xattn_in['Wq'], 'L0_xattn_bq': _L0_xattn_in['bq'], 'L0_xattn_Wk': _L0_xattn_in['Wk'], 'L0_xattn_bk': _L0_xattn_in['bk'], 'L0_xattn_Wv': _L0_xattn_in['Wv'], 'L0_xattn_bv': _L0_xattn_in['bv'], 'L0_xattn_Wo': _L0_xattn_in['Wo'], 'L0_xattn_qn_w': _L0_xattn_in['qn_w'], 'L0_xattn_kn_w': _L0_xattn_in['kn_w'], 'L0_ffn_gate_w': _L0_ffn_in['gate_w'], 'L0_ffn_w1': _L0_ffn_in['w1'], 'L0_ffn_w2': _L0_ffn_in['w2'], 'L0_ffn_w3': _L0_ffn_in['w3'], 'L0_ffn_sw1': _L0_ffn_in['sw1'], 'L0_ffn_sw2': _L0_ffn_in['sw2'], 'L0_ffn_sw3': _L0_ffn_in['sw3']}

def reference(x, ctx_2048, mask_1xSxS2_ff0, L0_attn_W_DKV, L0_attn_b_DKV, L0_attn_W_UK, L0_attn_b_UK, L0_attn_W_UV, L0_attn_b_UV, L0_attn_W_DQ, L0_attn_b_DQ, L0_attn_W_UQ, L0_attn_b_UQ, L0_attn_W_QR, L0_attn_b_QR, L0_attn_W_KR, L0_attn_b_KR, L0_xattn_Wq, L0_xattn_bq, L0_xattn_Wk, L0_xattn_bk, L0_xattn_Wv, L0_xattn_bv, L0_xattn_Wo, L0_xattn_qn_w, L0_xattn_kn_w, L0_ffn_gate_w, L0_ffn_w1, L0_ffn_w2, L0_ffn_w3, L0_ffn_sw1, L0_ffn_sw2, L0_ffn_sw3):
    import jax
    import jax.numpy as jnp

    def _L0_attn_ref(x, W_DKV, b_DKV, W_UK, b_UK, W_UV, b_UV, W_DQ, b_DQ, W_UQ, b_UQ, W_QR, b_QR, W_KR, b_KR):
        import jax, jax.numpy as jnp
        import numpy as np
        B, T, D_MODEL, N_HEAD, D_C = (2, 256, 256, 16, 64)
        D_HEAD = D_MODEL // N_HEAD
        D_ROPE = D_C // N_HEAD

        def _rope(x):
            t, d = (x.shape[2], x.shape[-1])
            freqs = 10000.0 ** (-(jnp.arange(0, d, 2, dtype=jnp.float32) / d))
            theta = jnp.arange(t, dtype=jnp.float32)[:, None] * freqs[None, :]
            cos, sin = (jnp.cos(theta), jnp.sin(theta))
            x1, x2 = (x[..., ::2], x[..., 1::2])
            return jnp.concatenate([x1 * cos - x2 * sin, x1 * sin + x2 * cos], axis=-1)

        def _heads(x):
            b, t, _ = x.shape
            return x.reshape(b, t, N_HEAD, -1).transpose(0, 2, 1, 3)
        b, t, _ = x.shape
        c_kv = x @ W_DKV + b_DKV
        k_content = _heads(c_kv @ W_UK + b_UK)
        v = _heads(c_kv @ W_UV + b_UV)
        c_q = x @ W_DQ + b_DQ
        q_content = _heads(c_q @ W_UQ + b_UQ)
        q_rope = _rope(_heads(c_q @ W_QR + b_QR))
        k_rope = _rope(_heads(x @ W_KR + b_KR))
        Q = jnp.concatenate([q_content, q_rope], axis=-1)
        K = jnp.concatenate([k_content, k_rope], axis=-1)
        scale = 1.0 / jnp.sqrt(jnp.float32(Q.shape[-1]))
        scores = jnp.einsum('bhqd,bhkd->bhqk', Q, K) * scale
        probs = jax.nn.softmax(scores, axis=-1)
        out = jnp.einsum('bhqk,bhkd->bhqd', probs, v)
        return out.transpose(0, 2, 1, 3).reshape(b, t, -1)

    def _L0_xattn_ref(hidden_states, encoder_hidden_states, attention_mask, Wq, bq, Wk, bk, Wv, bv, Wo, qn_w, kn_w):
        import jax, jax.numpy as jnp
        import numpy as np
        H = 256
        NH = 16
        NKV = 4
        HD = 128
        GROUPS = NH // NKV
        EPS = 1e-06
        B, S, SE = (1, 256, 512)

        def _rmsnorm(x, w, eps=EPS):
            xf = x.astype(jnp.float32)
            var = jnp.mean(xf * xf, axis=-1, keepdims=True)
            return (xf * jax.lax.rsqrt(var + eps)).astype(x.dtype) * w
        b, s, _ = hidden_states.shape
        se = encoder_hidden_states.shape[1]
        q = (hidden_states @ Wq + bq).reshape(b, s, NH, HD).transpose(0, 2, 1, 3)
        k = (encoder_hidden_states @ Wk + bk).reshape(b, se, NKV, HD).transpose(0, 2, 1, 3)
        v = (encoder_hidden_states @ Wv + bv).reshape(b, se, NKV, HD).transpose(0, 2, 1, 3)
        k = jnp.repeat(k, GROUPS, axis=1)
        v = jnp.repeat(v, GROUPS, axis=1)
        q = _rmsnorm(q, qn_w)
        k = _rmsnorm(k, kn_w)
        scale = 1.0 / np.sqrt(HD).astype(np.float32)
        scores = jnp.einsum('bhsd,bhed->bhse', q, k) * scale
        scores = scores + attention_mask[:, None, :, :]
        probs = jax.nn.softmax(scores.astype(jnp.float32), axis=-1).astype(q.dtype)
        out = jnp.einsum('bhse,bhed->bhsd', probs, v)
        out = out.transpose(0, 2, 1, 3).reshape(b, s, NH * HD)
        return out @ Wo

    def _L0_ffn_ref(x, gate_w, w1, w2, w3, sw1, sw2, sw3):
        import jax, jax.numpy as jnp
        import numpy as np
        DIM = 256
        INTER = 176
        N_ROUTED = 15
        TOPK = 2
        SHARED_INTER = 176

        def _swiglu(x, wa, wb, wo):
            return jax.nn.silu(x @ wa.T) * (x @ wb.T) @ wo.T
        shape = x.shape
        xf = x.reshape(-1, shape[-1])
        T = xf.shape[0]
        probs = jax.nn.softmax(xf @ gate_w.T, axis=-1)
        weights, indices = jax.lax.top_k(probs, TOPK)
        combine = jnp.zeros((T, N_ROUTED), xf.dtype).at[jnp.arange(T)[:, None], indices].add(weights)
        y = jnp.zeros_like(xf)
        for i in range(N_ROUTED):
            y = y + _swiglu(xf, w1[i], w3[i], w2[i]) * combine[:, i:i + 1]
        z = _swiglu(xf, sw1, sw3, sw2)
        return (y + z).reshape(shape)
    x = x + _L0_attn_ref(_layernorm(x, axis=-1), L0_attn_W_DKV, L0_attn_b_DKV, L0_attn_W_UK, L0_attn_b_UK, L0_attn_W_UV, L0_attn_b_UV, L0_attn_W_DQ, L0_attn_b_DQ, L0_attn_W_UQ, L0_attn_b_UQ, L0_attn_W_QR, L0_attn_b_QR, L0_attn_W_KR, L0_attn_b_KR)
    x = x + _L0_xattn_ref(_layernorm(x, axis=-1), ctx_2048, mask_1xSxS2_ff0, L0_xattn_Wq, L0_xattn_bq, L0_xattn_Wk, L0_xattn_bk, L0_xattn_Wv, L0_xattn_bv, L0_xattn_Wo, L0_xattn_qn_w, L0_xattn_kn_w)
    x = x + _L0_ffn_ref(_layernorm(x, axis=-1), L0_ffn_gate_w, L0_ffn_w1, L0_ffn_w2, L0_ffn_w3, L0_ffn_sw1, L0_ffn_sw2, L0_ffn_sw3)
    return x

_drawn_inputs = setup_inputs


def setup_inputs(seed=0):
    import zlib

    import numpy as np

    out = dict(_drawn_inputs(seed))
    spreads = {'L0_attn_b_DKV': (0.0, 0.455),
     'L0_attn_b_UK': (0.0, 0.8),
     'L0_attn_b_UV': (0.0, 0.1),
     'L0_attn_b_DQ': (0.0, 0.8),
     'L0_attn_b_UQ': (0.0, 0.8),
     'L0_attn_b_QR': (0.0, 0.8),
     'L0_attn_b_KR': (0.0, 0.8),
     'L0_xattn_qn_w': (1.0, 0.6),
     'L0_xattn_kn_w': (1.0, 0.6)}
    factors = {'L0_attn_W_DKV': 8.0,
     'L0_attn_W_UK': 8.0,
     'L0_attn_W_UV': 3.148,
     'L0_attn_W_DQ': 8.0,
     'L0_attn_W_UQ': 8.0,
     'L0_attn_W_QR': 8.0,
     'L0_attn_W_KR': 8.0,
     'L0_xattn_bq': 8.0,
     'L0_xattn_bk': 8.0,
     'L0_xattn_bv': 3.309,
     'L0_ffn_gate_w': 8.0,
     'L0_ffn_w1': 8.0,
     'L0_ffn_w2': 8.0,
     'L0_ffn_w3': 8.0,
     'L0_ffn_sw1': 4.168,
     'L0_ffn_sw2': 4.15,
     'L0_ffn_sw3': 4.131}
    for name, (base, spread) in spreads.items():
        noise = np.random.default_rng([zlib.crc32(name.encode()), seed]).standard_normal(out[name].shape)
        drawn = base * np.exp(spread * noise) if base else spread * noise
        out[name] = jnp.asarray(drawn.astype(out[name].dtype))
    for name, factor in factors.items():
        out[name] = (out[name] * factor).astype(out[name].dtype)
    return out
```

```python
from contextlib import ExitStack

import numpy as np

import concourse.bass as bass
from concourse import mybir

F32 = mybir.dt.float32
F32R = mybir.dt.float32r
ALU = mybir.AluOpType
ACT = mybir.ActivationFunctionType
X = mybir.AxisListType.X

P = 128
B, T, D = 4, 256, 256
NT = B * T // P
TB = T // P
C = D // P
LN_EPS = 1e-5
NH, DC = 16, 64
DH, DR = D // NH, DC // NH
DQ = DH + DR
HW = 64
KS = 3 * DQ
KM = KS + 2
NP = NH // 2
SA_SCALE = float(DQ) ** -0.5
SE, XH, KV, HD = 512, 16, 4, 128
KT_ = SE // P
GR = XH // KV
GW = GR * HD
RMS_EPS = 1e-6
XSCALE = float(HD) ** -0.5

NE, INTER = 15, 176
IH = INTER // 2
EW = 16
NSLOT = (2 * B * T - NE) // P + NE
FINITE_LOW = -3.0e38


def xattn_tasks():
    tasks = {}

    def put(slot, *task):
        tasks.setdefault(slot, []).append(task)

    for b in range(B):
        lead = 8 * (4 * b - 2) if b else -19
        own = 8 * (4 * b - 1) if b else -10
        put(lead + 0, "LNV", b)
        put(lead + 1, "CT", b, 0)
        put(lead + 2, "CT", b, 1)
        put(lead + 3, "LNW", b)
        put(lead + 4, "XT", b)
        for kt in range(KT_):
            put(own + kt // 2, "KP", b, kt)
            put(own + kt // 2 + 1, "SS", "K", b, kt)
            put(own + 2 + kt // 2, "VP", b, kt)
        put(own + 3, "VE", "K", b)
        put(own + 4, "NW", "K", b)
    for n in range(B * KV):
        own = 8 * (n - 1) if n else -10
        for qt in range(TB):
            put(own + 2 * qt + (n == 0), "QP", n, qt)
            put(own + 2 * qt + 1 + (n == 0), "SS", "Q", n, qt)
            put(own + 7, "QT", n, qt)
        put(own + 4, "VE", "Q", n)
        put(own + 5, "NW", "Q", n)
        put(own + 5, "VS", n)
        put(own + 6, "KT", n)
    return tasks


def layer(nc, x, ctx_in, mask, W_DKV, b_DKV, W_UK, b_UK, W_UV, b_UV, W_DQ, b_DQ, W_UQ, b_UQ, W_QR, b_QR,
          W_KR, b_KR, Wq, bq, Wk, bk, Wv, bv, Wo, qn_w, kn_w, gate_wT, w13T, w2T, rope_cs, out):
    es = ExitStack()
    with es:
        def sb(name, shape, dt=F32, stack=es):
            return stack.enter_context(nc.sbuf_tensor(name, shape, dt))

        def sem(name):
            return es.enter_context(nc.semaphore(name))

        ps = [es.enter_context(nc.psum_tensor(f"bank{i}", [P, 512], F32)) for i in range(8)]

        xs = sb("xs", [P, NT, D])
        ident = sb("ident", [P, P])
        OFF_K, OFF_V, OFF_Q, W_COLS = 0, C * KV * HD, 2 * C * KV * HD, 2 * C * KV * HD + C * XH * HD
        Wkvq = [sb(f"Wkvq{i}", [P, W_COLS], F32R) for i in "hl"]
        bias_hl = sb("bias_hl", [98, 2, 512], F32R)
        ones2 = sb("ones2", [98, P], F32R)
        stats = sb("stats", [P, 2, 6])
        wqk = sb("wqk", [P, 1])
        mv = sb("mv", [P, NT, 2])
        ve = sb("ve", [P, 16])
        lnv = sb("lnv", [P, 16])
        r0 = sb("r0", [P, 16])
        nwt = sb("nwt", [P, 16])
        rln = sb("rln", [P, NT])

        upper = sb("upper", [P, P])
        onesf = sb("onesf", [P, P])
        iota_e = sb("iota_e", [P, EW])
        iota_t = sb("iota_t", [P, NT])
        iota_j = sb("iota_j", [P, 32])

        esA = ExitStack()
        es.enter_context(esA)
        w1 = sb("w1", [P, C, 192], F32, esA)
        w2kv = sb("w2kv", [DC, 2 * D], F32, esA)
        w2q = sb("w2q", [P, D + DC], F32, esA)
        b1 = sb("b1", [P, 192], F32, esA)
        b2 = sb("b2", [P, 832], F32, esA)
        cs = sb("cs", [P, TB, 2, 4], F32, esA)
        xn = sb("xn", [P, 2, D], F32, esA)
        xnT = sb("xnT", [P, 2, C, P], F32, esA)
        c1 = sb("c1", [P, 2, 128], F32, esA)
        rr = sb("rr", [P, 3, 2, DC], F32, esA)
        cT = sb("cT", [P, 2, P], F32, esA)
        cat = sb("cat", [P, 2, 2, NH, DQ], F32, esA)
        rp1 = sb("rp1", [P, 2 * NH, DR], F32, esA)
        rp2 = sb("rp2", [P, 2 * NH, DR], F32, esA)
        qks = sb("qks", [P, 2, 2, NH, HW], F32R, esA)
        qkT = sb("qkT", [P, 2, NP, B * T], F32R, esA)
        va = sb("va", [P, NT, NH, DH + 1], F32, esA)
        mneg = sb("mneg", [P, 2, TB, NH], F32, esA)
        msp = sb("msp", [P, TB, 2, 2, NP], F32R, esA)
        mT = sb("mT", [32, 2, T], F32R, esA)
        pTs = sb("pTs", [P, 3, 2, T], F32, esA)
        rsv = sb("rsv", [P, TB, NH], F32, esA)
        osa = sb("osa", [P, TB, NH, DH], F32, esA)
        wraw = sb("wraw", [P, 2, 512], F32, esA)
        braw = sb("braw", [6, 512], F32, esA)
        bsp = [sb(f"bsp{i}", [6, 512], F32R, esA) for i in "hl"]
        qkw = sb("qkw", [P, 2], F32, esA)
        zeros = sb("zeros", [P, D], F32, esA)
        esA.close()

        esD = ExitStack()
        es.enter_context(esD)
        WoS = [sb(f"Wo{i}", [P, XH, D], F32R, esD) for i in "hl"]
        wraw2 = sb("wraw2", [P, 2, 512], F32, esD)
        msk = sb("msk", [P, TB, SE], F32, esD)
        craw = sb("craw", [P, KT_, D], F32, esD)
        ctxT = [sb(f"ctxT{i}", [P, C, SE], F32R, esD) for i in "hl"]
        xnD = sb("xnD", [P, TB, D], F32, esD)
        xT = [sb(f"xT{i}", [P, C, T], F32R, esD) for i in "hl"]
        kraw = sb("kraw", [P, KT_, KV * HD], F32, esD)
        vraw = sb("vraw", [P, KT_, KV * HD], F32, esD)
        qraw = sb("qraw", [P, TB, GW], F32, esD)
        sq = sb("sq", [P, 2, 512], F32, esD)
        ssK = sb("ssK", [P, 16], F32, esD)
        ssQ = sb("ssQ", [P, 8], F32, esD)
        rK = sb("rK", [P, 16], F32, esD)
        rQ = sb("rQ", [P, 8], F32, esD)
        kT = [sb(f"kT{i}", [P, 2, SE], F32R, esD) for i in "hl"]
        vS = [sb(f"vS{i}", [P, 2, KT_, HD], F32R, esD) for i in "hl"]
        qT = [sb(f"qT{i}", [P, 2, TB, GW], F32R, esD) for i in "hl"]
        pb = sb("pb", [P, 3, SE], F32, esD)
        nmax = sb("nmax", [P, 3], F32, esD)
        psm = sb("psm", [P, 3], F32, esD)
        rinv = sb("rinv", [P, 3], F32, esD)
        pT = [sb(f"pT{i}", [P, 2, KT_, T], F32R, esD) for i in "hl"]
        oT = [sb(f"oT{i}", [P, T], F32R, esD) for i in "hl"]
        esD.close()

        esF = ExitStack()
        es.enter_context(esF)
        w13 = sb("w13", [P, NE + 1, C, 2 * INTER], F32, esF)
        w2s = sb("w2s", [IH, NE + 1, 2, D], F32, esF)
        gw = sb("gw", [P, C, EW], F32, esF)
        xn3 = sb("xn3", [P, NT, D], F32, esF)
        xn3T = sb("xn3T", [P, C, B * T], F32, esF)
        lg = sb("lg", [P, NT, EW], F32, esF)
        lge = sb("lge", [P, NT, EW], F32, esF)
        eq = sb("eq", [P, NT, EW], F32, esF)
        oh = [sb(f"onehot{i}", [P, NT, EW], F32, esF) for i in range(2)]
        chosen = sb("chosen", [P, NT, EW], F32, esF)
        top = [sb(f"top{i}", [P, NT], F32, esF) for i in range(2)]
        first_e = sb("first_e", [P, NT], F32, esF)
        cw = [sb(f"combine{i}", [P, NT], F32, esF) for i in range(2)]
        tot = sb("tot", [P, NT, EW], F32, esF)
        before = sb("before", [P, NT + 1, EW], F32, esF)
        more = sb("more", [P, EW, NT], F32, esF)
        ntile = sb("ntile", [P, EW], F32, esF)
        tend = sb("tend", [P, EW], F32, esF)
        pos = sb("pos", [P, NT, EW], F32, esF)
        slotf = sb("slotf", [P, 2, NT], F32, esF)
        sloti = sb("sloti", [P, 2, NT], mybir.dt.int32, esF)
        isof = sb("isof", [P, 32, EW], F32, esF)
        expf = sb("expf", [P, 32], F32, esF)
        expi = sb("expi", [P, 32], mybir.dt.int32, esF)
        xg = sb("xg", [P, 2, D], F32, esF)
        xgT = sb("xgT", [P, 2, C, P], F32, esF)
        sg = sb("sg", [P, 2, INTER], F32, esF)
        hh = sb("hh", [P, 2, INTER], F32, esF)
        hT = sb("hT", [IH, 2, 2, P], F32, esF)
        ys = sb("ys", [P, 2, D], F32, esF)
        yg = [sb(f"yg{i}", [P, NT, D], F32, esF) for i in range(2)]
        esF.close()
        xg_dram = nc.dram_tensor("rows_by_slot", (NSLOT * P, D), F32, kind="Internal").ap()
        yg_dram = nc.dram_tensor("results_by_slot", (NSLOT * P, D), F32, kind="Internal").ap()

        ld_small, ld_b, ld_mask, ld_ctx, st_out, mrow = [
            sem(n) for n in ("ld_small", "ld_b", "ld_mask", "ld_ctx", "st_out", "mrow_moved")]
        act_self, dve_self, pool_self = sem("act_self"), sem("dve_self"), sem("pool_self")
        consts = sem("consts_ready")
        w_read, w_split, b_split, qkw_read = sem("w_chunk_read"), sem("w_split"), sem("b_split"), sem("qkw_read")
        var_ready, r0_ready, rln_ready = sem("var_ready"), sem("r0_ready"), sem("rln_ready")
        xn_ready, xnT_ps, xnT_ready, c_ps, c_ready, cT_ps, cT_ready, kvq_ps, cat_ready = [
            sem(n) for n in ("xn_ready", "xnT_ps", "xnT_ready", "c_ps", "c_ready", "cT_ps", "cT_ready",
                             "kvq_ps", "cat_ready")]
        kvq_read = sem("kvq_read")
        hi_ready, lo_ready, qk_ps, qkA, qkD = [sem(n) for n in ("hi_ready", "lo_ready", "qk_ps", "qk_by_act", "qk_by_dve")]
        s1_ps, s1_max, m_hi, m_lo, mT_ps, mT_ready = [
            sem(n) for n in ("s1_ps", "s1_max", "m_hi", "m_lo", "mT_ps", "mT_ready")]
        sT_ps, pTs_ready, o_ps, x1_ready = [sem(n) for n in ("sT_ps", "pTs_ready", "o_ps", "x1_ready")]
        ld_x = [sem(f"ld_x{i}") for i in range(2)]
        m_ps, ctx_hi, ctx_lo, xT_hi, xT_lo = [sem(n) for n in ("m_ps", "ctx_hi", "ctx_lo", "xT_hi", "xT_lo")]
        bias_placed, wo_split, w_high = sem("bias_placed"), sem("wo_split"), sem("w_high")
        ld_w, ld_wo = [[sem(f"{n}{i}") for i in range(2)] for n in ("ld_w", "ld_wo")]
        xnD_ready, raw_ready, v_ready, sq_ready, ss_ready = [
            sem(n) for n in ("xnD_ready", "raw_ready", "v_ready", "sq_ready", "ss_ready")]
        rk_var, rk_r0, rk_ready, normed = [sem(n) for n in ("rk_var", "rk_r0", "rk_ready", "normed")]
        v_split, kT_hi, kT_lo, qT_hi, qT_lo = [sem(n) for n in ("v_split", "kT_hi", "kT_lo", "qT_hi", "qT_lo")]
        S_ps, S_masked, exp_done, rinv_ready, p_normed, pT_ps, pT_hi, pT_lo = [
            sem(n) for n in ("S_ps", "S_masked", "exp_done", "rinv_ready", "p_normed", "pT_ps", "pT_hi", "pT_lo")]
        pv_ps, o_hi, o_lo, wo_ps, x2_ready = [sem(n) for n in ("pv_ps", "o_hi", "o_lo", "wo_ps", "x2_ready")]

        ld_e, zeroed, zero_src = [sem(n) for n in ("ld_experts", "xg_zeroed", "zero_src")]
        ld_shared = sem("ld_shared")
        xn3_ready, x3_ps, x3_T, gate_ps, lgm_ready, lge_ready, chosen_ready, rank_ps, slots_ready, scattered = [
            sem(n) for n in ("xn3_ready", "x3_ps", "x3_T", "gate_ps", "lgm_ready", "lge_ready", "chosen_ready", "rank_ps",
                             "slots_ready", "scattered")]
        xg_ld = [sem(f"xg_ld{i}") for i in range(2)]
        y_st = [sem(f"y_st{i}") for i in range(2)]
        gathered = [sem(f"gathered{t}") for t in range(NT)]
        xg_ps, xgT_ready, up_ps, sg_ready, hh_ready, h_ps, hT_ready, y_ps, y_read, done = [
            sem(n) for n in ("xg_ps", "xgT_ready", "up_ps", "sg_ready", "hh_ready", "h_ps", "hT_ready", "y_ps", "y_read",
                             "done")]

        x_dram = x.rearrange("b (j p) d -> p (b j) d", p=P)
        out_dram = out.rearrange("b (j p) d -> p (b j) d", p=P)

        chunks = []
        for c in range(C):
            rows = slice(c * P, (c + 1) * P)
            chunks.append((OFF_K + 512 * c, Wk[rows, :]))
            chunks.append((OFF_V + 512 * c, Wv[rows, :]))
            for g in range(KV):
                chunks.append((OFF_Q + XH * HD * c + GW * g, Wq[rows, g * GW:(g + 1) * GW]))
        wo_chunks = [Wo[i * 2 * P:(i + 1) * 2 * P, :].rearrange("(h p) n -> p h n", p=P) for i in range(XH // 2)]

        def stage_slots():
            return range(NT + 4)

        M_LAG, P2_LAG, PV_LAG = 17, 22, 2
        UNITS = B * NH
        side = {}
        tasks = xattn_tasks()
        FIRST, LAST = min(tasks), 8 * B * KV + 6
        for s in range(FIRST, LAST):
            for task in tasks.get(s, ()):
                if task[0] in ("CT", "XT", "KP", "VP", "QP", "KT", "QT"):
                    side[task] = len(side)
        norm_unit = {}
        norm_chain = {}
        for s in range(FIRST, LAST):
            for task in tasks.get(s, ()):
                if task[0] in ("KP", "QP"):
                    norm_unit[(task[0][0], *task[1:])] = len(norm_unit)
                if task[0] == "VE":
                    norm_chain[task[1:]] = len(norm_chain)

        side_order = list(side)

        def released(task):
            kind, *a = task
            if kind in ("KP", "QP"):
                return raw_ready, norm_unit[(kind[0], *a)] + 1
            return {"CT": lambda b, c: (ctx_lo, C * b + c + 1), "XT": lambda b: (xT_lo, b + 1),
                    "VP": lambda b, kt: (v_ready, KT_ * b + kt + 1), "KT": lambda n: (kT_lo, n + 1),
                    "QT": lambda n, qt: (qT_lo, TB * n + qt + 1)}[kind](*a)

        def side_bank(task):
            return ps[6 + side[task] % 2]

        block = es.enter_context(nc.Block())

        @block.sync
        def _(sp):
            sp.dma_start(xs[:, 0:TB, :], x_dram[:, 0:TB, :]).then_inc(ld_x[0], 16)
            sp.dma_start(xs[:, TB:NT, :], x_dram[:, TB:NT, :]).then_inc(ld_x[1], 16)
            w1_parts = ((0, W_DKV), (DC, W_DQ), (2 * DC, W_KR))
            for off, w in w1_parts:
                sp.dma_start(w1[:, :, off:off + DC], w.rearrange("(c p) n -> p c n", p=P)).then_inc(ld_small, 16)
            for off, v, n in ((0, b_DKV, DC), (DC, b_DQ, DC), (2 * DC, b_KR, DC)):
                sp.dma_start(b1[:, off:off + n], v.rearrange("(a n) -> a n", a=1).to_broadcast([P, n])).then_inc(ld_small, 16)
            sp.dma_start(w2kv[:, 0:D], W_UK).then_inc(ld_small, 16)
            sp.dma_start(w2kv[:, D:2 * D], W_UV).then_inc(ld_small, 16)
            sp.dma_start(w2q[DC:P, 0:D], W_UQ).then_inc(ld_small, 16)
            sp.dma_start(w2q[DC:P, D:D + DC], W_QR).then_inc(ld_small, 16)
            for off, v, n in ((0, b_UK, D), (D, b_UV, D), (2 * D, b_UQ, D), (3 * D, b_QR, DC)):
                sp.dma_start(b2[:, off:off + n], v.rearrange("(a n) -> a n", a=1).to_broadcast([P, n])).then_inc(ld_small, 16)
            sp.dma_start(cs[:], rope_cs).then_inc(ld_small, 16)
            for row, v in ((0, bq), (4, bk), (5, bv)):
                sp.dma_start(braw[row:row + v.shape[0] // 512, :], v.rearrange("(a n) -> a n", n=512)).then_inc(ld_b, 16)
            sp.dma_start(qkw[:, 0:1], qn_w.rearrange("(p a) -> p a", a=1)).then_inc(ld_b, 16)
            sp.dma_start(qkw[:, 1:2], kn_w.rearrange("(p a) -> p a", a=1)).then_inc(ld_b, 16)
            for i, (off, src) in enumerate(chunks):
                if i >= 2:
                    sp.wait_ge(w_split, i - 1)
                if i == 2:
                    sp.wait_ge(b_split, 3)
                    for j in range(6):
                        for part in range(2):
                            row = 32 * (j % 4) + part
                            sp.dma_start(bias_hl[row:row + 1, j // 4, :].bitcast(F32), bsp[part][j:j + 1, :].bitcast(F32)).then_inc(bias_placed, 16)
                sp.dma_start(wraw[:, i % 2, :], src).then_inc(ld_w[i % 2], 16)
            sp.wait_ge(zero_src, 1)
            sp.dma_start(xg_dram.rearrange("(j p) d -> p j d", p=P),
                         zeros[:].unsqueeze(1).to_broadcast([P, NSLOT, D])).then_inc(zeroed, 16)
            for b in range(B):
                if b:
                    sp.wait_ge(mrow, 64 * b)
                sp.wait_ge(mT_ready, b + 1)
                for jj in range(2):
                    for part in range(2):
                        row = jj * 16 + part * 8
                        to = 64 * jj + KS + part
                        sp.dma_start(qkT[to:to + 1, 0, :, b * T:(b + 1) * T].bitcast(F32), mT[row:row + 8, b % 2, :].bitcast(F32)).then_inc(mrow, 16)
            sp.wait_ge(x1_ready, B)
            sp.wait_ge(w_split, len(chunks))
            sp.wait_ge(bias_placed, 16 * 12)
            sp.wait_ge(zeroed, 16)
            sp.dma_start(msk[:], mask.rearrange("a (j p) e -> p (a j) e", p=P)).then_inc(ld_mask, 16)
            for b in range(B):
                if b == 1:
                    for i, src in enumerate(wo_chunks):
                        if i >= 2:
                            sp.wait_ge(wo_split, i - 1)
                        sp.dma_start(wraw2[:, i % 2, :].rearrange("p (h n) -> p h n", h=2), src).then_inc(ld_wo[i % 2], 16)
                if b:
                    sp.wait_ge(m_ps, side[("CT", b - 1, 1)] + 1)
                sp.dma_start(craw[:], ctx_in[b].rearrange("(k p) d -> p k d", p=P)).then_inc(ld_ctx, 16)
            sp.wait_ge(x2_ready, B)
            sp.dma_start(gw[:, :, 0:NE], gate_wT.rearrange("(c p) e -> p c e", p=P)).then_inc(ld_shared, 16)
            sp.dma_start(w13[:, NE, :, :], w13T[NE].rearrange("(c p) n -> p c n", p=P)).then_inc(ld_shared, 16)
            sp.dma_start(w2s[:, NE, :, :], w2T[NE].rearrange("(c p) n -> p c n", p=IH)).then_inc(ld_shared, 16)
            for e in range(0, NE, 5):
                sp.dma_start(w13[:, e:e + 5].rearrange("p e c n -> p (e c) n"),
                             w13T[e:e + 5].rearrange("e (c p) n -> p (e c) n", p=P)).then_inc(ld_e, 16)
                sp.dma_start(w2s[:, e:e + 5].rearrange("p e c n -> p (e c) n"),
                             w2T[e:e + 5].rearrange("e (c p) n -> p (e c) n", p=IH)).then_inc(ld_e, 16)

            xg_rows = xg_dram.rearrange("(j p) d -> p j d", p=P)
            yg_rows = yg_dram.rearrange("(j p) d -> p j d", p=P)

            def load(j, k, par):
                sp.dma_start(xg[:, par:par + 1, :], xg_rows[:, bass.ds(j, 1), :]).then_inc(xg_ld[par], 16)

            def store(j, par):
                sp.wait_ge(y_read, j + NT + 1)
                sp.dma_start(yg_rows[:, bass.ds(j, 1), :], ys[:, par:par + 1, :]).then_inc(y_st[par], 16)

            sp.wait_ge(scattered, 16 * 2 * NT)
            load(0, 0, 0)
            load(1, 0, 1)
            with sp.Fori(0, NSLOT // 2 - 1) as k:
                for par in range(2):
                    sp.wait_ge(xg_ps, 2 * k + par + 1)
                    load(2 * k + par + 2, k + 1, par)
                    store(2 * k + par, par)
            for j in (NSLOT - 2, NSLOT - 1):
                store(j, j % 2)
            for t in range(NT):
                sp.wait_ge(done, t + 1)
                sp.dma_start(out_dram[:, t, :], xs[:, t, :]).then_inc(st_out, 16)
            sp.wait_ge(st_out, 16 * NT)

        @block.gpsimd
        def _(pool):
            n_self = 0

            def link(ins):
                nonlocal n_self
                n_self += 1
                ins.then_inc(pool_self, 1)
                pool.wait_ge(pool_self, n_self)

            link(pool.memset(ident[:], 0.0))
            link(pool.memset(qks[:].bitcast(F32), 0.0))
            pool.memset(va[:, :, :, DH:DH + 1], 1.0).then_inc(consts, 1)
            pool.affine_select(out=ident[:], in_=ident[:], compare_op=ALU.not_equal, fill=1.0, base=0,
                               pattern=[[-1, P]], channel_multiplier=1).then_inc(consts, 1)
            pool.memset(qks[:, :, 1, :, KS:KM].bitcast(F32), 1.0).then_inc(consts, 1)
            pool.memset(ones2[:].bitcast(F32), 1.0).then_inc(consts, 1)
            pool.memset(zeros[:], 0.0).then_inc(zero_src, 1)
            pool.memset(onesf[:], 1.0).then_inc(pool_self, 1)
            link(pool.memset(upper[:], 1.0))
            n_self += 1
            pool.wait_ge(pool_self, n_self)
            pool.affine_select(out=upper[:], in_=upper[:], compare_op=ALU.is_gt, fill=0.0, base=0, pattern=[[1, P]],
                               channel_multiplier=-1).then_inc(consts, 1)
            pool.iota(iota_e[:], pattern=[[1, EW]], base=0, channel_multiplier=0,
                      allow_small_or_imprecise_dtypes=True).then_inc(consts, 1)
            pool.iota(iota_t[:], pattern=[[P, NT]], base=0, channel_multiplier=0,
                      allow_small_or_imprecise_dtypes=True).then_inc(consts, 1)
            pool.iota(iota_j[:], pattern=[[1, 32]], base=0, channel_multiplier=0,
                      allow_small_or_imprecise_dtypes=True).then_inc(consts, 1)
            pool.wait_ge(ld_b, 16 * 5)
            link(pool.tensor_tensor(wqk[:], qkw[:, 0:1], qkw[:, 1:2], ALU.mult))
            pool.tensor_scalar(wqk[:], wqk[:], XSCALE, None, ALU.mult).then_inc(b_split, 1)
            pool.tensor_copy(bsp[0][:], braw[:]).then_inc(b_split, 1)
            pool.wait_ge(b_split, 2)
            pool.tensor_tensor(bsp[1][:], braw[:], bsp[0][:].bitcast(F32), ALU.subtract).then_inc(b_split, 1)

            def split_weights(i):
                off, _ = chunks[i]
                pool.wait_ge(w_high, i + 1)
                pool.tensor_tensor(Wkvq[1][:, off:off + 512], wraw[:, i % 2, :], Wkvq[0][:, off:off + 512].bitcast(F32),
                                   ALU.subtract).then_inc(w_split, 1)

            for k in stage_slots():
                t = k - 3
                if 0 <= t < NT:
                    pool.wait_ge(hi_ready, t + 1)
                    pool.tensor_tensor(qks[:, t % 2, 0, :, 2 * DQ:KS], cat[:, t % 2, 0], qks[:, t % 2, 0, :, 0:DQ].bitcast(F32),
                                       ALU.subtract).then_inc(lo_ready, 1)
                    pool.tensor_tensor(qks[:, t % 2, 1, :, DQ:2 * DQ], cat[:, t % 2, 1], qks[:, t % 2, 1, :, 0:DQ].bitcast(F32),
                                       ALU.subtract).then_inc(lo_ready, 1)
                split_weights(k)

            def square(u, raw):
                pool.wait_ge(raw_ready, u + 1)
                if u >= 2:
                    pool.wait_ge(ss_ready, u - 1)
                pool.tensor_tensor(sq[:, u % 2, :], raw, raw, ALU.mult).then_inc(sq_ready, 1)

            def split_wo(i):
                pool.wait_ge(ld_wo[i % 2], 16 * (i // 2 + 1))
                high, low = [w[:, 2 * i:2 * i + 2, :].rearrange("p h n -> p (h n)") for w in WoS]
                link(pool.tensor_copy(high, wraw2[:, i % 2, :]))
                pool.tensor_tensor(low, wraw2[:, i % 2, :], high.bitcast(F32), ALU.subtract).then_inc(wo_split, 1)

            for s in range(FIRST, LAST):
                if -8 <= s < 0:
                    split_wo(s + 8)
                for kind, *a in tasks.get(s, ()):
                    if kind == "KP":
                        square(norm_unit[("K", *a)], kraw[:, a[1], :])
                    if kind == "QP":
                        square(norm_unit[("Q", *a)], qraw[:, a[1], :])
                    if kind == "NW":
                        n = norm_chain[tuple(a)]
                        pool.wait_ge(rk_ready, n + 1)
                        raw, r, tiles = (kraw, rK, KT_) if a[0] == "K" else (qraw, rQ, TB)
                        v = raw[:].rearrange("p k (g d) -> p (k g) d", d=HD)
                        pool.tensor_tensor(v, v, r[:].unsqueeze(2).to_broadcast([P, 4 * tiles, HD]), ALU.mult).then_inc(normed, 1)
                    if kind == "VS":
                        n, = a
                        pool.wait_ge(v_ready, 4 * (n // 4 + 1))
                        if n >= 2:
                            pool.wait_ge(pv_ps, 4 * (n - 1))
                        src = vraw[:, :, (n % 4) * HD:(n % 4 + 1) * HD]
                        link(pool.tensor_copy(vS[0][:, n % 2], src))
                        pool.tensor_tensor(vS[1][:, n % 2], src, vS[0][:, n % 2].bitcast(F32), ALU.subtract).then_inc(v_split, 1)

            pool.wait_ge(zeroed, 16)
            pool.wait_ge(xn3_ready, NT)
            pool.wait_ge(slots_ready, 1)
            for t in range(NT):
                for k in range(2):
                    pool.indirect_dma_start(out=xg_dram, out_offset=bass.IndirectOffsetOnAxis(sloti[:, k, t:t + 1], axis=0),
                                            in_=xn3[:, t, :], in_offset=None).then_inc(scattered, 16)
            for par in range(2):
                pool.wait_ge(y_st[par], 16 * (NSLOT // 2))
            for t in range(NT):
                for k in range(2):
                    pool.indirect_dma_start(out=yg[k][:, t, :], out_offset=None, in_=yg_dram,
                                            in_offset=bass.IndirectOffsetOnAxis(sloti[:, k, t:t + 1], axis=0)
                                            ).then_inc(gathered[t], 16)

        @block.scalar
        def _(act):
            n_self = 0

            def link(ins):
                nonlocal n_self
                n_self += 1
                ins.then_inc(act_self, 1)
                act.wait_ge(act_self, n_self)

            def rsqrt_guess(n, ready, at, done):
                act.wait_ge(ready, at)
                link(nc.scalar.activation(lnv[:, 0:n], ve[:, 0:n], ACT.Ln))
                nc.scalar.activation(r0[:, 0:n], lnv[:, 0:n], ACT.Exp, scale=-0.5).then_inc(done, 1)

            act.preload_act_table_set("natural_log_exp_and_others")
            rsqrt_guess(TB, var_ready, 1, r0_ready)
            rsqrt_guess(NT - TB, var_ready, 2, r0_ready)
            for k in stage_slots():
                t = k - 4
                if 0 <= t < NT:
                    for g in range(2):
                        act.wait_ge(qk_ps, 4 * t + g + 1)
                        act.copy(qkT[:, 0, 4 * g:4 * g + 4, t * P:(t + 1) * P],
                                 ps[5 + g % 2][:].rearrange("p (a n) -> p a n", a=4)).then_inc(qkA, 1)
                t = k - 3
                if 0 <= t < NT:
                    act.wait_ge(cat_ready, t + 1)
                    if t >= 2:
                        act.wait_ge(qk_ps, 4 * (t - 1))
                    src = cat[:, t % 2].rearrange("p a h d -> p (a h) d")
                    dst = qks[:, t % 2].rearrange("p a h d -> p (a h) d")
                    act.copy(dst[:, :, 0:DQ], src)
                    act.copy(dst[:, 0:NH, DQ:2 * DQ], src[:, 0:NH, :])
                    act.copy(dst[:, NH:2 * NH, 2 * DQ:KS], src[:, NH:2 * NH, :]).then_inc(hi_ready, 1)
                t = k - 2
                if 0 <= t < NT:
                    act.wait_ge(cT_ps, t + 1)
                    if t >= 2:
                        act.wait_ge(kvq_ps, t - 1)
                    act.copy(cT[:, t % 2, :], ps[2][:, 0:P]).then_inc(cT_ready, 1)
                t = k
                if 0 <= t < NT:
                    act.wait_ge(xnT_ps, t + 1)
                    if t >= 2:
                        act.wait_ge(c_ps, t - 1)
                    act.copy(xnT[:, t % 2].rearrange("p c n -> p (c n)"), ps[0][:, 0:D]).then_inc(xnT_ready, 1)
                off, _ = chunks[k]
                act.wait_ge(ld_w[k % 2], 16 * (k // 2 + 1))
                act.copy(Wkvq[0][:, off:off + 512], wraw[:, k % 2, :]).then_inc(w_high, 1)

            for u in range(UNITS + P2_LAG + 1):
                b = (u - M_LAG + 1) // NH
                if u >= M_LAG - 1 and (u - M_LAG + 1) % NH == 0 and b < B:
                    act.wait_ge(s1_max, NH * (b + 1))
                    if b:
                        act.wait_ge(mT_ps, b)
                    act.copy(msp[:, :, :, 0, :], mneg[:, b % 2].rearrange("p q (a j) -> p q j a", j=2)).then_inc(m_hi, 1)
                    act.wait_ge(mT_ps, b + 1)
                    if b >= 2:
                        act.wait_ge(mrow, 64 * (b - 1))
                    act.copy(mT[:, b % 2, :], ps[(17 * b + 16) % 2][0:32, 0:T]).then_inc(mT_ready, 1)
                v = u - P2_LAG
                if 0 <= v < UNITS:
                    act.wait_ge(sT_ps, v + 1)
                    if v >= 3:
                        act.wait_ge(o_ps, v - 2)
                    nc.scalar.activation(pTs[:, v % 3].rearrange("p k t -> p (k t)"), ps[2 + v % 2][:], ACT.Exp,
                                         scale=SA_SCALE).then_inc(pTs_ready, 1)

            for s in range(FIRST, LAST):
                if 0 <= s - 2 < 8 * B * KV:
                    i = s - 2
                    act.wait_ge(pT_ps, i + 1)
                    if i // 2 >= 2:
                        act.wait_ge(pv_ps, i // 2 - 1)
                    act.copy(pT[0][:, (i // 2) % 2, :, (i % 2) * P:(i % 2 + 1) * P],
                             ps[2 + i % 2][:].rearrange("p (k n) -> p k n", k=KT_)).then_inc(pT_hi, 1)
                if 0 <= s < 8 * B * KV:
                    act.wait_ge(S_masked, s + 1)
                    nc.scalar.activation(pb[:, s % 3, :], pb[:, s % 3, :], ACT.Exp, bias=nmax[:, s % 3:s % 3 + 1], scale=-1.0,
                                         accum_out=psm[:, s % 3:s % 3 + 1]).then_inc(exp_done, 1)
                if s >= 4 and s % 2 == 0 and (s - 4) // 2 < B * XH:
                    h = (s - 4) // 2
                    act.wait_ge(pv_ps, h + 1)
                    if h >= 1:
                        act.wait_ge(wo_ps, h)
                    act.copy(oT[0][:], ps[4][:, 0:T]).then_inc(o_hi, 1)
                for task in tasks.get(s, ()):
                    kind, *a = task
                    if kind in ("CT", "XT", "KP", "VP", "QP", "KT", "QT"):
                        act.wait_ge(m_ps, side[task] + 1)
                        bank = side_bank(task)
                    if kind == "LNV":
                        rsqrt_guess(TB, var_ready, 3 + a[0], r0_ready)
                    if kind == "VE":
                        n = norm_chain[tuple(a)]
                        rsqrt_guess(16 if a[0] == "K" else 8, rk_var, n + 1, rk_r0)
                    if kind == "CT":
                        b, c = a
                        if b:
                            act.wait_ge(m_ps, side[("VP", b - 1, KT_ - 1)] + 1)
                        act.copy(ctxT[0][:, c, :], bank[:]).then_inc(ctx_hi, 1)
                    if kind == "XT":
                        b, = a
                        if b:
                            act.wait_ge(m_ps, side[("QP", 4 * b - 1, 1)] + 1)
                        act.copy(xT[0][:].rearrange("p c n -> p (c n)"), bank[:]).then_inc(xT_hi, 1)
                    if kind == "KP":
                        b, kt = a
                        if b:
                            act.wait_ge(m_ps, side[("KT", 4 * b - 1)] + 1)
                        act.copy(kraw[:, kt, :], bank[:]).then_inc(raw_ready, 1)
                    if kind == "QP":
                        n, qt = a
                        if n:
                            act.wait_ge(m_ps, side[("QT", n - 1, qt)] + 1)
                        act.copy(qraw[:, qt, :], bank[:]).then_inc(raw_ready, 1)
                    if kind == "VP":
                        b, kt = a
                        if b:
                            act.wait_ge(v_split, 4 * b)
                        act.copy(vraw[:, kt, :], bank[:]).then_inc(v_ready, 1)
                    if kind == "KT":
                        n, = a
                        if n >= 2:
                            act.wait_ge(S_ps, 8 * (n - 1))
                        nc.scalar.activation(kT[0][:, n % 2, :], bank[:], ACT.Copy, scale=wqk[:, 0:1]).then_inc(kT_hi, 1)
                    if kind == "QT":
                        n, qt = a
                        if n >= 2:
                            act.wait_ge(S_ps, 8 * (n - 1))
                        act.copy(qT[0][:, n % 2, qt, :], bank[:]).then_inc(qT_hi, 1)

            rsqrt_guess(NT, var_ready, 3 + B, r0_ready)
            for u in range(4):
                act.wait_ge(x3_ps, u + 1)
                act.copy(xn3T[:, u // 2, (u % 2) * 512:(u % 2 + 1) * 512], ps[u][:]).then_inc(x3_T, 1)
            act.wait_ge(lgm_ready, 1)
            nc.scalar.activation(lge[:], lg[:], ACT.Exp).then_inc(lge_ready, 1)

            def silu(i, par):
                act.wait_ge(up_ps, i + 1)
                nc.scalar.activation(sg[:, par, :], ps[2 + par][:, 0:INTER], ACT.Silu).then_inc(sg_ready, 1)

            def turn_rows(j, par):
                act.wait_ge(xg_ps, j + 1)
                act.copy(xgT[:, par].rearrange("p c n -> p (c n)"), ps[par][:, 0:D]).then_inc(xgT_ready, 1)

            for i in range(NT):
                if i >= 2:
                    act.wait_ge(hh_ready, i - 1)
                silu(i, i % 2)
            turn_rows(0, 0)
            act.wait_ge(hh_ready, NT - 1)
            silu(NT, 0)
            turn_rows(1, 1)
            with act.Fori(0, NSLOT // 2 - 1) as k:
                for par in range(2):
                    j = 2 * k + par + 1
                    act.wait_ge(hh_ready, j + (NT - 1))
                    silu(j + NT, 1 - par)
                    turn_rows(j + 1, par)
            act.wait_ge(hh_ready, NT + NSLOT - 2)
            silu(NT + NSLOT - 1, 1)

        @block.vector
        def _(dve):
            n_self = 0

            def link(ins):
                nonlocal n_self
                n_self += 1
                ins.then_inc(dve_self, 1)
                dve.wait_ge(dve_self, n_self)

            def polish(n, ready, at, r, done):
                dve.wait_ge(ready, at)
                link(dve.tensor_tensor(nwt[:, 0:n], r0[:, 0:n], r0[:, 0:n], ALU.mult))
                link(dve.tensor_tensor(nwt[:, 0:n], nwt[:, 0:n], ve[:, 0:n], ALU.mult))
                link(dve.tensor_scalar(nwt[:, 0:n], nwt[:, 0:n], -0.5, 1.5, ALU.mult, ALU.add))
                dve.tensor_tensor(r, r0[:, 0:n], nwt[:, 0:n], ALU.mult).then_inc(done, 1)

            def row_stats(tiles):
                for i, t in enumerate(tiles):
                    link(dve.bn_stats(stats[:, t % 2, :], xs[:, t, :]))
                    link(dve.bn_aggr(mv[:, t, :], stats[:, t % 2, :]))
                dve.tensor_scalar(ve[:, 0:len(tiles)], mv[:, tiles[0]:tiles[-1] + 1, 1], LN_EPS, None, ALU.add).then_inc(var_ready, 1)

            dve.wait_ge(ld_x[0], 16)
            row_stats(range(TB))
            polish(TB, r0_ready, 1, rln[:, 0:TB], rln_ready)
            dve.wait_ge(ld_x[1], 16)
            row_stats(range(TB, NT))
            polish(NT - TB, r0_ready, 2, rln[:, TB:NT], rln_ready)
            dve.wait_ge(rln_ready, 2)
            for k in stage_slots():
                t = k - 4
                if 0 <= t < NT:
                    for g in range(2, 4):
                        dve.wait_ge(qk_ps, 4 * t + g + 1)
                        dve.tensor_copy(qkT[:, 1, 4 * (g - 2):4 * (g - 2) + 4, t * P:(t + 1) * P],
                                        ps[5 + g % 2][:].rearrange("p (a n) -> p a n", a=4)).then_inc(qkD, 1)
                t = k - 1
                if 0 <= t < NT:
                    if t == 0:
                        dve.wait_ge(ld_small, 16 * 15)
                    dve.wait_ge(c_ps, t + 1)
                    if t >= 2:
                        dve.wait_ge(cT_ps, t - 1)
                    dve.tensor_tensor(rr[:, t % 3, 1, :], ps[1][:, 128:192], b1[:, 128:192], ALU.add)
                    dve.tensor_tensor(c1[:, t % 2, :], ps[1][:, 0:128], b1[:, 0:128], ALU.add).then_inc(c_ready, 1)
                t = k
                if 0 <= t < NT:
                    if t >= 2:
                        dve.wait_ge(xnT_ps, t - 1)
                    dve.tensor_scalar(xn[:, t % 2, :], xs[:, t, :], mv[:, t, 0:1], rln[:, t:t + 1], ALU.subtract,
                                      ALU.mult).then_inc(xn_ready, 1)
                t = k - 3
                if 0 <= t < NT:
                    dve.wait_ge(kvq_ps, t + 1)
                    if t >= 2:
                        dve.wait_ge(lo_ready, 2 * (t - 1))
                        dve.wait_ge(hi_ready, t - 1)

                    def heads(a):
                        return a.rearrange("p (h d) -> p h d", h=NH)
                    dve.tensor_tensor(cat[:, t % 2, 1, :, 0:DH], heads(ps[3][:, 0:D]), heads(b2[:, 0:D]), ALU.add)
                    if t == 0:
                        dve.wait_ge(consts, 1)
                    dve.tensor_tensor(va[:, t, :, 0:DH], heads(ps[3][:, D:2 * D]), heads(b2[:, D:2 * D]), ALU.add)
                    dve.tensor_tensor(cat[:, t % 2, 0, :, 0:DH], heads(ps[4][:, 0:D]), heads(b2[:, 2 * D:3 * D]), ALU.add)
                    dve.tensor_tensor(rr[:, t % 3, 0, :], ps[4][:, D:D + DC], b2[:, 3 * D:3 * D + DC],
                                      ALU.add).then_inc(kvq_read, 1)
                    dve.wait_ge(kvq_read, t + 1)
                    dve.wait_ge(c_ready, t + 1)
                    rin = rr[:, t % 3].rearrange("p a (h d) -> p (a h) d", d=DR)
                    cos4 = cs[:, t % TB, 0:1, :].to_broadcast([P, 2 * NH, DR])
                    sin4 = cs[:, t % TB, 1:2, :].to_broadcast([P, 2 * NH, DR])
                    dve.tensor_tensor(rp1[:], rin, cos4, ALU.mult)
                    link(dve.tensor_tensor(rp2[:], rin, sin4, ALU.mult))
                    co = cat[:, t % 2].rearrange("p a h d -> p (a h) d")
                    dve.tensor_tensor(co[:, :, DH:DH + 2], rp1[:, :, 0:DR:2], rp1[:, :, 1:DR:2], ALU.subtract)
                    dve.tensor_tensor(co[:, :, DH + 2:DQ], rp2[:, :, 0:DR:2], rp2[:, :, 1:DR:2], ALU.add).then_inc(cat_ready, 1)

            for u in range(UNITS + P2_LAG + PV_LAG + 3):
                if u < UNITS:
                    b, h = u // NH, u % NH
                    dve.wait_ge(s1_ps, u + 1)
                    if h == 0 and b >= 2:
                        dve.wait_ge(m_lo, b - 1)
                    dve.tensor_reduce(mneg[:, b % 2, :, h:h + 1], ps[(17 * b + h) % 2][:].rearrange("p (q k) -> p q k", q=TB),
                                      X, ALU.max, negate=True).then_inc(s1_max, 1)
                b = (u - M_LAG + 1) // NH
                if u >= M_LAG - 1 and (u - M_LAG + 1) % NH == 0 and b < B:
                    dve.wait_ge(m_hi, b + 1)
                    dve.tensor_tensor(msp[:, :, :, 1, :], mneg[:, b % 2].rearrange("p q (a j) -> p q j a", j=2),
                                      msp[:, :, :, 0, :].bitcast(F32), ALU.subtract).then_inc(m_lo, 1)
                v = u - P2_LAG - PV_LAG - 1
                if v >= 0 and v % NH == NH - 1:
                    b = v // NH
                    dve.wait_ge(o_ps, NH * (b + 1))
                    for q in range(TB):
                        o = ps[4 + 2 * (b % 2) + q][:, 0:NH * (DH + 1)].rearrange("p (h d) -> p h d", h=NH)
                        link(dve.reciprocal(rsv[:, q, :].unsqueeze(2), o[:, :, DH:DH + 1]))
                        link(dve.tensor_tensor(osa[:, q], o[:, :, 0:DH], rsv[:, q, :].unsqueeze(2).to_broadcast([P, NH, DH]), ALU.mult))
                    dve.tensor_tensor(xs[:, TB * b:TB * b + TB, :], xs[:, TB * b:TB * b + TB, :],
                                      osa[:].rearrange("p q h d -> p q (h d)"), ALU.add).then_inc(x1_ready, 1)

            dve.wait_ge(x1_ready, B)
            dve.wait_ge(w_split, len(chunks))
            dve.wait_ge(bias_placed, 16 * 12)
            for s in range(FIRST, LAST):
                if 0 <= s - 1 < 8 * B * KV:
                    i = s - 1
                    dve.wait_ge(exp_done, i + 1)
                    dve.reciprocal(rinv[:, i % 3:i % 3 + 1], psm[:, i % 3:i % 3 + 1]).then_inc(rinv_ready, 1)
                    dve.wait_ge(rinv_ready, i + 1)
                    dve.tensor_scalar(pb[:, i % 3, :], pb[:, i % 3, :], rinv[:, i % 3:i % 3 + 1], None,
                                      ALU.mult).then_inc(p_normed, 1)
                if 0 <= s - 2 < 8 * B * KV:
                    i = s - 2
                    dve.wait_ge(pT_hi, i + 1)
                    cols = slice((i % 2) * P, (i % 2 + 1) * P)
                    dve.tensor_tensor(pT[1][:, (i // 2) % 2, :, cols], ps[2 + i % 2][:].rearrange("p (k n) -> p k n", k=KT_),
                                      pT[0][:, (i // 2) % 2, :, cols].bitcast(F32), ALU.subtract).then_inc(pT_lo, 1)
                if 0 <= s < 8 * B * KV:
                    dve.wait_ge(S_ps, s + 1)
                    if s == 0:
                        dve.wait_ge(ld_mask, 16)
                    if s >= 3:
                        dve.wait_ge(pT_ps, s - 2)
                    dve.tensor_tensor_reduce(pb[:, s % 3, :], ps[s % 2][:], msk[:, s % 2, :], -1.0, 3.0e38, ALU.add, ALU.min,
                                             nmax[:, s % 3:s % 3 + 1]).then_inc(S_masked, 1)
                if s >= 4 and s % 2 == 0 and (s - 4) // 2 < B * XH:
                    h = (s - 4) // 2
                    dve.wait_ge(o_hi, h + 1)
                    dve.tensor_tensor(oT[1][:], ps[4][:, 0:T], oT[0][:].bitcast(F32), ALU.subtract).then_inc(o_lo, 1)
                if s >= 5 and s % 2 == 1 and (s - 5) // 2 < B * XH and ((s - 5) // 2) % XH == XH - 1:
                    h = (s - 5) // 2
                    b = h // XH
                    dve.wait_ge(wo_ps, h + 1)
                    dve.tensor_tensor(xs[:, TB * b:TB * b + TB, :], ps[5][:].rearrange("p (q d) -> p q d", q=TB),
                                      xs[:, TB * b:TB * b + TB, :], ALU.add).then_inc(x2_ready, 1)
                for task in tasks.get(s, ()):
                    kind, *a = task
                    if task in side:
                        bank = side_bank(task)
                    if kind == "LNV":
                        row_stats(range(TB * a[0], TB * a[0] + TB))
                    if kind == "LNW":
                        b, = a
                        polish(TB, r0_ready, 3 + b, rln[:, TB * b:TB * b + TB], rln_ready)
                        dve.wait_ge(rln_ready, 3 + b)
                        if b:
                            dve.wait_ge(m_ps, side[("XT", b - 1)] + 1)
                        for q in range(TB):
                            t = TB * b + q
                            dve.tensor_scalar(xnD[:, q, :], xs[:, t, :], mv[:, t, 0:1], rln[:, t:t + 1], ALU.subtract,
                                              ALU.mult).then_inc(xnD_ready, 1)
                    if kind == "CT":
                        b, c = a
                        dve.wait_ge(ctx_hi, 2 * b + c + 1)
                        dve.tensor_tensor(ctxT[1][:, c, :], bank[:], ctxT[0][:, c, :].bitcast(F32), ALU.subtract).then_inc(ctx_lo, 1)
                    if kind == "XT":
                        b, = a
                        dve.wait_ge(xT_hi, b + 1)
                        dve.tensor_tensor(xT[1][:].rearrange("p c n -> p (c n)"), bank[:],
                                          xT[0][:].rearrange("p c n -> p (c n)").bitcast(F32), ALU.subtract).then_inc(xT_lo, 1)
                    if kind == "SS":
                        which, i, t = a
                        u = norm_unit[(which, i, t)]
                        dve.wait_ge(sq_ready, u + 1)
                        to = (ssK if which == "K" else ssQ)[:, 4 * t:4 * t + 4]
                        dve.tensor_reduce(to, sq[:, u % 2, :].rearrange("p (g d) -> p g d", g=4), X, ALU.add).then_inc(ss_ready, 1)
                    if kind == "VE":
                        which, i = a
                        ss, n = (ssK, 16) if which == "K" else (ssQ, 8)
                        u = norm_unit[(which, i, n // 4 - 1)]
                        dve.wait_ge(ss_ready, u + 1)
                        dve.tensor_scalar(ve[:, 0:n], ss[:], 1.0 / HD, RMS_EPS, ALU.mult, ALU.add).then_inc(rk_var, 1)
                    if kind == "NW":
                        n = norm_chain[tuple(a)]
                        r = rK if a[0] == "K" else rQ
                        polish(16 if a[0] == "K" else 8, rk_r0, n + 1, r[:], rk_ready)
                    if kind == "KT":
                        n, = a
                        dve.wait_ge(kT_hi, n + 1)
                        dve.scalar_tensor_tensor(kT[1][:, n % 2, :], bank[:], wqk[:, 0:1], kT[0][:, n % 2, :].bitcast(F32),
                                                 ALU.mult, ALU.subtract).then_inc(kT_lo, 1)
                    if kind == "QT":
                        n, qt = a
                        dve.wait_ge(qT_hi, 2 * n + qt + 1)
                        dve.tensor_tensor(qT[1][:, n % 2, qt, :], bank[:], qT[0][:, n % 2, qt, :].bitcast(F32),
                                          ALU.subtract).then_inc(qT_lo, 1)

            dve.wait_ge(x2_ready, B)
            row_stats(range(NT))
            polish(NT, r0_ready, 3 + B, rln[:], rln_ready)
            dve.wait_ge(rln_ready, 3 + B)
            for t in range(NT):
                dve.tensor_scalar(xn3[:, t, :], xs[:, t, :], mv[:, t, 0:1], rln[:, t:t + 1], ALU.subtract,
                                  ALU.mult).then_inc(xn3_ready, 1)

            def by_row(a):
                return a.unsqueeze(2).to_broadcast([P, NT, EW])
            experts = iota_e[:].unsqueeze(1).to_broadcast([P, NT, EW])

            def pick(k):
                link(dve.tensor_reduce(top[k][:], lg[:], X, ALU.max))
                link(dve.tensor_tensor(eq[:], lg[:], by_row(top[k][:]), ALU.is_equal))
                link(dve.scalar_tensor_tensor(eq[:], eq[:], -float(EW), experts, ALU.mult, ALU.add))
                link(dve.tensor_reduce(first_e[:], eq[:], X, ALU.min))
                link(dve.tensor_tensor(oh[k][:], eq[:], by_row(first_e[:]), ALU.is_equal))

            dve.wait_ge(consts, 8)
            link(dve.memset(lg[:, :, NE:EW], FINITE_LOW))
            dve.wait_ge(gate_ps, 1)
            link(dve.tensor_copy(lg[:, :, 0:NE], ps[4][:, 0:NT * EW].rearrange("p (t e) -> p t e", t=NT)[:, :, 0:NE]))
            pick(0)
            dve.tensor_tensor(lg[:], lg[:], by_row(top[0][:]), ALU.subtract).then_inc(lgm_ready, 1)
            dve.wait_ge(lge_ready, 1)
            link(dve.scalar_tensor_tensor(lg[:], oh[0][:], FINITE_LOW, lg[:], ALU.mult, ALU.add))
            pick(1)
            dve.tensor_tensor(chosen[:], oh[0][:], oh[1][:], ALU.add).then_inc(chosen_ready, 1)
            link(dve.tensor_reduce(top[0][:], lge[:], X, ALU.add))
            link(dve.reciprocal(cw[0][:], top[0][:]))
            link(dve.tensor_tensor(lge[:], lge[:], oh[1][:], ALU.mult))
            link(dve.tensor_reduce(top[1][:], lge[:], X, ALU.add))
            link(dve.tensor_tensor(cw[1][:], top[1][:], cw[0][:], ALU.mult))

            def product(i, par):
                dve.wait_ge(sg_ready, i + 1)
                dve.tensor_tensor(hh[:, par, :], ps[2 + par][:, INTER:2 * INTER], sg[:, par, :], ALU.mult).then_inc(hh_ready, 1)

            def turn_hidden(i, par):
                dve.wait_ge(h_ps, i + 1)
                dve.tensor_copy(hT[:, par].rearrange("p c n -> p (c n)"), ps[4 + par][0:IH, 0:2 * P]).then_inc(hT_ready, 1)

            def add_shared(t):
                dve.wait_ge(y_ps, t + 1)
                dve.tensor_tensor(xs[:, t, :], ps[6 + t % 2][:, 0:D], xs[:, t, :], ALU.add).then_inc(y_read, 1)

            def keep_result(j, par, stored):
                if stored is not None:
                    dve.wait_ge(y_st[par], stored)
                dve.wait_ge(y_ps, j + NT + 1)
                dve.tensor_copy(ys[:, par, :], ps[6 + par][:, 0:D]).then_inc(y_read, 1)

            for i in range(NT + 1):
                if i >= 2:
                    dve.wait_ge(h_ps, i - 1)
                product(i, i % 2)
                if i >= 1:
                    add_shared(i - 1)
                turn_hidden(i, i % 2)
                if i == 1:
                    dve.wait_ge(rank_ps, 1)
                    per_tile = ps[0][:, P:2 * P].rearrange("p (t e) -> p t e", t=NT)
                    link(dve.tensor_copy(tot[:], per_tile))
                    link(dve.memset(before[:, 0, :], 0.0))
                    for t in range(NT):
                        link(dve.tensor_tensor(before[:, t + 1, :], before[:, t, :], tot[:, t, :], ALU.add))
                    count = before[:, NT, :].unsqueeze(2).to_broadcast([P, EW, NT])
                    link(dve.tensor_tensor(more[:], count, iota_t[:].unsqueeze(1).to_broadcast([P, EW, NT]), ALU.is_gt))
                    link(dve.tensor_reduce(ntile[:], more[:], X, ALU.add))
                    link(dve.tensor_tensor_scan(tend[:], onesf[:, 0:EW], ntile[:], 0.0, ALU.mult, ALU.add))
                    link(dve.tensor_tensor(ntile[:], tend[:], ntile[:], ALU.subtract))
                    rank = ps[0][:, 0:P].rearrange("p (t e) -> p t e", t=NT)
                    link(dve.tensor_tensor(pos[:], rank, before[:, 0:NT, :], ALU.add))
                    link(dve.scalar_tensor_tensor(pos[:], ntile[:].unsqueeze(1).to_broadcast([P, NT, EW]), float(P), pos[:],
                                                  ALU.mult, ALU.add))
                    for k in range(2):
                        link(dve.tensor_tensor(eq[:], oh[k][:], pos[:], ALU.mult))
                        link(dve.tensor_reduce(slotf[:, k, :], eq[:], X, ALU.add))
                    dve.tensor_copy(sloti[:], slotf[:]).then_inc(slots_ready, 1)
                    link(dve.tensor_tensor(isof[:], iota_j[:].unsqueeze(2).to_broadcast([P, 32, EW]),
                                           tend[:].unsqueeze(1).to_broadcast([P, 32, EW]), ALU.is_ge))
                    link(dve.tensor_reduce(expf[:], isof[:], X, ALU.add))
                    link(dve.tensor_scalar(expf[:], expf[:], float(NE - 1), None, ALU.min))
                    dve.tensor_copy(expi[:], expf[:]).then_inc(slots_ready, 1)
            def two_tiles(k, stored):
                for par in range(2):
                    j = 2 * k + par + 1
                    dve.wait_ge(h_ps, j + (NT - 1))
                    product(j + NT, 1 - par)
                    keep_result(j - 1, par, stored)
                    turn_hidden(j + NT, 1 - par)

            two_tiles(0, None)
            with dve.Fori(1, NSLOT // 2 - 1) as k:
                two_tiles(k, 16 * k)
            last = NSLOT - 1
            dve.wait_ge(h_ps, last + NT - 1)
            product(last + NT, 1)
            keep_result(last - 1, 0, 16 * (last // 2))
            turn_hidden(last + NT, 1)
            keep_result(last, 1, 16 * (last // 2))
            for t in range(NT):
                dve.wait_ge(gathered[t], 32)
                link(dve.scalar_tensor_tensor(xs[:, t, :], yg[0][:, t, :], cw[0][:, t:t + 1], xs[:, t, :], ALU.mult, ALU.add))
                dve.scalar_tensor_tensor(xs[:, t, :], yg[1][:, t, :], cw[1][:, t:t + 1], xs[:, t, :], ALU.mult,
                                         ALU.add).then_inc(done, 1)

        @block.tensor
        def _(pe):
            def split_product(o, lhs, rhs, first, last):
                for i, (a, b) in enumerate(((0, 0), (0, 1), (1, 0))):
                    ins = pe.matmul(o, lhs[a], rhs[b], start=first and i == 0, stop=last and i == 2, skip_group_check=True)
                return ins

            def add_bias(bank, j):
                rows = slice(32 * (j % 4), 32 * (j % 4) + 2)
                return pe.matmul(bank[:], ones2[rows, :], bias_hl[rows, j // 4, :], start=False, stop=True, skip_group_check=True)

            pe.wait_ge(consts, 4)
            for k in stage_slots():
                t = k - 4
                if 0 <= t < NT:
                    pe.wait_ge(lo_ready, 2 * t + 2)
                    for g in range(4):
                        if g < 2 and t:
                            pe.wait_ge(qkD, 2 * (t - 1) + g + 1)
                        if g >= 2:
                            pe.wait_ge(qkA, 2 * t + g - 1)
                        for i in range(4):
                            pair = 4 * (g % 2) + i
                            ins = pe.transpose(ps[5 + g % 2][:, i * P:(i + 1) * P],
                                               qks[:, t % 2, g // 2, 2 * pair:2 * pair + 2, :].rearrange("p h d -> p (h d)").bitcast(F32), ident[:])
                        ins.then_inc(qk_ps, 1)
                t = k - 3
                if 0 <= t < NT:
                    pe.wait_ge(cT_ready, t + 1)
                    if t:
                        pe.wait_ge(kvq_read, t)
                    pe.matmul(ps[3][:], cT[0:DC, t % 2, :], w2kv[:], start=True, stop=True)
                    pe.matmul(ps[4][:, 0:D + DC], cT[DC:P, t % 2, :], w2q[DC:P, :], start=True, stop=True).then_inc(kvq_ps, 1)
                t = k - 2
                if 0 <= t < NT:
                    pe.wait_ge(c_ready, t + 1)
                    if t:
                        pe.wait_ge(cT_ready, t)
                    pe.transpose(ps[2][:, 0:P], c1[:, t % 2, :], ident[:]).then_inc(cT_ps, 1)
                t = k - 1
                if 0 <= t < NT:
                    pe.wait_ge(xnT_ready, t + 1)
                    if t == 0:
                        pe.wait_ge(ld_small, 16 * 15)
                    if t:
                        pe.wait_ge(c_ready, t)
                    for c in range(C):
                        ins = pe.matmul(ps[1][:, 0:192], xnT[:, t % 2, c, :], w1[:, c, :], start=c == 0, stop=c == C - 1)
                    ins.then_inc(c_ps, 1)
                t = k
                if 0 <= t < NT:
                    pe.wait_ge(xn_ready, t + 1)
                    if t:
                        pe.wait_ge(xnT_ready, t)
                    for c in range(C):
                        ins = pe.transpose(ps[0][:, c * P:(c + 1) * P], xn[:, t % 2, c * P:(c + 1) * P], ident[:])
                    ins.then_inc(xnT_ps, 1)

            pe.wait_ge(qkA, 2 * NT)
            pe.wait_ge(qkD, 2 * NT)
            for u in range(UNITS + P2_LAG + PV_LAG + 1):
                if u < UNITS:
                    b, h = u // NH, u % NH
                    unit = 17 * b + h
                    lo = HW * (h % 2)
                    if h == 1 and b:
                        pe.wait_ge(mT_ready, b)
                    elif u >= 2:
                        pe.wait_ge(s1_max, u if h == 0 else u - 1)
                    for q in range(TB):
                        t = TB * b + q
                        ins = pe.matmul(ps[unit % 2][:, q * T:(q + 1) * T], qkT[lo:lo + KS, 0, h // 2, t * P:(t + 1) * P],
                                        qkT[lo:lo + KS, 1, h // 2, b * T:(b + 1) * T], start=True, stop=True)
                    ins.then_inc(s1_ps, 1)
                b = (u - M_LAG + 1) // NH
                if u >= M_LAG - 1 and (u - M_LAG + 1) % NH == 0 and b < B:
                    pe.wait_ge(m_lo, b + 1)
                    for q in range(TB):
                        ins = pe.transpose(ps[(17 * b + 16) % 2][0:32, q * P:(q + 1) * P],
                                           msp[:, q].rearrange("p a b c -> p (a b c)").bitcast(F32), ident[:])
                    ins.then_inc(mT_ps, 1)
                v = u - P2_LAG
                if 0 <= v < UNITS:
                    b, h = v // NH, v % NH
                    lo = HW * (h % 2)
                    if h == 0:
                        pe.wait_ge(mrow, 64 * (b + 1))
                    if v >= 2:
                        pe.wait_ge(pTs_ready, v - 1)
                    for kc in range(TB):
                        t = TB * b + kc
                        ins = pe.matmul(ps[2 + v % 2][:, kc * T:(kc + 1) * T], qkT[lo:lo + KM, 1, h // 2, t * P:(t + 1) * P],
                                        qkT[lo:lo + KM, 0, h // 2, b * T:(b + 1) * T], start=True, stop=True)
                    ins.then_inc(sT_ps, 1)
                v = u - P2_LAG - PV_LAG
                if 0 <= v < UNITS:
                    b, h = v // NH, v % NH
                    pe.wait_ge(pTs_ready, v + 1)
                    if h == 0 and b >= 2:
                        pe.wait_ge(x1_ready, b - 1)
                    for q in range(TB):
                        for kc in range(TB):
                            ins = pe.matmul(ps[4 + 2 * (b % 2) + q][:, h * (DH + 1):(h + 1) * (DH + 1)],
                                            pTs[:, v % 3, kc, q * P:(q + 1) * P], va[:, TB * b + kc, h, :],
                                            start=kc == 0, stop=kc == TB - 1)
                    ins.then_inc(o_ps, 1)

            pe.wait_ge(x1_ready, B)
            pe.wait_ge(w_split, len(chunks))
            pe.wait_ge(bias_placed, 16 * 12)
            STEPS = 8 * B * KV
            for s in range(FIRST, LAST):
                if 0 <= s - 2 < STEPS:
                    i = s - 2
                    pe.wait_ge(p_normed, i + 1)
                    if i >= 2:
                        pe.wait_ge(pT_lo, i - 1)
                    for kt in range(KT_):
                        ins = pe.transpose(ps[2 + i % 2][:, kt * P:(kt + 1) * P], pb[:, i % 3, kt * P:(kt + 1) * P], ident[:])
                    ins.then_inc(pT_ps, 1)
                if 0 <= s < STEPS:
                    n, r, q = s // 8, (s % 8) // 2, s % 2
                    pe.wait_ge(kT_lo, n + 1)
                    pe.wait_ge(qT_lo, 2 * n + q + 1)
                    if s >= 2:
                        pe.wait_ge(S_masked, s - 1)
                    split_product(ps[s % 2][:], [z[:, n % 2, q, r * P:(r + 1) * P] for z in qT],
                                  [z[:, n % 2, :] for z in kT], True, True).then_inc(S_ps, 1)
                if s >= 4 and s % 2 == 0 and (s - 4) // 2 < B * XH:
                    h = (s - 4) // 2
                    n = h // GR
                    pe.wait_ge(pT_lo, 2 * h + 2)
                    pe.wait_ge(v_split, n + 1)
                    if h:
                        pe.wait_ge(o_lo, h)
                    for kt in range(KT_):
                        ins = split_product(ps[4][:, 0:T], [z[:, n % 2, kt, :] for z in vS], [z[:, h % 2, kt, :] for z in pT],
                                            kt == 0, kt == KT_ - 1)
                    ins.then_inc(pv_ps, 1)
                if s >= 5 and s % 2 == 1 and (s - 5) // 2 < B * XH:
                    h = (s - 5) // 2
                    b, hd = h // XH, h % XH
                    pe.wait_ge(o_lo, h + 1)
                    if hd == 0 and b:
                        pe.wait_ge(x2_ready, b)
                    if h == 0:
                        pe.wait_ge(wo_split, len(wo_chunks))
                    for q in range(TB):
                        ins = split_product(ps[5][:, q * D:(q + 1) * D], [z[:, q * P:(q + 1) * P] for z in oT],
                                            [z[:, hd, :] for z in WoS], hd == 0 and q == 0, hd == XH - 1)
                    ins.then_inc(wo_ps, 1)
                for task in tasks.get(s, ()):
                    kind, *a = task
                    if task not in side:
                        continue
                    m = side[task]
                    bank = side_bank(task)
                    if m >= 2:
                        pe.wait_ge(*released(side_order[m - 2]))
                    if kind == "CT":
                        b, c = a
                        pe.wait_ge(ld_ctx, 16 * (b + 1))
                        for kt in range(KT_):
                            ins = pe.transpose(bank[:, kt * P:(kt + 1) * P], craw[:, kt, c * P:(c + 1) * P], ident[:])
                    if kind == "XT":
                        b, = a
                        pe.wait_ge(xnD_ready, TB * (b + 1))
                        for c in range(C):
                            for q in range(TB):
                                ins = pe.transpose(bank[:, c * T + q * P:c * T + (q + 1) * P], xnD[:, q, c * P:(c + 1) * P], ident[:])
                    if kind in ("KP", "VP"):
                        b, kt = a
                        pe.wait_ge(ctx_lo, 2 * (b + 1))
                        off, j = (OFF_K, 4) if kind == "KP" else (OFF_V, 5)
                        for c in range(C):
                            split_product(bank[:], [z[:, c, kt * P:(kt + 1) * P] for z in ctxT],
                                          [z[:, off + c * 512:off + (c + 1) * 512] for z in Wkvq], c == 0, False)
                        ins = add_bias(bank, j)
                    if kind == "QP":
                        n, qt = a
                        g = n % 4
                        pe.wait_ge(xT_lo, n // 4 + 1)
                        for c in range(C):
                            off = OFF_Q + c * 2048 + g * GW
                            split_product(bank[:], [z[:, c, qt * P:(qt + 1) * P] for z in xT],
                                          [z[:, off:off + GW] for z in Wkvq], c == 0, False)
                        ins = add_bias(bank, g)
                    if kind == "KT":
                        n, = a
                        pe.wait_ge(normed, norm_chain[("K", n // 4)] + 1)
                        for kt in range(KT_):
                            ins = pe.transpose(bank[:, kt * P:(kt + 1) * P], kraw[:, kt, (n % 4) * HD:(n % 4 + 1) * HD], ident[:])
                    if kind == "QT":
                        n, qt = a
                        pe.wait_ge(normed, norm_chain[("Q", n)] + 1)
                        for r in range(GR):
                            ins = pe.transpose(bank[:, r * P:(r + 1) * P], qraw[:, qt, r * P:(r + 1) * P], ident[:])
                    ins.then_inc(m_ps, 1)


            for u in range(4):
                pe.wait_ge(xn3_ready, 4 * (u % 2) + 4)
                if u == 0:
                    pe.wait_ge(x2_ready, B)
                for i in range(4):
                    t = 4 * (u % 2) + i
                    ins = pe.transpose(ps[u][:, i * P:(i + 1) * P], xn3[:, t, (u // 2) * P:(u // 2 + 1) * P], ident[:])
                ins.then_inc(x3_ps, 1)
            pe.wait_ge(x3_T, 4)
            pe.wait_ge(ld_shared, 48)
            for t in range(NT):
                for c in range(C):
                    ins = pe.matmul(ps[4][:, t * EW:t * EW + NE], xn3T[:, c, t * P:(t + 1) * P], gw[:, c, 0:NE],
                                    start=c == 0, stop=c == C - 1)
            ins.then_inc(gate_ps, 1)

            def up(i, par, lhs, e):
                for c in range(C):
                    ins = pe.matmul(ps[2 + par][:, 0:2 * INTER], lhs[c], w13[:, e, c, :], start=c == 0, stop=c == C - 1)
                ins.then_inc(up_ps, 1)

            def turn_hidden(i, par):
                pe.wait_ge(hh_ready, i + 1)
                for c in range(2):
                    ins = pe.transpose(ps[4 + par][0:IH, c * P:(c + 1) * P], hh[:, par, c * IH:(c + 1) * IH], ident[:])
                ins.then_inc(h_ps, 1)

            def down(i, par, e):
                pe.wait_ge(hT_ready, i + 1)
                for c in range(2):
                    ins = pe.matmul(ps[6 + par][:, 0:D], hT[:, par, c, :], w2s[:, e, c, :], start=c == 0, stop=c == 1)
                ins.then_inc(y_ps, 1)

            def turn_rows(j, par, ld):
                pe.wait_ge(xg_ld[par], ld)
                for c in range(C):
                    ins = pe.transpose(ps[par][:, c * P:(c + 1) * P], xg[:, par, c * P:(c + 1) * P], ident[:])
                ins.then_inc(xg_ps, 1)

            for i in range(NT):
                if i >= 2:
                    pe.wait_ge(hh_ready, i - 1)
                up(i, i % 2, [xn3T[:, c, i * P:(i + 1) * P] for c in range(C)], NE)
                if i == 0:
                    pe.wait_ge(chosen_ready, 1)
                    flat = chosen[:].rearrange("p t e -> p (t e)")
                    pe.matmul(ps[0][:, 0:P], upper[:], flat, start=True, stop=True)
                    pe.matmul(ps[0][:, P:2 * P], onesf[:], flat, start=True, stop=True).then_inc(rank_ps, 1)
                if i >= 1:
                    if i >= 3:
                        pe.wait_ge(y_read, i - 2)
                    down(i - 1, (i - 1) % 2, NE)
                turn_hidden(i, i % 2)

            pe.wait_ge(slots_ready, 2)
            pe.wait_ge(ld_e, 16 * 6)

            def expert(j):
                return pe.value_load(expi[0:1, bass.ds(j, 1)], min_val=0, max_val=NE - 1)

            def routed(j, par, down_before, e_before, turn_next):
                e = expert(j)
                pe.wait_ge(xgT_ready, j + 1)
                pe.wait_ge(hh_ready, j + (NT - 1))
                for c in range(C):
                    ins = pe.matmul(ps[2 + par][:, 0:2 * INTER], xgT[:, par, c, :],
                                    w13[:, bass.ds(e, 1), c, :].rearrange("p e n -> p (e n)"), start=c == 0, stop=c == C - 1)
                ins.then_inc(up_ps, 1)
                pe.wait_ge(y_read, j + (NT - 2))
                pe.wait_ge(hT_ready, j + NT)
                for c in range(2):
                    if e_before is None:
                        rhs = w2s[:, NE, c, :]
                    else:
                        rhs = w2s[:, bass.ds(e_before, 1), c, :].rearrange("p e n -> p (e n)")
                    ins = pe.matmul(ps[7 - par][:, 0:D], hT[:, 1 - par, c, :], rhs, start=c == 0, stop=c == 1)
                ins.then_inc(y_ps, 1)
                turn_hidden(j + NT, par)
                if turn_next is not None:
                    turn_rows(j + 1, 1 - par, turn_next)
                return e

            turn_rows(0, 0, 16)
            routed(0, 0, None, None, 16)
            with pe.Fori(0, NSLOT // 2 - 1) as k:
                for par in (1, 0):
                    j = 2 * k + 2 - par
                    routed(j, par, None, expert(j - 1), 16 * (k + 2))
            last = NSLOT - 1
            e = routed(last, 1, None, expert(last - 1), None)
            pe.wait_ge(hT_ready, last + NT + 1)
            for c in range(2):
                ins = pe.matmul(ps[7][:, 0:D], hT[:, 1, c, :], w2s[:, bass.ds(e, 1), c, :].rearrange("p e n -> p (e n)"),
                                start=c == 0, stop=c == 1)
            ins.then_inc(y_ps, 1)


_INS = ["x", "ctx_2048", "mask_1xSxS2_ff0"] + ["L0_attn_" + n for n in (
    "W_DKV", "b_DKV", "W_UK", "b_UK", "W_UV", "b_UV", "W_DQ", "b_DQ", "W_UQ", "b_UQ", "W_QR", "b_QR", "W_KR", "b_KR")] + [
    "L0_xattn_" + n for n in ("Wq", "bq", "Wk", "bk", "Wv", "bv", "Wo", "qn_w", "kn_w")]


def rope_table():
    f32 = np.float32
    freqs = f32(10000.0) ** (-(np.arange(0, DR, 2, dtype=f32) / f32(DR)))
    theta = np.arange(T, dtype=f32)[:, None] * freqs[None, :]
    cos, sin = np.cos(theta), np.sin(theta)
    rows = np.stack([np.stack([cos, sin], -1).reshape(T, DR), np.stack([sin, cos], -1).reshape(T, DR)], 1)
    return np.ascontiguousarray(rows.reshape(TB, P, 2, DR).transpose(1, 0, 2, 3).astype(f32))


def kernel(**inputs):
    import concourse.bacc as bacc
    from concourse.bass_utils import run_bass_kernel_spmd

    nc = bacc.Bacc("TRN2", target_bir_lowering=False, num_devices=1)
    arrays, args = {}, []

    def give(name, a):
        arrays[name] = a
        args.append(nc.dram_tensor(name, a.shape, mybir.dt.from_np(a.dtype), kind="ExternalInput").ap())

    for name in _INS:
        give(f"in_{name}", np.ascontiguousarray(inputs[name]))
    f = {n: inputs["L0_ffn_" + n] for n in ("gate_w", "w1", "w2", "w3", "sw1", "sw2", "sw3")}
    give("gate_wT", np.ascontiguousarray(f["gate_w"].T))
    w1, w3, w2 = (np.concatenate([f[n], f["s" + n][None]]) for n in ("w1", "w3", "w2"))
    give("w13T", np.ascontiguousarray(np.concatenate([w1, w3], 1).transpose(0, 2, 1)))
    give("w2T", np.ascontiguousarray(w2.transpose(0, 2, 1)))
    give("rope_cs", rope_table())
    args.append(nc.dram_tensor("out_0", (B, T, D), F32, kind="ExternalOutput").ap())
    layer(nc, *args)
    r = run_bass_kernel_spmd(nc, [arrays], core_ids=[0])
    return r.results[0]["out_0"]
```

```python
from contextlib import ExitStack

import numpy as np

import concourse.bass as bass
from concourse import mybir

F32 = mybir.dt.float32
F32R = mybir.dt.float32r
ALU = mybir.AluOpType
ACT = mybir.ActivationFunctionType
X = mybir.AxisListType.X

P = 128
B, T, D = 4, 256, 256
NT = B * T // P
TB = T // P
LN1_SETS = NT // TB
C = D // P
LN_EPS = 1e-5
NH, DC = 16, 64
DH, DR = D // NH, DC // NH
DQ = DH + DR
HW = 64
KS = 3 * DQ
KM = KS + 2
VW = 32
NP = NH // 2
SA_SCALE = float(DQ) ** -0.5
SE, XH, KV, HD = 512, 16, 4, 128
KT_ = SE // P
GR = XH // KV
GW = GR * HD
RMS_EPS = 1e-6
XSCALE = float(HD) ** -0.5

NE, INTER = 15, 176
IH = INTER // 2
EW = 16
XG = 4
NSLOT = (2 * B * T - NE) // P + NE
FINITE_LOW = -3.0e38


def xattn_tasks():
    tasks = {}

    def put(slot, *task):
        tasks.setdefault(slot, []).append(task)

    for b in range(B):
        lead = 8 * (4 * b - 2) if b else -19
        own = 8 * (4 * b - 1) if b else -10
        put(lead + 0, "LNV", b)
        put(lead + 0, "CT", b, 0)
        put(lead + 2, "CT", b, 1)
        put(lead + 2, "LNW", b)
        put(lead + 3, "XT", b)
        for kt in range(KT_):
            put(own - 3 + kt, "KP", b, kt)
            put(own - 1 + kt, "SS", "K", b, kt)
            put(own + 1 + kt, "VP", b, kt)
        put(own + 2, "VE", "K", b)
        put(own + 3, "NW", "K", b)
    for n in range(B * KV):
        own = 8 * (n - 1) if n else -10
        for qt in range(TB):
            put(own - 1 + 2 * qt, "QP", n, qt)
            put(own + 1 + 2 * qt, "SS", "Q", n, qt)
        put(own + 3, "VE", "Q", n)
        put(own + 4, "NW", "Q", n)
        put(own + (4 if n % KV else 5), "KT", n)
        for qt in range(TB):
            put(own + 5 + qt, "QT", n, qt)
        put(own + 6, "VS", n)
    return tasks


EVACUATED = ("CT", "XT", "KP", "VP", "QP", "KT", "QT")


def layer(nc, x, ctx_in, mask, W_DKV, b_DKV, W_UK, b_UK, W_UV, b_UV, W_DQ, b_DQ, W_UQ, b_UQ, W_QR, b_QR,
          W_KR, b_KR, Wq, bq, Wk, bk, Wv, bv, Wo, qn_w, kn_w, gate_wT, w13T, w2T, rope_cs, out):
    es = ExitStack()
    with es:
        def sb(name, shape, dt=F32, stack=es):
            return stack.enter_context(nc.sbuf_tensor(name, shape, dt))

        def sem(name):
            return es.enter_context(nc.semaphore(name))

        ps = [es.enter_context(nc.psum_tensor(f"bank{i}", [P, 512], F32)) for i in range(8)]

        xs = sb("xs", [P, NT, D])
        ident = sb("ident", [P, P])
        OFF_K, OFF_V, OFF_Q, W_COLS = 0, C * KV * HD, 2 * C * KV * HD, 2 * C * KV * HD + C * XH * HD
        Wkvq = [sb(f"Wkvq{i}", [P, W_COLS], F32R) for i in "hl"]
        bias_hl = sb("bias_hl", [98, 2, 512], F32R)
        ones2 = sb("ones2", [98, P], F32R)
        stats = sb("stats", [P, 2, 6])
        wqk = sb("wqk", [P, 1])
        mv = sb("mv", [P, NT, 2])
        ve = sb("ve", [P, 16])
        lnv = sb("lnv", [P, 16])
        r0 = sb("r0", [P, 16])
        nwt = sb("nwt", [P, 16])
        rln = sb("rln", [P, NT])

        upper = sb("upper", [P, P])
        onesf = sb("onesf", [P, P])
        zeros = sb("zeros", [P, D])
        iota_e = sb("iota_e", [P, EW])
        iota_t = sb("iota_t", [P, NT])
        iota_j = sb("iota_j", [P, 32])

        esA = ExitStack()
        es.enter_context(esA)
        w1 = sb("w1", [P, C, 192], F32, esA)
        w2kv = sb("w2kv", [DC, 2 * D], F32, esA)
        w2q = sb("w2q", [P, D + DC], F32, esA)
        b1 = sb("b1", [P, 192], F32, esA)
        b2 = sb("b2", [P, 832], F32, esA)
        cs = sb("cs", [P, TB, 2, 4], F32, esA)
        xn = sb("xn", [P, 2, D], F32, esA)
        xnT = sb("xnT", [P, 2, C, P], F32, esA)
        c1 = sb("c1", [P, 2, 128], F32, esA)
        rr = sb("rr", [P, 3, 2, DC], F32, esA)
        cT = sb("cT", [P, 2, P], F32, esA)
        cat = sb("cat", [P, 2, 2, NH, DQ], F32, esA)
        rp1 = sb("rp1", [P, 2 * NH, DR], F32, esA)
        rp2 = sb("rp2", [P, 2 * NH, DR], F32, esA)
        qks = sb("qks", [P, 2, 2, NH, HW], F32R, esA)
        wraw = sb("wraw", [P, 2, 512], F32, esA)
        braw = sb("braw", [6, 512], F32, esA)
        bsp = [sb(f"bsp{i}", [6, 512], F32R, esA) for i in "hl"]
        qkw = sb("qkw", [P, 2], F32, esA)
        qkT = sb("qkT", [P, 2, NP, B * T], F32R, esA)
        va = sb("va", [P, NT, NH, VW], F32, esA)
        oTs = sb("oTs", [P, 2, 2 * T], F32, esA)
        mneg = sb("mneg", [P, 2, TB, NH], F32, esA)
        msp = sb("msp", [P, TB, 2, 2, NP], F32R, esA)
        mT = sb("mT", [32, 2, T], F32R, esA)
        pTs = sb("pTs", [P, 3, 2, T], F32, esA)
        rsv = sb("rsv", [P, TB, NH], F32, esA)
        osa = sb("osa", [P, TB, NH, DH], F32, esA)
        esA.close()

        esD = ExitStack()
        es.enter_context(esD)
        WoS = [sb(f"Wo{i}", [P, XH, D], F32R, esD) for i in "hl"]
        wraw2 = sb("wraw2", [P, 2, 512], F32, esD)
        craw = sb("craw", [P, KT_, D], F32, esD)
        msk = sb("msk", [P, TB, SE], F32, esD)
        ctxT = [sb(f"ctxT{i}", [P, C, SE], F32R, esD) for i in "hl"]
        xnD = sb("xnD", [P, TB, D], F32, esD)
        xT = [sb(f"xT{i}", [P, C, T], F32R, esD) for i in "hl"]
        kraw = sb("kraw", [P, KT_, KV * HD], F32, esD)
        vraw = sb("vraw", [P, KT_, KV * HD], F32, esD)
        qraw = sb("qraw", [P, TB, GW], F32, esD)
        sq = sb("sq", [P, 2, 512], F32, esD)
        ssK = sb("ssK", [P, 16], F32, esD)
        ssQ = sb("ssQ", [P, 8], F32, esD)
        rK = sb("rK", [P, 16], F32, esD)
        rQ = sb("rQ", [P, 8], F32, esD)
        kT = [sb(f"kT{i}", [P, 2, SE], F32R, esD) for i in "hl"]
        vS = [sb(f"vS{i}", [P, 2, KT_, HD], F32R, esD) for i in "hl"]
        qT = [sb(f"qT{i}", [P, 2, TB, GW], F32R, esD) for i in "hl"]
        pb = sb("pb", [P, 3, SE], F32, esD)
        nmax = sb("nmax", [P, 3], F32, esD)
        psm = sb("psm", [P, 3], F32, esD)
        rinv = sb("rinv", [P, 3], F32, esD)
        pT = [sb(f"pT{i}", [P, 2, KT_, T], F32R, esD) for i in "hl"]
        oT = [sb(f"oT{i}", [P, T], F32R, esD) for i in "hl"]
        esD.close()

        esF = ExitStack()
        es.enter_context(esF)
        w13 = sb("w13", [P, NE + 1, C, 2 * INTER], F32, esF)
        w2s = sb("w2s", [IH, NE + 1, 2, D], F32, esF)
        gw = sb("gw", [P, C, EW], F32, esF)
        xn3 = sb("xn3", [P, NT, D], F32, esF)
        xn3T = sb("xn3T", [P, C, B * T], F32, esF)
        lg = sb("lg", [P, NT, EW], F32, esF)
        lge = sb("lge", [P, NT, EW], F32, esF)
        eq = sb("eq", [P, NT, EW], F32, esF)
        oh = [sb(f"onehot{i}", [P, NT, EW], F32, esF) for i in range(2)]
        chosen = sb("chosen", [P, NT, EW], F32, esF)
        top = [sb(f"top{i}", [P, NT], F32, esF) for i in range(2)]
        first_e = sb("first_e", [P, NT], F32, esF)
        cw = [sb(f"combine{i}", [P, NT], F32, esF) for i in range(2)]
        tot = sb("tot", [P, NT, EW], F32, esF)
        before = sb("before", [P, NT + 1, EW], F32, esF)
        more = sb("more", [P, EW, NT], F32, esF)
        ntile = sb("ntile", [P, EW], F32, esF)
        tend = sb("tend", [P, EW], F32, esF)
        pos = sb("pos", [P, NT, EW], F32, esF)
        slotf = sb("slotf", [P, 2, NT], F32, esF)
        sloti = sb("sloti", [P, 2, NT], mybir.dt.int32, esF)
        isof = sb("isof", [P, 32, EW], F32, esF)
        expf = sb("expf", [P, 32], F32, esF)
        packf = sb("packf", [P, 32 // XG], F32, esF)
        expi = sb("expi", [P, 32 // XG], mybir.dt.int32, esF)
        xg = sb("xg", [P, XG, D], F32, esF)
        xgT = sb("xgT", [P, 2, C, P], F32, esF)
        sg = sb("sg", [P, 2, INTER], F32, esF)
        hh = sb("hh", [P, 2, INTER], F32, esF)
        hT = sb("hT", [IH, 2, 2, P], F32, esF)
        ys = sb("ys", [P, 2, D], F32, esF)
        yg = [sb(f"yg{i}", [P, NT, D], F32, esF) for i in range(2)]
        esF.close()
        xg_dram = nc.dram_tensor("rows_by_slot", (NSLOT * P, D), F32, kind="Internal").ap()
        yg_dram = nc.dram_tensor("results_by_slot", (NSLOT * P, D), F32, kind="Internal").ap()

        ld_small, ld_down, ld_b, ld_mask, ld_ctx, st_out, mrow = [
            sem(n) for n in ("ld_small", "ld_down", "ld_b", "ld_mask", "ld_ctx", "st_out", "mrow_moved")]
        act_self, dve_self, pool_self = sem("act_self"), sem("dve_self"), sem("pool_self")
        consts = sem("consts_ready")
        w_read, w_split, b_split, qkw_read = sem("w_chunk_read"), sem("w_split"), sem("b_split"), sem("qkw_read")
        var_ready, r0_ready, rln_ready = sem("var_ready"), sem("r0_ready"), sem("rln_ready")
        xn_ready, xnT_ps, xnT_ready, c_ps, c_ready, cT_ps, cT_ready, kvq_ps, cat_ready = [
            sem(n) for n in ("xn_ready", "xnT_ps", "xnT_ready", "c_ps", "c_ready", "cT_ps", "cT_ready",
                             "kvq_ps", "cat_ready")]
        kvq_read = sem("kvq_read")
        hi_ready, lo_ready, qk_ps, qkA, qkD = [sem(n) for n in ("hi_ready", "lo_ready", "qk_ps", "qk_by_act", "qk_by_dve")]
        s1_ps, s1_max, m_hi, m_lo, mT_ps, mT_ready = [
            sem(n) for n in ("s1_ps", "s1_max", "m_hi", "m_lo", "mT_ps", "mT_ready")]
        sT_ps, pTs_ready, o_ps, oTs_ready, o_rows, x1_ready = [
            sem(n) for n in ("sT_ps", "pTs_ready", "o_ps", "oTs_ready", "o_rows", "x1_ready")]
        ld_x = [sem(f"ld_x{i}") for i in range(2)]
        m_ps, ctx_hi, ctx_lo, xT_hi, xT_lo = [sem(n) for n in ("m_ps", "ctx_hi", "ctx_lo", "xT_hi", "xT_lo")]
        bias_placed, wo_high, wo_split, w_high = [sem(n) for n in ("bias_placed", "wo_high", "wo_split", "w_high")]
        ld_w, ld_wo = [[sem(f"{n}{i}") for i in range(2)] for n in ("ld_w", "ld_wo")]
        xnD_ready, raw_ready, v_ready, sq_ready, ss_ready = [
            sem(n) for n in ("xnD_ready", "raw_ready", "v_ready", "sq_ready", "ss_ready")]
        rk_var, rk_r0, rk_ready, normed = [sem(n) for n in ("rk_var", "rk_r0", "rk_ready", "normed")]
        v_split, kT_hi, kT_lo, qT_hi, qT_lo = [sem(n) for n in ("v_split", "kT_hi", "kT_lo", "qT_hi", "qT_lo")]
        S_ps, S_masked, exp_done, rinv_ready, p_normed, pT_ps, pT_hi, pT_lo = [
            sem(n) for n in ("S_ps", "S_masked", "exp_done", "rinv_ready", "p_normed", "pT_ps", "pT_hi", "pT_lo")]
        pv_ps, o_hi, o_lo, wo_ps, x2_ready = [sem(n) for n in ("pv_ps", "o_hi", "o_lo", "wo_ps", "x2_ready")]

        ld_e, zeroed, zero_src = [sem(n) for n in ("ld_experts", "xg_zeroed", "zero_src")]
        ld_shared = sem("ld_shared")
        xn3_ready, x3_ps, x3_T, gate_ps, lgm_ready, lge_ready, chosen_ready, rank_ps, slots_ready, scattered = [
            sem(n) for n in ("xn3_ready", "x3_ps", "x3_T", "gate_ps", "lgm_ready", "lge_ready", "chosen_ready", "rank_ps",
                             "slots_ready", "scattered")]
        xg_ld = [sem(f"xg_ld{i}") for i in range(XG)]
        y_st = [sem(f"y_st{i}") for i in range(2)]
        gathered = [sem(f"gathered{t}") for t in range(NT)]
        xg_ps, xgT_ready, up_ps, sg_ready, hh_ready, h_ps, hT_ready, y_ps, y_read, done = [
            sem(n) for n in ("xg_ps", "xgT_ready", "up_ps", "sg_ready", "hh_ready", "h_ps", "hT_ready", "y_ps", "y_read",
                             "done")]

        x_dram = x.rearrange("b (j p) d -> p (b j) d", p=P)
        out_dram = out.rearrange("b (j p) d -> p (b j) d", p=P)

        chunks = []
        for c in range(C):
            rows = slice(c * P, (c + 1) * P)
            chunks.append((OFF_K + 512 * c, Wk[rows, :]))
            chunks.append((OFF_V + 512 * c, Wv[rows, :]))
            for g in range(KV):
                chunks.append((OFF_Q + XH * HD * c + GW * g, Wq[rows, g * GW:(g + 1) * GW]))
        wo_chunks = [Wo[i * 2 * P:(i + 1) * 2 * P, :].rearrange("(h p) n -> p h n", p=P) for i in range(XH // 2)]

        def stage_slots():
            return range(NT + 4)

        TURN_BANKS = (5, 6, 7, 2)
        M_LAG, P2_LAG, PV_LAG, TURN_LAG = 17, 21, 2, 3
        UNITS = B * NH
        side = {}
        tasks = xattn_tasks()
        FIRST, LAST = min(tasks), 8 * B * KV + 7
        for s in range(FIRST, LAST):
            for task in tasks.get(s, ()):
                if task[0] in EVACUATED:
                    side[task] = len(side)
        norm_unit = {}
        norm_chain = {}
        for s in range(FIRST, LAST):
            for task in tasks.get(s, ()):
                if task[0] in ("KP", "QP"):
                    norm_unit[(task[0][0], *task[1:])] = len(norm_unit)
                if task[0] == "VE":
                    norm_chain[task[1:]] = len(norm_chain)

        side_order = list(side)

        def released(task):
            kind, *a = task
            if kind in ("KP", "QP"):
                return raw_ready, norm_unit[(kind[0], *a)] + 1
            return {"CT": lambda b, c: (ctx_lo, C * b + c + 1), "XT": lambda b: (xT_lo, b + 1),
                    "VP": lambda b, kt: (v_ready, KT_ * b + kt + 1), "KT": lambda n: (kT_lo, n + 1),
                    "QT": lambda n, qt: (qT_lo, TB * n + qt + 1)}[kind](*a)

        def products_of(s):
            return [t for t in tasks.get(s - 1, ()) if t[0] in EVACUATED]

        def other_work(s):
            return [t for t in tasks.get(s, ()) if t[0] not in EVACUATED]

        def side_bank(task):
            return ps[6 + side[task] % 2]

        block = es.enter_context(nc.Block())

        @block.sync
        def _(sp):
            sp.dma_start(xs[:, 0:TB, :], x_dram[:, 0:TB, :]).then_inc(ld_x[0], 16)
            for off, w in ((0, W_DKV), (DC, W_DQ), (2 * DC, W_KR)):
                sp.dma_start(w1[:, :, off:off + DC], w.rearrange("(c p) n -> p c n", p=P)).then_inc(ld_down, 16)
            for off, v, n in ((0, b_DKV, DC), (DC, b_DQ, DC), (2 * DC, b_KR, DC)):
                sp.dma_start(b1[:, off:off + n], v.rearrange("(a n) -> a n", a=1).to_broadcast([P, n])).then_inc(ld_down, 16)
            sp.dma_start(xs[:, TB:NT, :], x_dram[:, TB:NT, :]).then_inc(ld_x[1], 16)
            for row, v in ((0, bq), (4, bk), (5, bv)):
                sp.dma_start(braw[row:row + v.shape[0] // 512, :], v.rearrange("(a n) -> a n", n=512)).then_inc(ld_b, 16)
            sp.dma_start(qkw[:, 0:1], qn_w.rearrange("(p a) -> p a", a=1)).then_inc(ld_b, 16)
            sp.dma_start(qkw[:, 1:2], kn_w.rearrange("(p a) -> p a", a=1)).then_inc(ld_b, 16)
            for i, (off, src) in enumerate(chunks):
                if i >= 2:
                    sp.wait_ge(w_split, i - 1)
                sp.dma_start(wraw[:, i % 2, :], src).then_inc(ld_w[i % 2], 16)
            sp.wait_ge(b_split, 3)
            for j in range(6):
                for part in range(2):
                    row = 32 * (j % 4) + part
                    sp.dma_start(bias_hl[row:row + 1, j // 4, :].bitcast(F32), bsp[part][j:j + 1, :].bitcast(F32)).then_inc(bias_placed, 16)
            sp.wait_ge(s1_ps, 1)
            sp.wait_ge(w_split, len(chunks))
            sp.wait_ge(bias_placed, 16 * 12)
            for i in range(2):
                sp.dma_start(wraw2[:, i, :].rearrange("p (h n) -> p h n", h=2), wo_chunks[i]).then_inc(ld_wo[i], 16)
            sp.dma_start(craw[:], ctx_in[0].rearrange("(k p) d -> p k d", p=P)).then_inc(ld_ctx, 16)
            sp.dma_start(msk[:], mask.rearrange("a (j p) e -> p (a j) e", p=P)).then_inc(ld_mask, 16)
            for b in range(B):
                if b:
                    sp.wait_ge(mrow, 64 * b)
                sp.wait_ge(mT_ready, b + 1)
                for jj in range(2):
                    for part in range(2):
                        row = jj * 16 + part * 8
                        to = 64 * jj + KS + part
                        sp.dma_start(qkT[to:to + 1, 0, :, b * T:(b + 1) * T].bitcast(F32), mT[row:row + 8, b % 2, :].bitcast(F32)).then_inc(mrow, 16)
            for b in range(1, B):
                sp.wait_ge(m_ps, side[("CT", b - 1, 1)] + 1)
                sp.dma_start(craw[:], ctx_in[b].rearrange("(k p) d -> p k d", p=P)).then_inc(ld_ctx, 16)
                if b == 1:
                    sp.wait_ge(zero_src, 1)
                    sp.dma_start(xg_dram.rearrange("(j p) d -> p j d", p=P),
                                 zeros[:].unsqueeze(1).to_broadcast([P, NSLOT, D])).then_inc(zeroed, 16)
            sp.wait_ge(x2_ready, B)
            sp.dma_start(gw[:, :, 0:NE], gate_wT.rearrange("(c p) e -> p c e", p=P)).then_inc(ld_shared, 16)
            sp.dma_start(w13[:, NE, :, :], w13T[NE].rearrange("(c p) n -> p c n", p=P)).then_inc(ld_shared, 16)
            sp.dma_start(w2s[:, NE, :, :], w2T[NE].rearrange("(c p) n -> p c n", p=IH)).then_inc(ld_shared, 16)
            for e in range(0, NE, 5):
                sp.dma_start(w13[:, e:e + 5].rearrange("p e c n -> p (e c) n"),
                             w13T[e:e + 5].rearrange("e (c p) n -> p (e c) n", p=P)).then_inc(ld_e, 16)
                sp.dma_start(w2s[:, e:e + 5].rearrange("p e c n -> p (e c) n"),
                             w2T[e:e + 5].rearrange("e (c p) n -> p (e c) n", p=IH)).then_inc(ld_e, 16)

            xg_rows = xg_dram.rearrange("(j p) d -> p j d", p=P)
            yg_rows = yg_dram.rearrange("(j p) d -> p j d", p=P)

            def load(j, buf):
                sp.dma_start(xg[:, buf:buf + 1, :], xg_rows[:, bass.ds(j, 1), :]).then_inc(xg_ld[buf], 16)

            def store(j, par):
                sp.wait_ge(y_read, j + NT + 1)
                sp.dma_start(yg_rows[:, bass.ds(j, 1), :], ys[:, par:par + 1, :]).then_inc(y_st[par], 16)

            sp.wait_ge(scattered, 16 * 2 * NT)
            for j in range(XG):
                load(j, j)
            with sp.Fori(0, NSLOT // XG - 1) as k:
                for i in range(XG):
                    sp.wait_ge(xg_ps, XG * k + i + 1)
                    load(XG * k + i + XG, i)
                    store(XG * k + i, i % 2)
            for j in range(XG * (NSLOT // XG - 1), NSLOT):
                if j + XG < NSLOT:
                    sp.wait_ge(xg_ps, j + 1)
                    load(j + XG, j % XG)
                store(j, j % 2)
            for t in range(NT):
                sp.wait_ge(done, t + 1)
                sp.dma_start(out_dram[:, t, :], xs[:, t, :]).then_inc(st_out, 16)
            sp.wait_ge(st_out, 16 * NT)

        @block.gpsimd
        def _(pool):
            n_self = 0

            def link(ins):
                nonlocal n_self
                n_self += 1
                ins.then_inc(pool_self, 1)
                pool.wait_ge(pool_self, n_self)

            link(pool.memset(ident[:], 0.0))
            pool.affine_select(out=ident[:], in_=ident[:], compare_op=ALU.not_equal, fill=1.0, base=0,
                               pattern=[[-1, P]], channel_multiplier=1).then_inc(consts, 1)
            link(pool.memset(qks[:].bitcast(F32), 0.0))
            pool.memset(qks[:, :, 1, :, KS:KM].bitcast(F32), 1.0).then_inc(consts, 1)
            link(pool.memset(va[:], 0.0))
            pool.memset(va[:, :, :, DH:DH + 1], 1.0).then_inc(consts, 1)
            pool.memset(ones2[:].bitcast(F32), 1.0).then_inc(consts, 1)
            pool.memset(zeros[:], 0.0).then_inc(zero_src, 1)
            pool.memset(onesf[:], 1.0).then_inc(pool_self, 1)
            link(pool.memset(upper[:], 1.0))
            n_self += 1
            pool.wait_ge(pool_self, n_self)
            pool.affine_select(out=upper[:], in_=upper[:], compare_op=ALU.is_gt, fill=0.0, base=0, pattern=[[1, P]],
                               channel_multiplier=-1).then_inc(consts, 1)
            pool.iota(iota_e[:], pattern=[[1, EW]], base=0, channel_multiplier=0,
                      allow_small_or_imprecise_dtypes=True).then_inc(consts, 1)
            pool.iota(iota_t[:], pattern=[[P, NT]], base=0, channel_multiplier=0,
                      allow_small_or_imprecise_dtypes=True).then_inc(consts, 1)
            pool.iota(iota_j[:], pattern=[[1, 32]], base=0, channel_multiplier=0,
                      allow_small_or_imprecise_dtypes=True).then_inc(consts, 1)
            pool.wait_ge(ld_b, 16 * 5)
            link(pool.tensor_tensor(wqk[:], qkw[:, 0:1], qkw[:, 1:2], ALU.mult))
            pool.tensor_scalar(wqk[:], wqk[:], XSCALE, None, ALU.mult).then_inc(b_split, 1)
            pool.tensor_copy(bsp[0][:], braw[:]).then_inc(b_split, 1)
            pool.wait_ge(b_split, 2)
            pool.tensor_tensor(bsp[1][:], braw[:], bsp[0][:].bitcast(F32), ALU.subtract).then_inc(b_split, 1)

            def split_weights(i):
                off, _ = chunks[i]
                pool.wait_ge(w_high, i + 1)
                pool.tensor_tensor(Wkvq[1][:, off:off + 512], wraw[:, i % 2, :], Wkvq[0][:, off:off + 512].bitcast(F32),
                                   ALU.subtract).then_inc(w_split, 1)

            for k in stage_slots():
                t = k - 3
                if 0 <= t < NT:
                    pool.wait_ge(hi_ready, t + 1)
                    pool.tensor_tensor(qks[:, t % 2, 0, :, 2 * DQ:KS], cat[:, t % 2, 0], qks[:, t % 2, 0, :, 0:DQ].bitcast(F32),
                                       ALU.subtract).then_inc(lo_ready, 1)
                    pool.tensor_tensor(qks[:, t % 2, 1, :, DQ:2 * DQ], cat[:, t % 2, 1], qks[:, t % 2, 1, :, 0:DQ].bitcast(F32),
                                       ALU.subtract).then_inc(lo_ready, 1)
                split_weights(k)

            def square(u, raw):
                pool.wait_ge(raw_ready, u + 1)
                if u >= 2:
                    pool.wait_ge(ss_ready, u - 1)
                pool.tensor_tensor(sq[:, u % 2, :], raw, raw, ALU.mult).then_inc(sq_ready, 1)

            for i in range(len(wo_chunks)):
                pool.wait_ge(wo_high, i + 1)
                high, low = [w[:, 2 * i:2 * i + 2, :].rearrange("p h n -> p (h n)") for w in WoS]
                pool.tensor_tensor(low, wraw2[:, i % 2, :], high.bitcast(F32), ALU.subtract).then_inc(wo_split, 1)

            for s in range(FIRST, LAST):
                for kind, *a in products_of(s) + other_work(s):
                    if kind == "KP":
                        square(norm_unit[("K", *a)], kraw[:, a[1], :])
                    if kind == "QP":
                        square(norm_unit[("Q", *a)], qraw[:, a[1], :])
                    if kind == "NW":
                        n = norm_chain[tuple(a)]
                        pool.wait_ge(rk_ready, n + 1)
                        raw, r, tiles = (kraw, rK, KT_) if a[0] == "K" else (qraw, rQ, TB)
                        v = raw[:].rearrange("p k (g d) -> p (k g) d", d=HD)
                        pool.tensor_tensor(v, v, r[:].unsqueeze(2).to_broadcast([P, 4 * tiles, HD]), ALU.mult).then_inc(normed, 1)
                    if kind == "VS":
                        n, = a
                        pool.wait_ge(v_ready, 4 * (n // 4 + 1))
                        if n >= 2:
                            pool.wait_ge(pv_ps, 4 * (n - 1))
                        src = vraw[:, :, (n % 4) * HD:(n % 4 + 1) * HD]
                        link(pool.tensor_copy(vS[0][:, n % 2], src))
                        pool.tensor_tensor(vS[1][:, n % 2], src, vS[0][:, n % 2].bitcast(F32), ALU.subtract).then_inc(v_split, 1)

            pool.wait_ge(zeroed, 16)
            pool.wait_ge(xn3_ready, NT)
            pool.wait_ge(slots_ready, 1)
            for t in range(NT):
                for k in range(2):
                    pool.indirect_dma_start(out=xg_dram, out_offset=bass.IndirectOffsetOnAxis(sloti[:, k, t:t + 1], axis=0),
                                            in_=xn3[:, t, :], in_offset=None).then_inc(scattered, 16)
            for par in range(2):
                pool.wait_ge(y_st[par], 16 * (NSLOT // 2))
            for t in range(NT):
                for k in range(2):
                    pool.indirect_dma_start(out=yg[k][:, t, :], out_offset=None, in_=yg_dram,
                                            in_offset=bass.IndirectOffsetOnAxis(sloti[:, k, t:t + 1], axis=0)
                                            ).then_inc(gathered[t], 16)

        @block.scalar
        def _(act):
            n_self = 0

            def link(ins):
                nonlocal n_self
                n_self += 1
                ins.then_inc(act_self, 1)
                act.wait_ge(act_self, n_self)

            def rsqrt_guess(n, ready, at, done):
                act.wait_ge(ready, at)
                link(nc.scalar.activation(lnv[:, 0:n], ve[:, 0:n], ACT.Ln))
                nc.scalar.activation(r0[:, 0:n], lnv[:, 0:n], ACT.Exp, scale=-0.5).then_inc(done, 1)

            act.preload_act_table_set("natural_log_exp_and_others")
            rsqrt_guess(TB, var_ready, 1, r0_ready)
            act.dma_start(w2kv[:, 0:D], W_UK).then_inc(ld_small, 16)
            act.dma_start(w2kv[:, D:2 * D], W_UV).then_inc(ld_small, 16)
            act.dma_start(w2q[DC:P, 0:D], W_UQ).then_inc(ld_small, 16)
            act.dma_start(w2q[DC:P, D:D + DC], W_QR).then_inc(ld_small, 16)
            for off, v, n in ((0, b_UK, D), (D, b_UV, D), (2 * D, b_UQ, D), (3 * D, b_QR, DC)):
                act.dma_start(b2[:, off:off + n], v.rearrange("(a n) -> a n", a=1).to_broadcast([P, n])).then_inc(ld_small, 16)
            act.dma_start(cs[:], rope_cs).then_inc(ld_small, 16)
            for k in stage_slots():
                t = k - 2
                if 0 <= t < NT:
                    act.wait_ge(cT_ps, t + 1)
                    if t >= 2:
                        act.wait_ge(kvq_ps, t - 1)
                    act.copy(cT[:, t % 2, :], ps[0][:, D:D + P]).then_inc(cT_ready, 1)
                t = k
                if 0 <= t < NT:
                    act.wait_ge(xnT_ps, t + 1)
                    if t >= 2:
                        act.wait_ge(c_ps, t - 1)
                    act.copy(xnT[:, t % 2].rearrange("p c n -> p (c n)"), ps[0][:, 0:D]).then_inc(xnT_ready, 1)
                t = k - 3
                if 0 <= t < NT:
                    act.wait_ge(cat_ready, t + 1)
                    if t >= 2:
                        act.wait_ge(qk_ps, 4 * (t - 1))
                    src = cat[:, t % 2].rearrange("p a h d -> p (a h) d")
                    dst = qks[:, t % 2].rearrange("p a h d -> p (a h) d")
                    act.copy(dst[:, :, 0:DQ], src)
                    act.copy(dst[:, 0:NH, DQ:2 * DQ], src[:, 0:NH, :])
                    act.copy(dst[:, NH:2 * NH, 2 * DQ:KS], src[:, NH:2 * NH, :]).then_inc(hi_ready, 1)
                t = k - 4
                if 0 <= t < NT:
                    for g in range(2):
                        act.wait_ge(qk_ps, 4 * t + g + 1)
                        act.copy(qkT[:, 0, 4 * g:4 * g + 4, t * P:(t + 1) * P],
                                 ps[TURN_BANKS[g]][:].rearrange("p (a n) -> p a n", a=4)).then_inc(qkA, 1)
                off, _ = chunks[k]
                act.wait_ge(ld_w[k % 2], 16 * (k // 2 + 1))
                act.copy(Wkvq[0][:, off:off + 512], wraw[:, k % 2, :]).then_inc(w_high, 1)

                if k % TB == 0 and k // TB + 1 < LN1_SETS:
                    rsqrt_guess(TB, var_ready, k // TB + 2, r0_ready)

            for u in range(UNITS + P2_LAG + PV_LAG + 2):
                i = (u - P2_LAG) // 4
                if u % 4 == 0 and 0 <= i < len(wo_chunks):
                    if 1 <= i < len(wo_chunks) - 1:
                        act.wait_ge(wo_split, i)
                        act.dma_start(wraw2[:, (i + 1) % 2, :].rearrange("p (h n) -> p h n", h=2),
                                      wo_chunks[i + 1]).then_inc(ld_wo[(i + 1) % 2], 16)
                    act.wait_ge(ld_wo[i % 2], 16 * (i // 2 + 1))
                    act.copy(WoS[0][:, 2 * i:2 * i + 2, :].rearrange("p h n -> p (h n)"),
                             wraw2[:, i % 2, :]).then_inc(wo_high, 1)
                b = (u - M_LAG + 1) // NH
                if u >= M_LAG - 1 and (u - M_LAG + 1) % NH == 0 and b < B:
                    act.wait_ge(s1_max, NH * (b + 1))
                    if b:
                        act.wait_ge(mT_ps, b)
                    act.copy(msp[:, :, :, 0, :], mneg[:, b % 2].rearrange("p q (a j) -> p q j a", j=2)).then_inc(m_hi, 1)
                    act.wait_ge(mT_ps, b + 1)
                    if b >= 2:
                        act.wait_ge(mrow, 64 * (b - 1))
                    act.copy(mT[:, b % 2, :], ps[(17 * b + 16) % 2][0:32, 0:T]).then_inc(mT_ready, 1)
                v = u - P2_LAG
                if 0 <= v < UNITS:
                    act.wait_ge(sT_ps, v + 1)
                    if v >= 3:
                        act.wait_ge(o_ps, v - 2)
                    nc.scalar.activation(pTs[:, v % 3].rearrange("p k t -> p (k t)"), ps[2 + v % 2][:], ACT.Exp,
                                         scale=SA_SCALE).then_inc(pTs_ready, 1)
                v = u - P2_LAG - PV_LAG - 1
                if v >= 0 and v % 8 == 7:
                    g = v // 8
                    act.wait_ge(o_ps, v + 1)
                    if g >= 2:
                        act.wait_ge(o_rows, g - 1)
                    act.copy(oTs[:, g % 2, :], ps[4 + g % 2][:]).then_inc(oTs_ready, 1)

            for s in range(FIRST, LAST):
                if s >= 5 and s % 2 == 1 and (s - 5) // 2 < B * XH:
                    h = (s - 5) // 2
                    act.wait_ge(pv_ps, h + 1)
                    if h >= 1:
                        act.wait_ge(wo_ps, h)
                    act.copy(oT[0][:], ps[4][:, 0:T]).then_inc(o_hi, 1)
                for task in products_of(s):
                    kind, *a = task
                    if kind in EVACUATED:
                        act.wait_ge(m_ps, side[task] + 1)
                        bank = side_bank(task)
                    if kind == "CT":
                        b, c = a
                        if b:
                            act.wait_ge(m_ps, side[("VP", b - 1, KT_ - 1)] + 1)
                        act.copy(ctxT[0][:, c, :], bank[:]).then_inc(ctx_hi, 1)
                    if kind == "XT":
                        b, = a
                        if b:
                            act.wait_ge(m_ps, side[("QP", 4 * b - 1, 1)] + 1)
                        act.copy(xT[0][:].rearrange("p c n -> p (c n)"), bank[:]).then_inc(xT_hi, 1)
                    if kind == "KP":
                        b, kt = a
                        if b:
                            act.wait_ge(m_ps, side[("KT", 4 * b - 1)] + 1)
                        act.copy(kraw[:, kt, :], bank[:]).then_inc(raw_ready, 1)
                    if kind == "QP":
                        n, qt = a
                        if n:
                            act.wait_ge(m_ps, side[("QT", n - 1, qt)] + 1)
                        act.copy(qraw[:, qt, :], bank[:]).then_inc(raw_ready, 1)
                    if kind == "VP":
                        b, kt = a
                        if b:
                            act.wait_ge(v_split, 4 * b)
                        act.copy(vraw[:, kt, :], bank[:]).then_inc(v_ready, 1)
                    if kind == "KT":
                        n, = a
                        if n >= 2:
                            act.wait_ge(S_ps, 8 * (n - 1))
                        nc.scalar.activation(kT[0][:, n % 2, :], bank[:], ACT.Copy, scale=wqk[:, 0:1]).then_inc(kT_hi, 1)
                    if kind == "QT":
                        n, qt = a
                        if n >= 2:
                            act.wait_ge(S_ps, 8 * (n - 1))
                        act.copy(qT[0][:, n % 2, qt, :], bank[:]).then_inc(qT_hi, 1)
                if 0 <= s - 2 < 8 * B * KV:
                    i = s - 2
                    act.wait_ge(pT_ps, i + 1)
                    if i // 2 >= 2:
                        act.wait_ge(pv_ps, i // 2 - 1)
                    act.copy(pT[0][:, (i // 2) % 2, :, (i % 2) * P:(i % 2 + 1) * P],
                             ps[2 + i % 2][:].rearrange("p (k n) -> p k n", k=KT_)).then_inc(pT_hi, 1)
                if 0 <= s < 8 * B * KV:
                    act.wait_ge(S_masked, s + 1)
                    nc.scalar.activation(pb[:, s % 3, :], pb[:, s % 3, :], ACT.Exp, bias=nmax[:, s % 3:s % 3 + 1], scale=-1.0,
                                         accum_out=psm[:, s % 3:s % 3 + 1]).then_inc(exp_done, 1)
                for kind, *a in other_work(s):
                    if kind == "LNV":
                        rsqrt_guess(TB, var_ready, LN1_SETS + 1 + a[0], r0_ready)
                    if kind == "VE":
                        n = norm_chain[tuple(a)]
                        rsqrt_guess(16 if a[0] == "K" else 8, rk_var, n + 1, rk_r0)

            rsqrt_guess(NT, var_ready, LN1_SETS + 1 + B, r0_ready)
            for u in range(4):
                act.wait_ge(x3_ps, u + 1)
                act.copy(xn3T[:, u // 2, (u % 2) * 512:(u % 2 + 1) * 512], ps[u][:]).then_inc(x3_T, 1)
            act.wait_ge(lgm_ready, 1)
            nc.scalar.activation(lge[:], lg[:], ACT.Exp).then_inc(lge_ready, 1)

            def silu(i, par):
                act.wait_ge(up_ps, i + 1)
                nc.scalar.activation(sg[:, par, :], ps[2 + par][:, 0:INTER], ACT.Silu).then_inc(sg_ready, 1)

            def turn_rows(j, par):
                act.wait_ge(xg_ps, j + 1)
                act.copy(xgT[:, par].rearrange("p c n -> p (c n)"), ps[par][:, 0:D]).then_inc(xgT_ready, 1)

            for i in range(NT):
                if i >= 2:
                    act.wait_ge(hh_ready, i - 1)
                silu(i, i % 2)
            turn_rows(0, 0)
            act.wait_ge(hh_ready, NT - 1)
            silu(NT, 0)
            turn_rows(1, 1)
            with act.Fori(0, NSLOT // 2 - 1) as k:
                for par in range(2):
                    j = 2 * k + par + 1
                    act.wait_ge(hh_ready, j + (NT - 1))
                    silu(j + NT, 1 - par)
                    turn_rows(j + 1, par)
            act.wait_ge(hh_ready, NT + NSLOT - 2)
            silu(NT + NSLOT - 1, 1)

        @block.vector
        def _(dve):
            n_self = 0

            def link(ins):
                nonlocal n_self
                n_self += 1
                ins.then_inc(dve_self, 1)
                dve.wait_ge(dve_self, n_self)

            def polish(n, ready, at, r, done):
                dve.wait_ge(ready, at)
                link(dve.tensor_tensor(nwt[:, 0:n], r0[:, 0:n], r0[:, 0:n], ALU.mult))
                link(dve.tensor_tensor(nwt[:, 0:n], nwt[:, 0:n], ve[:, 0:n], ALU.mult))
                link(dve.tensor_scalar(nwt[:, 0:n], nwt[:, 0:n], -0.5, 1.5, ALU.mult, ALU.add))
                dve.tensor_tensor(r, r0[:, 0:n], nwt[:, 0:n], ALU.mult).then_inc(done, 1)

            def row_stats(tiles):
                for i, t in enumerate(tiles):
                    link(dve.bn_stats(stats[:, t % 2, :], xs[:, t, :]))
                    link(dve.bn_aggr(mv[:, t, :], stats[:, t % 2, :]))
                dve.tensor_scalar(ve[:, 0:len(tiles)], mv[:, tiles[0]:tiles[-1] + 1, 1], LN_EPS, None, ALU.add).then_inc(var_ready, 1)

            dve.wait_ge(ld_x[0], 16)
            row_stats(range(TB))
            polish(TB, r0_ready, 1, rln[:, 0:TB], rln_ready)
            for k in stage_slots():
                t = k
                if 0 <= t < NT:
                    dve.wait_ge(rln_ready, t // TB + 1)
                    if t >= 2:
                        dve.wait_ge(xnT_ps, t - 1)
                    dve.tensor_scalar(xn[:, t % 2, :], xs[:, t, :], mv[:, t, 0:1], rln[:, t:t + 1], ALU.subtract,
                                      ALU.mult).then_inc(xn_ready, 1)
                t = k - 3
                if 0 <= t < NT:
                    dve.wait_ge(kvq_ps, t + 1)
                    if t >= 2:
                        dve.wait_ge(lo_ready, 2 * (t - 1))
                        dve.wait_ge(hi_ready, t - 1)

                    def heads(a):
                        return a.rearrange("p (h d) -> p h d", h=NH)
                    dve.tensor_tensor(cat[:, t % 2, 1, :, 0:DH], heads(ps[3][:, 0:D]), heads(b2[:, 0:D]), ALU.add)
                    if t == 0:
                        dve.wait_ge(consts, 4)
                        dve.wait_ge(ld_small, 16 * 9)
                    dve.tensor_tensor(va[:, t, :, 0:DH], heads(ps[3][:, D:2 * D]), heads(b2[:, D:2 * D]), ALU.add)
                    dve.tensor_tensor(cat[:, t % 2, 0, :, 0:DH], heads(ps[4][:, 0:D]), heads(b2[:, 2 * D:3 * D]), ALU.add)
                    dve.tensor_tensor(rr[:, t % 3, 0, :], ps[4][:, D:D + DC], b2[:, 3 * D:3 * D + DC],
                                      ALU.add).then_inc(kvq_read, 1)
                    dve.wait_ge(kvq_read, t + 1)
                    dve.wait_ge(c_ready, t + 1)
                    rin = rr[:, t % 3].rearrange("p a (h d) -> p (a h) d", d=DR)
                    cos4 = cs[:, t % TB, 0:1, :].to_broadcast([P, 2 * NH, DR])
                    sin4 = cs[:, t % TB, 1:2, :].to_broadcast([P, 2 * NH, DR])
                    dve.tensor_tensor(rp1[:], rin, cos4, ALU.mult)
                    link(dve.tensor_tensor(rp2[:], rin, sin4, ALU.mult))
                    co = cat[:, t % 2].rearrange("p a h d -> p (a h) d")
                    dve.tensor_tensor(co[:, :, DH:DH + 2], rp1[:, :, 0:DR:2], rp1[:, :, 1:DR:2], ALU.subtract)
                    dve.tensor_tensor(co[:, :, DH + 2:DQ], rp2[:, :, 0:DR:2], rp2[:, :, 1:DR:2], ALU.add).then_inc(cat_ready, 1)
                t = k - 1
                if 0 <= t < NT:
                    if t == 0:
                        dve.wait_ge(ld_down, 16 * 6)
                    dve.wait_ge(c_ps, t + 1)
                    if t >= 2:
                        dve.wait_ge(cT_ps, t - 1)
                    dve.tensor_tensor(rr[:, t % 3, 1, :], ps[1][:, 128:192], b1[:, 128:192], ALU.add)
                    dve.tensor_tensor(c1[:, t % 2, :], ps[1][:, 0:128], b1[:, 0:128], ALU.add).then_inc(c_ready, 1)
                t = k - 4
                if 0 <= t < NT:
                    for g in range(2, 4):
                        dve.wait_ge(qk_ps, 4 * t + g + 1)
                        dve.tensor_copy(qkT[:, 1, 4 * (g - 2):4 * (g - 2) + 4, t * P:(t + 1) * P],
                                        ps[TURN_BANKS[g]][:].rearrange("p (a n) -> p a n", a=4)).then_inc(qkD, 1)

                if k % TB == 0 and k // TB + 1 < LN1_SETS:
                    if k == 0:
                        dve.wait_ge(ld_x[1], 16)
                    first = k + TB
                    row_stats(range(first, first + TB))
                    polish(TB, r0_ready, k // TB + 2, rln[:, first:first + TB], rln_ready)

            for u in range(UNITS + P2_LAG + PV_LAG + TURN_LAG + 1):
                if u < UNITS:
                    b, h = u // NH, u % NH
                    dve.wait_ge(s1_ps, u + 1)
                    if h == 0 and b >= 2:
                        dve.wait_ge(m_lo, b - 1)
                    dve.tensor_reduce(mneg[:, b % 2, :, h:h + 1], ps[(17 * b + h) % 2][:].rearrange("p (q k) -> p q k", q=TB),
                                      X, ALU.max, negate=True).then_inc(s1_max, 1)
                b = (u - M_LAG + 1) // NH
                if u >= M_LAG - 1 and (u - M_LAG + 1) % NH == 0 and b < B:
                    dve.wait_ge(m_hi, b + 1)
                    dve.tensor_tensor(msp[:, :, :, 1, :], mneg[:, b % 2].rearrange("p q (a j) -> p q j a", j=2),
                                      msp[:, :, :, 0, :].bitcast(F32), ALU.subtract).then_inc(m_lo, 1)
                v = u - P2_LAG - PV_LAG - TURN_LAG - 1
                if v >= 0 and v % NH == NH - 1:
                    b = v // NH
                    dve.wait_ge(o_rows, 2 * (b + 1))
                    for q in range(TB):
                        o = ps[6 + q][:].rearrange("p (h d) -> p h d", h=NH)
                        link(dve.reciprocal(rsv[:, q, :].unsqueeze(2), o[:, :, DH:DH + 1]))
                        link(dve.tensor_tensor(osa[:, q], o[:, :, 0:DH], rsv[:, q, :].unsqueeze(2).to_broadcast([P, NH, DH]), ALU.mult))
                    dve.tensor_tensor(xs[:, TB * b:TB * b + TB, :], xs[:, TB * b:TB * b + TB, :],
                                      osa[:].rearrange("p q h d -> p q (h d)"), ALU.add).then_inc(x1_ready, 1)

            dve.wait_ge(x1_ready, B)
            dve.wait_ge(w_split, len(chunks))
            dve.wait_ge(bias_placed, 16 * 12)
            for s in range(FIRST, LAST):
                if s >= 5 and s % 2 == 1 and (s - 5) // 2 < B * XH:
                    h = (s - 5) // 2
                    dve.wait_ge(o_hi, h + 1)
                    dve.tensor_tensor(oT[1][:], ps[4][:, 0:T], oT[0][:].bitcast(F32), ALU.subtract).then_inc(o_lo, 1)
                if 0 <= s < 8 * B * KV:
                    dve.wait_ge(S_ps, s + 1)
                    if s == 0:
                        dve.wait_ge(ld_mask, 16)
                    if s >= 3:
                        dve.wait_ge(pT_ps, s - 2)
                    dve.tensor_tensor_reduce(pb[:, s % 3, :], ps[s % 2][:], msk[:, s % 2, :], -1.0, 3.0e38, ALU.add, ALU.min,
                                             nmax[:, s % 3:s % 3 + 1]).then_inc(S_masked, 1)
                for task in products_of(s):
                    kind, *a = task
                    if task in side:
                        bank = side_bank(task)
                    if kind == "CT":
                        b, c = a
                        dve.wait_ge(ctx_hi, 2 * b + c + 1)
                        dve.tensor_tensor(ctxT[1][:, c, :], bank[:], ctxT[0][:, c, :].bitcast(F32), ALU.subtract).then_inc(ctx_lo, 1)
                    if kind == "XT":
                        b, = a
                        dve.wait_ge(xT_hi, b + 1)
                        dve.tensor_tensor(xT[1][:].rearrange("p c n -> p (c n)"), bank[:],
                                          xT[0][:].rearrange("p c n -> p (c n)").bitcast(F32), ALU.subtract).then_inc(xT_lo, 1)
                    if kind == "KT":
                        n, = a
                        dve.wait_ge(kT_hi, n + 1)
                        dve.scalar_tensor_tensor(kT[1][:, n % 2, :], bank[:], wqk[:, 0:1], kT[0][:, n % 2, :].bitcast(F32),
                                                 ALU.mult, ALU.subtract).then_inc(kT_lo, 1)
                    if kind == "QT":
                        n, qt = a
                        dve.wait_ge(qT_hi, 2 * n + qt + 1)
                        dve.tensor_tensor(qT[1][:, n % 2, qt, :], bank[:], qT[0][:, n % 2, qt, :].bitcast(F32),
                                          ALU.subtract).then_inc(qT_lo, 1)
                if 0 <= s - 1 < 8 * B * KV:
                    i = s - 1
                    dve.wait_ge(exp_done, i + 1)
                    dve.reciprocal(rinv[:, i % 3:i % 3 + 1], psm[:, i % 3:i % 3 + 1]).then_inc(rinv_ready, 1)
                    dve.wait_ge(rinv_ready, i + 1)
                    dve.tensor_scalar(pb[:, i % 3, :], pb[:, i % 3, :], rinv[:, i % 3:i % 3 + 1], None,
                                      ALU.mult).then_inc(p_normed, 1)
                if 0 <= s - 2 < 8 * B * KV:
                    i = s - 2
                    dve.wait_ge(pT_hi, i + 1)
                    cols = slice((i % 2) * P, (i % 2 + 1) * P)
                    dve.tensor_tensor(pT[1][:, (i // 2) % 2, :, cols], ps[2 + i % 2][:].rearrange("p (k n) -> p k n", k=KT_),
                                      pT[0][:, (i // 2) % 2, :, cols].bitcast(F32), ALU.subtract).then_inc(pT_lo, 1)
                if s >= 6 and s % 2 == 0 and (s - 6) // 2 < B * XH and ((s - 6) // 2) % XH == XH - 1:
                    h = (s - 6) // 2
                    b = h // XH
                    dve.wait_ge(wo_ps, h + 1)
                    dve.tensor_tensor(xs[:, TB * b:TB * b + TB, :], ps[5][:].rearrange("p (q d) -> p q d", q=TB),
                                      xs[:, TB * b:TB * b + TB, :], ALU.add).then_inc(x2_ready, 1)
                for kind, *a in other_work(s):
                    if kind == "LNV":
                        row_stats(range(TB * a[0], TB * a[0] + TB))
                    if kind == "LNW":
                        b, = a
                        polish(TB, r0_ready, LN1_SETS + 1 + b, rln[:, TB * b:TB * b + TB], rln_ready)
                        dve.wait_ge(rln_ready, LN1_SETS + 1 + b)
                        if b:
                            dve.wait_ge(m_ps, side[("XT", b - 1)] + 1)
                        for q in range(TB):
                            t = TB * b + q
                            dve.tensor_scalar(xnD[:, q, :], xs[:, t, :], mv[:, t, 0:1], rln[:, t:t + 1], ALU.subtract,
                                              ALU.mult).then_inc(xnD_ready, 1)
                    if kind == "SS":
                        which, i, t = a
                        u = norm_unit[(which, i, t)]
                        dve.wait_ge(sq_ready, u + 1)
                        to = (ssK if which == "K" else ssQ)[:, 4 * t:4 * t + 4]
                        dve.tensor_reduce(to, sq[:, u % 2, :].rearrange("p (g d) -> p g d", g=4), X, ALU.add).then_inc(ss_ready, 1)
                    if kind == "VE":
                        which, i = a
                        ss, n = (ssK, 16) if which == "K" else (ssQ, 8)
                        u = norm_unit[(which, i, n // 4 - 1)]
                        dve.wait_ge(ss_ready, u + 1)
                        dve.tensor_scalar(ve[:, 0:n], ss[:], 1.0 / HD, RMS_EPS, ALU.mult, ALU.add).then_inc(rk_var, 1)
                    if kind == "NW":
                        n = norm_chain[tuple(a)]
                        r = rK if a[0] == "K" else rQ
                        polish(16 if a[0] == "K" else 8, rk_r0, n + 1, r[:], rk_ready)

            dve.wait_ge(x2_ready, B)
            row_stats(range(NT))
            polish(NT, r0_ready, LN1_SETS + 1 + B, rln[:], rln_ready)
            dve.wait_ge(rln_ready, LN1_SETS + 1 + B)
            for t in range(NT):
                dve.tensor_scalar(xn3[:, t, :], xs[:, t, :], mv[:, t, 0:1], rln[:, t:t + 1], ALU.subtract,
                                  ALU.mult).then_inc(xn3_ready, 1)

            def by_row(a):
                return a.unsqueeze(2).to_broadcast([P, NT, EW])
            experts = iota_e[:].unsqueeze(1).to_broadcast([P, NT, EW])

            def pick(k):
                link(dve.tensor_reduce(top[k][:], lg[:], X, ALU.max))
                link(dve.tensor_tensor(eq[:], lg[:], by_row(top[k][:]), ALU.is_equal))
                link(dve.scalar_tensor_tensor(eq[:], eq[:], -float(EW), experts, ALU.mult, ALU.add))
                link(dve.tensor_reduce(first_e[:], eq[:], X, ALU.min))
                link(dve.tensor_tensor(oh[k][:], eq[:], by_row(first_e[:]), ALU.is_equal))

            dve.wait_ge(consts, 8)
            link(dve.memset(lg[:, :, NE:EW], FINITE_LOW))
            dve.wait_ge(gate_ps, 1)
            link(dve.tensor_copy(lg[:, :, 0:NE], ps[4][:, 0:NT * EW].rearrange("p (t e) -> p t e", t=NT)[:, :, 0:NE]))
            pick(0)
            dve.tensor_tensor(lg[:], lg[:], by_row(top[0][:]), ALU.subtract).then_inc(lgm_ready, 1)
            dve.wait_ge(lge_ready, 1)
            link(dve.scalar_tensor_tensor(lg[:], oh[0][:], FINITE_LOW, lg[:], ALU.mult, ALU.add))
            pick(1)
            dve.tensor_tensor(chosen[:], oh[0][:], oh[1][:], ALU.add).then_inc(chosen_ready, 1)
            link(dve.tensor_reduce(top[0][:], lge[:], X, ALU.add))
            link(dve.reciprocal(cw[0][:], top[0][:]))
            link(dve.tensor_tensor(lge[:], lge[:], oh[1][:], ALU.mult))
            link(dve.tensor_reduce(top[1][:], lge[:], X, ALU.add))
            link(dve.tensor_tensor(cw[1][:], top[1][:], cw[0][:], ALU.mult))

            dve.wait_ge(rank_ps, 1)
            per_tile = ps[0][:, P:2 * P].rearrange("p (t e) -> p t e", t=NT)
            link(dve.tensor_copy(tot[:], per_tile))
            link(dve.memset(before[:, 0, :], 0.0))
            for t in range(NT):
                link(dve.tensor_tensor(before[:, t + 1, :], before[:, t, :], tot[:, t, :], ALU.add))
            count = before[:, NT, :].unsqueeze(2).to_broadcast([P, EW, NT])
            link(dve.tensor_tensor(more[:], count, iota_t[:].unsqueeze(1).to_broadcast([P, EW, NT]), ALU.is_gt))
            link(dve.tensor_reduce(ntile[:], more[:], X, ALU.add))
            link(dve.tensor_tensor_scan(tend[:], onesf[:, 0:EW], ntile[:], 0.0, ALU.mult, ALU.add))
            link(dve.tensor_tensor(ntile[:], tend[:], ntile[:], ALU.subtract))
            rank = ps[0][:, 0:P].rearrange("p (t e) -> p t e", t=NT)
            link(dve.tensor_tensor(pos[:], rank, before[:, 0:NT, :], ALU.add))
            link(dve.scalar_tensor_tensor(pos[:], ntile[:].unsqueeze(1).to_broadcast([P, NT, EW]), float(P), pos[:],
                                          ALU.mult, ALU.add))
            for k in range(2):
                link(dve.tensor_tensor(eq[:], oh[k][:], pos[:], ALU.mult))
                link(dve.tensor_reduce(slotf[:, k, :], eq[:], X, ALU.add))
            dve.tensor_copy(sloti[:], slotf[:]).then_inc(slots_ready, 1)
            link(dve.tensor_tensor(isof[:], iota_j[:].unsqueeze(2).to_broadcast([P, 32, EW]),
                                   tend[:].unsqueeze(1).to_broadcast([P, 32, EW]), ALU.is_ge))
            link(dve.tensor_reduce(expf[:], isof[:], X, ALU.add))
            link(dve.tensor_scalar(expf[:], expf[:], float(NE - 1), None, ALU.min))
            link(dve.tensor_copy(packf[:], expf[:, 0:32:XG]))
            for i in range(1, XG + 1):
                these = expf[:, i:32:XG]
                words = packf[:, 0:these.shape[1]]
                link(dve.scalar_tensor_tensor(words, these, float(EW ** i), words, ALU.mult, ALU.add))
            dve.tensor_copy(expi[:], packf[:]).then_inc(slots_ready, 1)

            def product(i, par):
                dve.wait_ge(sg_ready, i + 1)
                dve.tensor_tensor(hh[:, par, :], ps[2 + par][:, INTER:2 * INTER], sg[:, par, :], ALU.mult).then_inc(hh_ready, 1)

            def turn_hidden(i, par):
                dve.wait_ge(h_ps, i + 1)
                dve.tensor_copy(hT[:, par].rearrange("p c n -> p (c n)"), ps[4 + par][0:IH, 0:2 * P]).then_inc(hT_ready, 1)

            def add_shared(t):
                dve.wait_ge(y_ps, t + 1)
                dve.tensor_tensor(xs[:, t, :], ps[6 + t % 2][:, 0:D], xs[:, t, :], ALU.add).then_inc(y_read, 1)

            def keep_result(j, par, stored):
                if stored is not None:
                    dve.wait_ge(y_st[par], stored)
                dve.wait_ge(y_ps, j + NT + 1)
                dve.tensor_copy(ys[:, par, :], ps[6 + par][:, 0:D]).then_inc(y_read, 1)

            for i in range(NT + 1):
                if i >= 2:
                    dve.wait_ge(h_ps, i - 1)
                product(i, i % 2)
                if i >= 1:
                    add_shared(i - 1)
                turn_hidden(i, i % 2)
            def two_tiles(k, stored):
                for par in range(2):
                    j = 2 * k + par + 1
                    dve.wait_ge(h_ps, j + (NT - 1))
                    product(j + NT, 1 - par)
                    keep_result(j - 1, par, stored)
                    turn_hidden(j + NT, 1 - par)

            two_tiles(0, None)
            with dve.Fori(1, NSLOT // 2 - 1) as k:
                two_tiles(k, 16 * k)
            last = NSLOT - 1
            dve.wait_ge(h_ps, last + NT - 1)
            product(last + NT, 1)
            keep_result(last - 1, 0, 16 * (last // 2))
            turn_hidden(last + NT, 1)
            keep_result(last, 1, 16 * (last // 2))
            for t in range(NT):
                dve.wait_ge(gathered[t], 32)
                link(dve.scalar_tensor_tensor(xs[:, t, :], yg[0][:, t, :], cw[0][:, t:t + 1], xs[:, t, :], ALU.mult, ALU.add))
                dve.scalar_tensor_tensor(xs[:, t, :], yg[1][:, t, :], cw[1][:, t:t + 1], xs[:, t, :], ALU.mult,
                                         ALU.add).then_inc(done, 1)

        @block.tensor
        def _(pe):
            def split_product(o, lhs, rhs, first, last):
                for i, (a, b) in enumerate(((0, 0), (0, 1), (1, 0))):
                    ins = pe.matmul(o, lhs[a], rhs[b], start=first and i == 0, stop=last and i == 2, skip_group_check=True)
                return ins

            def add_bias(bank, j):
                rows = slice(32 * (j % 4), 32 * (j % 4) + 2)
                return pe.matmul(bank[:], ones2[rows, :], bias_hl[rows, j // 4, :], start=False, stop=True, skip_group_check=True)

            pe.wait_ge(consts, 1)
            for k in stage_slots():
                t = k - 3
                if 0 <= t < NT:
                    pe.wait_ge(cT_ready, t + 1)
                    if t == 0:
                        pe.wait_ge(ld_small, 16 * 9)
                        pe.wait_ge(consts, 4)
                    if t:
                        pe.wait_ge(kvq_read, t)
                    pe.matmul(ps[3][:], cT[0:DC, t % 2, :], w2kv[:], start=True, stop=True)
                    pe.matmul(ps[4][:, 0:D + DC], cT[DC:P, t % 2, :], w2q[DC:P, :], start=True, stop=True).then_inc(kvq_ps, 1)
                t = k - 1
                if 0 <= t < NT:
                    pe.wait_ge(xnT_ready, t + 1)
                    if t == 0:
                        pe.wait_ge(ld_down, 16 * 6)
                    if t:
                        pe.wait_ge(c_ready, t)
                    for c in range(C):
                        ins = pe.matmul(ps[1][:, 0:192], xnT[:, t % 2, c, :], w1[:, c, :], start=c == 0, stop=c == C - 1)
                    ins.then_inc(c_ps, 1)
                t = k
                if 0 <= t < NT:
                    pe.wait_ge(xn_ready, t + 1)
                    if t:
                        pe.wait_ge(xnT_ready, t)
                    for c in range(C):
                        ins = pe.transpose(ps[0][:, c * P:(c + 1) * P], xn[:, t % 2, c * P:(c + 1) * P], ident[:])
                    ins.then_inc(xnT_ps, 1)
                t = k - 2
                if 0 <= t < NT:
                    pe.wait_ge(c_ready, t + 1)
                    if t:
                        pe.wait_ge(cT_ready, t)
                    pe.transpose(ps[0][:, D:D + P], c1[:, t % 2, :], ident[:]).then_inc(cT_ps, 1)
                t = k - 4
                if 0 <= t < NT:
                    pe.wait_ge(lo_ready, 2 * t + 2)
                    for g in range(4):
                        if t:
                            pe.wait_ge(qkA if g < 2 else qkD, 2 * (t - 1) + g % 2 + 1)
                        for i in range(4):
                            pair = 4 * (g % 2) + i
                            ins = pe.transpose(ps[TURN_BANKS[g]][:, i * P:(i + 1) * P],
                                               qks[:, t % 2, g // 2, 2 * pair:2 * pair + 2, :].rearrange("p h d -> p (h d)").bitcast(F32), ident[:])
                        ins.then_inc(qk_ps, 1)

            pe.wait_ge(qkA, 2 * NT)
            pe.wait_ge(qkD, 2 * NT)
            for u in range(UNITS + P2_LAG + PV_LAG + TURN_LAG):
                if u < UNITS:
                    b, h = u // NH, u % NH
                    unit = 17 * b + h
                    lo = HW * (h % 2)
                    if h == 1 and b:
                        pe.wait_ge(mT_ready, b)
                    elif u >= 2:
                        pe.wait_ge(s1_max, u if h == 0 else u - 1)
                    for q in range(TB):
                        t = TB * b + q
                        ins = pe.matmul(ps[unit % 2][:, q * T:(q + 1) * T], qkT[lo:lo + KS, 0, h // 2, t * P:(t + 1) * P],
                                        qkT[lo:lo + KS, 1, h // 2, b * T:(b + 1) * T], start=True, stop=True)
                    ins.then_inc(s1_ps, 1)
                b = (u - M_LAG + 1) // NH
                if u >= M_LAG - 1 and (u - M_LAG + 1) % NH == 0 and b < B:
                    pe.wait_ge(m_lo, b + 1)
                    for q in range(TB):
                        ins = pe.transpose(ps[(17 * b + 16) % 2][0:32, q * P:(q + 1) * P],
                                           msp[:, q].rearrange("p a b c -> p (a b c)").bitcast(F32), ident[:])
                    ins.then_inc(mT_ps, 1)
                v = u - P2_LAG
                if 0 <= v < UNITS:
                    b, h = v // NH, v % NH
                    lo = HW * (h % 2)
                    if h == 0:
                        pe.wait_ge(mrow, 64 * (b + 1))
                    if v >= 2:
                        pe.wait_ge(pTs_ready, v - 1)
                    for kc in range(TB):
                        t = TB * b + kc
                        ins = pe.matmul(ps[2 + v % 2][:, kc * T:(kc + 1) * T], qkT[lo:lo + KM, 1, h // 2, t * P:(t + 1) * P],
                                        qkT[lo:lo + KM, 0, h // 2, b * T:(b + 1) * T], start=True, stop=True)
                    ins.then_inc(sT_ps, 1)
                v = u - P2_LAG - PV_LAG
                if 0 <= v < UNITS:
                    b, h = v // NH, v % NH
                    pe.wait_ge(pTs_ready, v + 1)
                    if v % 8 == 0 and v >= 16:
                        pe.wait_ge(oTs_ready, v // 8 - 1)
                    row, col = VW * (v % 4), T * (v % 8 // 4)
                    for kc in range(TB):
                        ins = pe.matmul(ps[4 + v // 8 % 2][row:row + VW, col:col + T], va[:, TB * b + kc, h, :],
                                        pTs[:, v % 3, kc, :], start=kc == 0, stop=kc == TB - 1)
                    ins.then_inc(o_ps, 1)
                v -= TURN_LAG
                if v >= 0 and v % 8 == 7:
                    g = v // 8
                    pe.wait_ge(oTs_ready, g + 1)
                    if g % 2 == 0 and g:
                        pe.wait_ge(x1_ready, g // 2)
                    for q in range(TB):
                        for half in range(2):
                            col = (2 * (g % 2) + half) * P
                            ins = pe.transpose(ps[6 + q][:, col:col + P], oTs[:, g % 2, half * T + q * P:half * T + (q + 1) * P],
                                               ident[:])
                    ins.then_inc(o_rows, 1)

            pe.wait_ge(x1_ready, B)
            pe.wait_ge(w_split, len(chunks))
            pe.wait_ge(bias_placed, 16 * 12)
            STEPS = 8 * B * KV
            for s in range(FIRST, LAST):
                if 0 <= s < STEPS:
                    n, r, q = s // 8, (s % 8) // 2, s % 2
                    pe.wait_ge(kT_lo, n + 1)
                    pe.wait_ge(qT_lo, 2 * n + q + 1)
                    if s >= 2:
                        pe.wait_ge(S_masked, s - 1)
                    split_product(ps[s % 2][:], [z[:, n % 2, q, r * P:(r + 1) * P] for z in qT],
                                  [z[:, n % 2, :] for z in kT], True, True).then_inc(S_ps, 1)
                if 0 <= s - 2 < STEPS:
                    i = s - 2
                    pe.wait_ge(p_normed, i + 1)
                    if i >= 2:
                        pe.wait_ge(pT_lo, i - 1)
                    for kt in range(KT_):
                        ins = pe.transpose(ps[2 + i % 2][:, kt * P:(kt + 1) * P], pb[:, i % 3, kt * P:(kt + 1) * P], ident[:])
                    ins.then_inc(pT_ps, 1)
                if s >= 4 and s % 2 == 0 and (s - 4) // 2 < B * XH:
                    h = (s - 4) // 2
                    n = h // GR
                    pe.wait_ge(pT_lo, 2 * h + 2)
                    pe.wait_ge(v_split, n + 1)
                    if h:
                        pe.wait_ge(o_lo, h)
                    for kt in range(KT_):
                        ins = split_product(ps[4][:, 0:T], [z[:, n % 2, kt, :] for z in vS], [z[:, h % 2, kt, :] for z in pT],
                                            kt == 0, kt == KT_ - 1)
                    ins.then_inc(pv_ps, 1)
                if s >= 5 and s % 2 == 1 and (s - 5) // 2 < B * XH:
                    h = (s - 5) // 2
                    b, hd = h // XH, h % XH
                    pe.wait_ge(o_lo, h + 1)
                    if hd == 0 and b:
                        pe.wait_ge(x2_ready, b)
                    if h == 0:
                        pe.wait_ge(wo_split, len(wo_chunks))
                    for q in range(TB):
                        ins = split_product(ps[5][:, q * D:(q + 1) * D], [z[:, q * P:(q + 1) * P] for z in oT],
                                            [z[:, hd, :] for z in WoS], hd == 0 and q == 0, hd == XH - 1)
                    ins.then_inc(wo_ps, 1)

                for task in tasks.get(s, ()):
                    kind, *a = task
                    if task not in side:
                        continue
                    m = side[task]
                    bank = side_bank(task)
                    if m >= 2:
                        pe.wait_ge(*released(side_order[m - 2]))
                    if kind == "CT":
                        b, c = a
                        pe.wait_ge(ld_ctx, 16 * (b + 1))
                        for kt in range(KT_):
                            ins = pe.transpose(bank[:, kt * P:(kt + 1) * P], craw[:, kt, c * P:(c + 1) * P], ident[:])
                    if kind == "XT":
                        b, = a
                        pe.wait_ge(xnD_ready, TB * (b + 1))
                        for c in range(C):
                            for q in range(TB):
                                ins = pe.transpose(bank[:, c * T + q * P:c * T + (q + 1) * P], xnD[:, q, c * P:(c + 1) * P], ident[:])
                    if kind in ("KP", "VP"):
                        b, kt = a
                        pe.wait_ge(ctx_lo, 2 * (b + 1))
                        off, j = (OFF_K, 4) if kind == "KP" else (OFF_V, 5)
                        for c in range(C):
                            split_product(bank[:], [z[:, c, kt * P:(kt + 1) * P] for z in ctxT],
                                          [z[:, off + c * 512:off + (c + 1) * 512] for z in Wkvq], c == 0, False)
                        ins = add_bias(bank, j)
                    if kind == "QP":
                        n, qt = a
                        g = n % 4
                        pe.wait_ge(xT_lo, n // 4 + 1)
                        for c in range(C):
                            off = OFF_Q + c * 2048 + g * GW
                            split_product(bank[:], [z[:, c, qt * P:(qt + 1) * P] for z in xT],
                                          [z[:, off:off + GW] for z in Wkvq], c == 0, False)
                        ins = add_bias(bank, g)
                    if kind == "KT":
                        n, = a
                        pe.wait_ge(normed, norm_chain[("K", n // 4)] + 1)
                        for kt in range(KT_):
                            ins = pe.transpose(bank[:, kt * P:(kt + 1) * P], kraw[:, kt, (n % 4) * HD:(n % 4 + 1) * HD], ident[:])
                    if kind == "QT":
                        n, qt = a
                        pe.wait_ge(normed, norm_chain[("Q", n)] + 1)
                        for r in range(GR):
                            ins = pe.transpose(bank[:, r * P:(r + 1) * P], qraw[:, qt, r * P:(r + 1) * P], ident[:])
                    ins.then_inc(m_ps, 1)


            for u in range(4):
                pe.wait_ge(xn3_ready, 4 * (u % 2) + 4)
                if u == 0:
                    pe.wait_ge(x2_ready, B)
                for i in range(4):
                    t = 4 * (u % 2) + i
                    ins = pe.transpose(ps[u][:, i * P:(i + 1) * P], xn3[:, t, (u // 2) * P:(u // 2 + 1) * P], ident[:])
                ins.then_inc(x3_ps, 1)
            pe.wait_ge(x3_T, 4)
            pe.wait_ge(ld_shared, 48)
            for t in range(NT):
                for c in range(C):
                    ins = pe.matmul(ps[4][:, t * EW:t * EW + NE], xn3T[:, c, t * P:(t + 1) * P], gw[:, c, 0:NE],
                                    start=c == 0, stop=c == C - 1)
            ins.then_inc(gate_ps, 1)

            def up(i, par, lhs, e):
                for c in range(C):
                    ins = pe.matmul(ps[2 + par][:, 0:2 * INTER], lhs[c], w13[:, e, c, :], start=c == 0, stop=c == C - 1)
                ins.then_inc(up_ps, 1)

            def turn_hidden(i, par):
                pe.wait_ge(hh_ready, i + 1)
                for c in range(2):
                    ins = pe.transpose(ps[4 + par][0:IH, c * P:(c + 1) * P], hh[:, par, c * IH:(c + 1) * IH], ident[:])
                ins.then_inc(h_ps, 1)

            def down(i, par, e):
                pe.wait_ge(hT_ready, i + 1)
                for c in range(2):
                    ins = pe.matmul(ps[6 + par][:, 0:D], hT[:, par, c, :], w2s[:, e, c, :], start=c == 0, stop=c == 1)
                ins.then_inc(y_ps, 1)

            def turn_rows(j, par, buf, ld):
                pe.wait_ge(xg_ld[buf], ld)
                for c in range(C):
                    ins = pe.transpose(ps[par][:, c * P:(c + 1) * P], xg[:, buf, c * P:(c + 1) * P], ident[:])
                ins.then_inc(xg_ps, 1)

            pe.wait_ge(chosen_ready, 1)
            flat = chosen[:].rearrange("p t e -> p (t e)")
            pe.matmul(ps[0][:, 0:P], upper[:], flat, start=True, stop=True)
            pe.matmul(ps[0][:, P:2 * P], onesf[:], flat, start=True, stop=True).then_inc(rank_ps, 1)
            for i in range(NT):
                if i >= 2:
                    pe.wait_ge(hh_ready, i - 1)
                up(i, i % 2, [xn3T[:, c, i * P:(i + 1) * P] for c in range(C)], NE)
                if i >= 1:
                    if i >= 3:
                        pe.wait_ge(y_read, i - 2)
                    down(i - 1, (i - 1) % 2, NE)
                turn_hidden(i, i % 2)

            pe.wait_ge(slots_ready, 2)
            pe.wait_ge(ld_e, 16 * 6)

            def experts_of(k):
                word = pe.value_load(expi[0:1, bass.ds(k, 1)], min_val=0, max_val=EW ** (XG + 1) - 1)
                return [word // EW ** i % EW for i in range(XG + 1)]

            def routed(j, par, e, e_before, buf, ld):
                pe.wait_ge(xgT_ready, j + 1)
                pe.wait_ge(hh_ready, j + (NT - 1))
                for c in range(C):
                    ins = pe.matmul(ps[2 + par][:, 0:2 * INTER], xgT[:, par, c, :],
                                    w13[:, bass.ds(e, 1), c, :].rearrange("p e n -> p (e n)"), start=c == 0, stop=c == C - 1)
                ins.then_inc(up_ps, 1)
                if buf is not None:
                    turn_rows(j + 1, 1 - par, buf, ld)
                pe.wait_ge(y_read, j + (NT - 2))
                pe.wait_ge(hT_ready, j + NT)
                for c in range(2):
                    if e_before is None:
                        rhs = w2s[:, NE, c, :]
                    else:
                        rhs = w2s[:, bass.ds(e_before, 1), c, :].rearrange("p e n -> p (e n)")
                    ins = pe.matmul(ps[7 - par][:, 0:D], hT[:, 1 - par, c, :], rhs, start=c == 0, stop=c == 1)
                ins.then_inc(y_ps, 1)
                turn_hidden(j + NT, par)

            turn_rows(0, 0, 0, 16)
            routed(0, 0, experts_of(0)[0], None, 1, 16)
            with pe.Fori(0, NSLOT // XG) as k:
                e = experts_of(k)
                for i in range(1, XG + 1):
                    buf = (i + 1) % XG
                    routed(XG * k + i, i % 2, e[i], e[i - 1], buf, 16 * (k + 1 + (i + 1) // XG))
            last = NSLOT - 1
            e = experts_of(last // XG)
            routed(last, 1, e[1], e[0], None, None)
            pe.wait_ge(hT_ready, last + NT + 1)
            for c in range(2):
                ins = pe.matmul(ps[7][:, 0:D], hT[:, 1, c, :], w2s[:, bass.ds(e[1], 1), c, :].rearrange("p e n -> p (e n)"),
                                start=c == 0, stop=c == 1)
            ins.then_inc(y_ps, 1)


_INS = ["x", "ctx_2048", "mask_1xSxS2_ff0"] + ["L0_attn_" + n for n in (
    "W_DKV", "b_DKV", "W_UK", "b_UK", "W_UV", "b_UV", "W_DQ", "b_DQ", "W_UQ", "b_UQ", "W_QR", "b_QR", "W_KR", "b_KR")] + [
    "L0_xattn_" + n for n in ("Wq", "bq", "Wk", "bk", "Wv", "bv", "Wo", "qn_w", "kn_w")]


def rope_table():
    f32 = np.float32
    freqs = f32(10000.0) ** (-(np.arange(0, DR, 2, dtype=f32) / f32(DR)))
    theta = np.arange(T, dtype=f32)[:, None] * freqs[None, :]
    cos, sin = np.cos(theta), np.sin(theta)
    rows = np.stack([np.stack([cos, sin], -1).reshape(T, DR), np.stack([sin, cos], -1).reshape(T, DR)], 1)
    return np.ascontiguousarray(rows.reshape(TB, P, 2, DR).transpose(1, 0, 2, 3).astype(f32))


def kernel(**inputs):
    import concourse.bacc as bacc
    from concourse.bass_utils import run_bass_kernel_spmd

    nc = bacc.Bacc("TRN2", target_bir_lowering=False, num_devices=1)
    arrays, args = {}, []

    def give(name, a):
        arrays[name] = a
        args.append(nc.dram_tensor(name, a.shape, mybir.dt.from_np(a.dtype), kind="ExternalInput").ap())

    for name in _INS:
        give(f"in_{name}", np.ascontiguousarray(inputs[name]))
    f = {n: inputs["L0_ffn_" + n] for n in ("gate_w", "w1", "w2", "w3", "sw1", "sw2", "sw3")}
    give("gate_wT", np.ascontiguousarray(f["gate_w"].T))
    w1, w3, w2 = (np.concatenate([f[n], f["s" + n][None]]) for n in ("w1", "w3", "w2"))
    give("w13T", np.ascontiguousarray(np.concatenate([w1, w3], 1).transpose(0, 2, 1)))
    give("w2T", np.ascontiguousarray(w2.transpose(0, 2, 1)))
    give("rope_cs", rope_table())
    args.append(nc.dram_tensor("out_0", (B, T, D), F32, kind="ExternalOutput").ap())
    layer(nc, *args)
    r = run_bass_kernel_spmd(nc, [arrays], core_ids=[0])
    return r.results[0]["out_0"]
```

```python
from contextlib import ExitStack

import numpy as np

import concourse.bass as bass
from concourse import mybir

F32 = mybir.dt.float32
F32R = mybir.dt.float32r
ALU = mybir.AluOpType
ACT = mybir.ActivationFunctionType
X = mybir.AxisListType.X

P = 128
B, T, D = 4, 256, 256
NT = B * T // P
TB = T // P
LN1_SETS = NT // TB
C = D // P
LN_EPS = 1e-5
NH, DC = 16, 64
DH, DR = D // NH, DC // NH
DQ = DH + DR
HW = 64
KS = 3 * DQ
KM = KS + 2
VW = 32
NP = NH // 2
SA_SCALE = float(DQ) ** -0.5
SE, XH, KV, HD = 512, 16, 4, 128
KT_ = SE // P
GR = XH // KV
GW = GR * HD
RMS_EPS = 1e-6
XSCALE = float(HD) ** -0.5

NE, INTER = 15, 176
IH = INTER // 2
EW = 16
LEAD = 4
XG = 4
NSLOT = (2 * B * T - NE) // P + NE
FINITE_LOW = -3.0e38


def xattn_tasks():
    tasks = {}

    def put(slot, *task):
        tasks.setdefault(slot, []).append(task)

    for b in range(B):
        lead = 8 * (4 * b - 2) if b else -19
        own = 8 * (4 * b - 1) if b else -10
        put(lead - 1, "LNV", b)
        put(lead + 0, "CT", b, 0)
        put(lead + 2, "CT", b, 1)
        put(lead + 1, "LNW", b)
        put(lead + 3, "XT", b)
        for kt in range(KT_):
            put(own - 4 + kt, "KP", b, kt)
            put(own - 2 + kt, "SS", "K", b, kt)
            put(own + 1 + kt, "VP", b, kt)
        put(own + 1, "VE", "K", b)
        put(own + 3, "NW", "K", b)
        if b < B - 1:
            late = 8 * B * KV - 11 + 2 * b
            put(late, "L3V", b)
            put(late + 2, "L3W", b)
            put(late + 3, "X3", b)
    for n in range(B * KV):
        own = 8 * (n - 1) if n else -10
        for qt in range(TB):
            put(own - 1 + 2 * qt, "QP", n, qt)
            put(own + 1 + 2 * qt, "SS", "Q", n, qt)
        put(own + 3, "VE", "Q", n)
        put(own + 4, "NW", "Q", n)
        put(own + (4 if n % KV else 5), "KT", n)
        for qt in range(TB):
            put(own + 5 + qt, "QT", n, qt)
        put(own + 6, "VS", n)
    return tasks


EVACUATED = ("CT", "XT", "KP", "VP", "QP", "KT", "QT", "X3")


def layer(nc, x, ctx_in, mask, W_DKV, b_DKV, W_UK, b_UK, W_UV, b_UV, W_DQ, b_DQ, W_UQ, b_UQ, W_QR, b_QR,
          W_KR, b_KR, Wq, bq, Wk, bk, Wv, bv, Wo, qn_w, kn_w, gate_wT, w13T, w2T, rope_cs, out):
    es = ExitStack()
    with es:
        def sb(name, shape, dt=F32, stack=es):
            return stack.enter_context(nc.sbuf_tensor(name, shape, dt))

        def sem(name):
            return es.enter_context(nc.semaphore(name))

        ps = [es.enter_context(nc.psum_tensor(f"bank{i}", [P, 512], F32)) for i in range(8)]

        xs = sb("xs", [P, NT, D])
        ident = sb("ident", [P, P])
        OFF_K, OFF_V, OFF_Q, W_COLS = 0, C * KV * HD, 2 * C * KV * HD, 2 * C * KV * HD + C * XH * HD
        Wkvq = [sb(f"Wkvq{i}", [P, W_COLS], F32R) for i in "hl"]
        bias_hl = sb("bias_hl", [98, 2, 512], F32R)
        ones2 = sb("ones2", [98, P], F32R)
        stats = sb("stats", [P, 2, 6])
        wqk = sb("wqk", [P, 1])
        mv = sb("mv", [P, NT, 2])
        ve = sb("ve", [P, 16])
        lnv = sb("lnv", [P, 16])
        r0 = sb("r0", [P, 16])
        nwt = sb("nwt", [P, 16])
        rln = sb("rln", [P, NT])

        upper = sb("upper", [P, P])
        onesf = sb("onesf", [P, P])
        zeros = sb("zeros", [P, D])
        iota_e = sb("iota_e", [P, EW])
        iota_t = sb("iota_t", [P, NT])
        iota_j = sb("iota_j", [P, 32])

        esA = ExitStack()
        es.enter_context(esA)
        w1 = sb("w1", [P, C, 192], F32, esA)
        w2kv = sb("w2kv", [DC, 2 * D], F32, esA)
        w2q = sb("w2q", [P, D + DC], F32, esA)
        b1 = sb("b1", [P, 192], F32, esA)
        b2 = sb("b2", [P, 832], F32, esA)
        cs = sb("cs", [P, TB, 2, 4], F32, esA)
        xn = sb("xn", [P, 2, D], F32, esA)
        xnT = sb("xnT", [P, 2, C, P], F32, esA)
        c1 = sb("c1", [P, 2, 128], F32, esA)
        rr = sb("rr", [P, 3, 2, DC], F32, esA)
        cT = sb("cT", [P, 2, P], F32, esA)
        cat = sb("cat", [P, 2, 2, NH, DQ], F32, esA)
        rp1 = sb("rp1", [P, 2 * NH, DR], F32, esA)
        rp2 = sb("rp2", [P, 2 * NH, DR], F32, esA)
        qks = sb("qks", [P, 2, 2, NH, HW], F32R, esA)
        wraw = sb("wraw", [P, 2, 512], F32, esA)
        braw = sb("braw", [6, 512], F32, esA)
        bsp = [sb(f"bsp{i}", [6, 512], F32R, esA) for i in "hl"]
        qkw = sb("qkw", [P, 2], F32, esA)
        qkT = sb("qkT", [P, 2, NP, B * T], F32R, esA)
        va = sb("va", [P, NT, NH, VW], F32, esA)
        oTs = sb("oTs", [P, 2, 2 * T], F32, esA)
        mneg = sb("mneg", [P, 2, TB, NH], F32, esA)
        msp = sb("msp", [P, TB, 2, 2, NP], F32R, esA)
        mT = sb("mT", [32, 2, T], F32R, esA)
        pTs = sb("pTs", [P, 3, 2, T], F32, esA)
        rsv = sb("rsv", [P, TB, NH], F32, esA)
        osa = sb("osa", [P, TB, NH, DH], F32, esA)
        esA.close()

        esD = ExitStack()
        es.enter_context(esD)
        WoS = [sb(f"Wo{i}", [P, XH, D], F32R, esD) for i in "hl"]
        wraw2 = sb("wraw2", [P, 2, 512], F32, esD)
        craw = sb("craw", [P, KT_, D], F32, esD)
        msk = sb("msk", [P, TB, SE], F32, esD)
        ctxT = [sb(f"ctxT{i}", [P, C, SE], F32R, esD) for i in "hl"]
        xnD = sb("xnD", [P, TB, D], F32, esD)
        xT = [sb(f"xT{i}", [P, C, T], F32R, esD) for i in "hl"]
        kraw = sb("kraw", [P, KT_, KV * HD], F32, esD)
        vraw = sb("vraw", [P, KT_, KV * HD], F32, esD)
        qraw = sb("qraw", [P, TB, GW], F32, esD)
        sq = sb("sq", [P, 2, 512], F32, esD)
        ssK = sb("ssK", [P, 16], F32, esD)
        ssQ = sb("ssQ", [P, 8], F32, esD)
        rK = sb("rK", [P, 16], F32, esD)
        rQ = sb("rQ", [P, 8], F32, esD)
        kT = [sb(f"kT{i}", [P, 2, SE], F32R, esD) for i in "hl"]
        vS = [sb(f"vS{i}", [P, 2, KT_, HD], F32R, esD) for i in "hl"]
        qT = [sb(f"qT{i}", [P, 2, TB, GW], F32R, esD) for i in "hl"]
        pb = sb("pb", [P, 3, SE], F32, esD)
        nmax = sb("nmax", [P, 3], F32, esD)
        psm = sb("psm", [P, 3], F32, esD)
        rinv = sb("rinv", [P, 3], F32, esD)
        pT = [sb(f"pT{i}", [P, 2, KT_, T], F32R, esD) for i in "hl"]
        oT = [sb(f"oT{i}", [P, T], F32R, esD) for i in "hl"]
        esD.close()

        esF = ExitStack()
        es.enter_context(esF)
        w13 = sb("w13", [P, NE + 1, C, 2 * INTER], F32, esF)
        xn3 = sb("xn3", [P, NT, D], F32, esF)
        xg = sb("xg", [P, XG, D], F32, esF)
        xgT = sb("xgT", [P, 2, C, P], F32, esF)
        xn3T = sb("xn3T", [P, C, B * T], F32, esF)
        gw = sb("gw", [P, C, EW], F32, esF)
        w2s = sb("w2s", [IH, NE + 1, 2, D], F32, esF)
        lg = sb("lg", [P, NT, EW], F32, esF)
        lge = sb("lge", [P, NT, EW], F32, esF)
        eq = sb("eq", [P, NT, EW], F32, esF)
        oh = [sb(f"onehot{i}", [P, NT, EW], F32, esF) for i in range(2)]
        chosen = sb("chosen", [P, NT, EW], F32, esF)
        top = [sb(f"top{i}", [P, NT], F32, esF) for i in range(2)]
        first_e = sb("first_e", [P, NT], F32, esF)
        cw = [sb(f"combine{i}", [P, NT], F32, esF) for i in range(2)]
        running = [sb(f"running{i}", [P, NT // 2 + NT, EW], F32, esF) for i in range(2)]
        more = sb("more", [P, EW, NT], F32, esF)
        ntile = sb("ntile", [P, EW], F32, esF)
        tend = sb("tend", [P, EW], F32, esF)
        pos = sb("pos", [P, NT, EW], F32, esF)
        slotf = sb("slotf", [P, 2, NT], F32, esF)
        sloti = sb("sloti", [P, 2, NT], mybir.dt.int32, esF)
        isof = sb("isof", [P, 32, EW], F32, esF)
        expf = sb("expf", [P, 32], F32, esF)
        packf = sb("packf", [P, 32 // XG], F32, esF)
        expi = sb("expi", [P, 32 // XG], mybir.dt.int32, esF)
        sg = sb("sg", [P, 2, INTER], F32, esF)
        hh = sb("hh", [P, 2, INTER], F32, esF)
        hT = sb("hT", [IH, 2, 2, P], F32, esF)
        ys = sb("ys", [P, 2, D], F32, esF)
        yg = [sb(f"yg{i}", [P, NT, D], F32, esF) for i in range(2)]
        esF.close()
        xg_dram = nc.dram_tensor("rows_by_slot", (NSLOT * P, D), F32, kind="Internal").ap()
        yg_dram = nc.dram_tensor("results_by_slot", (NSLOT * P, D), F32, kind="Internal").ap()

        ld_small, ld_down, ld_b, ld_mask, ld_ctx, st_out, mrow = [
            sem(n) for n in ("ld_small", "ld_down", "ld_b", "ld_mask", "ld_ctx", "st_out", "mrow_moved")]
        act_self, dve_self, pool_self = sem("act_self"), sem("dve_self"), sem("pool_self")
        consts = sem("consts_ready")
        w_split, b_split = sem("w_split"), sem("b_split")
        var_ready, r0_ready, rln_ready = sem("var_ready"), sem("r0_ready"), sem("rln_ready")
        xn_ready, xnT_ps, xnT_ready, c_ps, c_ready, cT_ps, cT_ready, kvq_ps, cat_ready = [
            sem(n) for n in ("xn_ready", "xnT_ps", "xnT_ready", "c_ps", "c_ready", "cT_ps", "cT_ready",
                             "kvq_ps", "cat_ready")]
        kvq_read = sem("kvq_read")
        hi_ready, lo_ready, qk_ps, qkA, qkD = [sem(n) for n in ("hi_ready", "lo_ready", "qk_ps", "qk_by_act", "qk_by_dve")]
        s1_ps, s1_max, m_hi, m_lo, mT_ps, mT_ready = [
            sem(n) for n in ("s1_ps", "s1_max", "m_hi", "m_lo", "mT_ps", "mT_ready")]
        sT_ps, pTs_ready, o_ps, oTs_ready, o_rows, x1_ready = [
            sem(n) for n in ("sT_ps", "pTs_ready", "o_ps", "oTs_ready", "o_rows", "x1_ready")]
        ld_x = [sem(f"ld_x{i}") for i in range(2)]
        m_ps, ctx_hi, ctx_lo, xT_hi, xT_lo = [sem(n) for n in ("m_ps", "ctx_hi", "ctx_lo", "xT_hi", "xT_lo")]
        bias_placed, wo_high, wo_split, w_high = [sem(n) for n in ("bias_placed", "wo_high", "wo_split", "w_high")]
        ld_w, ld_wo = [[sem(f"{n}{i}") for i in range(2)] for n in ("ld_w", "ld_wo")]
        xnD_ready, raw_ready, v_ready, sq_ready, ss_ready = [
            sem(n) for n in ("xnD_ready", "raw_ready", "v_ready", "sq_ready", "ss_ready")]
        rk_var, rk_r0, rk_ready, k_normed, q_normed = [
            sem(n) for n in ("rk_var", "rk_r0", "rk_ready", "k_normed", "q_normed")]
        v_split, kT_hi, kT_lo, qT_hi, qT_lo = [sem(n) for n in ("v_split", "kT_hi", "kT_lo", "qT_hi", "qT_lo")]
        S_ps, S_masked, exp_done, rinv_ready, pT_ps, pT_hi, pT_lo = [
            sem(n) for n in ("S_ps", "S_masked", "exp_done", "rinv_ready", "pT_ps", "pT_hi", "pT_lo")]
        p_normed = [sem(f"p_normed{i}") for i in range(2)]
        pv_ps, o_hi, o_lo, wo_ps, x2_ready = [sem(n) for n in ("pv_ps", "o_hi", "o_lo", "wo_ps", "x2_ready")]

        ld_e, zeroed, zero_src = [sem(n) for n in ("ld_experts", "xg_zeroed", "zero_src")]
        ld_shared, ld_gate = sem("ld_shared"), sem("ld_gate")
        xn3_ready, x3_ps, x3_T, gate_ps, lgm_ready, lge_ready, chosen_ready, rank_ps, slots_ready, scattered = [
            sem(n) for n in ("xn3_ready", "x3_ps", "x3_T", "gate_ps", "lgm_ready", "lge_ready", "chosen_ready", "rank_ps",
                             "slots_ready", "scattered")]
        xg_ld = [sem(f"xg_ld{i}") for i in range(XG)]
        y_st = [sem(f"y_st{i}") for i in range(2)]
        gathered = [sem(f"gathered{t}") for t in range(NT)]
        xg_ps, xgT_ready, up_ps, sg_ready, hh_ready, h_ps, hT_ready, y_ps, y_read, done = [
            sem(n) for n in ("xg_ps", "xgT_ready", "up_ps", "sg_ready", "hh_ready", "h_ps", "hT_ready", "y_ps", "y_read",
                             "done")]

        x_dram = x.rearrange("b (j p) d -> p (b j) d", p=P)
        out_dram = out.rearrange("b (j p) d -> p (b j) d", p=P)

        chunks = []
        for c in range(C):
            rows = slice(c * P, (c + 1) * P)
            chunks.append((OFF_K + 512 * c, Wk[rows, :]))
            chunks.append((OFF_V + 512 * c, Wv[rows, :]))
            for g in range(KV):
                chunks.append((OFF_Q + XH * HD * c + GW * g, Wq[rows, g * GW:(g + 1) * GW]))
        wo_chunks = [Wo[i * 2 * P:(i + 1) * 2 * P, :].rearrange("(h p) n -> p h n", p=P) for i in range(XH // 2)]

        def stage_slots():
            return range(NT + 4)

        TURN_BANKS = (5, 6, 7, 2)
        M_LAG, P2_LAG, PV_LAG, TURN_LAG = 17, 21, 2, 3
        UNITS = B * NH
        side = {}
        tasks = xattn_tasks()
        FIRST, LAST = min(tasks), 8 * B * KV + 7
        for s in range(FIRST, LAST):
            for task in tasks.get(s, ()):
                if task[0] in EVACUATED:
                    side[task] = len(side)
        norm_unit = {}
        norm_chain = {}
        for s in range(FIRST, LAST):
            for task in tasks.get(s, ()):
                if task[0] in ("KP", "QP"):
                    norm_unit[(task[0][0], *task[1:])] = len(norm_unit)
                if task[0] == "VE":
                    norm_chain[task[1:]] = len(norm_chain)

        ln_set = {}
        for s in range(FIRST, LAST):
            for task in tasks.get(s, ()):
                if task[0] in ("LNV", "L3V"):
                    ln_set[(task[0][:2], task[1])] = LN1_SETS + 1 + len(ln_set)
        LN_SETS = LN1_SETS + 1 + len(ln_set)

        side_order = list(side)

        def released(task):
            kind, *a = task
            if kind in ("KP", "QP"):
                return raw_ready, norm_unit[(kind[0], *a)] + 1
            return {"CT": lambda b, c: (ctx_lo, C * b + c + 1), "XT": lambda b: (xT_lo, b + 1), "X3": lambda b: (x3_T, b + 1),
                    "VP": lambda b, kt: (v_ready, KT_ * b + kt + 1), "KT": lambda n: (kT_lo, n + 1),
                    "QT": lambda n, qt: (qT_lo, TB * n + qt + 1)}[kind](*a)

        def products_of(s):
            return [t for t in tasks.get(s - 1, ()) if t[0] in EVACUATED]

        def other_work(s):
            return [t for t in tasks.get(s, ()) if t[0] not in EVACUATED]

        def side_bank(task):
            return ps[6 + side[task] % 2]

        block = es.enter_context(nc.Block())

        @block.sync
        def _(sp):
            sp.dma_start(xs[:, 0:TB, :], x_dram[:, 0:TB, :]).then_inc(ld_x[0], 16)
            for off, w in ((0, W_DKV), (DC, W_DQ), (2 * DC, W_KR)):
                sp.dma_start(w1[:, :, off:off + DC], w.rearrange("(c p) n -> p c n", p=P)).then_inc(ld_down, 16)
            for off, v, n in ((0, b_DKV, DC), (DC, b_DQ, DC), (2 * DC, b_KR, DC)):
                sp.dma_start(b1[:, off:off + n], v.rearrange("(a n) -> a n", a=1).to_broadcast([P, n])).then_inc(ld_down, 16)
            sp.dma_start(xs[:, TB:NT, :], x_dram[:, TB:NT, :]).then_inc(ld_x[1], 16)
            for row, v in ((0, bq), (4, bk), (5, bv)):
                sp.dma_start(braw[row:row + v.shape[0] // 512, :], v.rearrange("(a n) -> a n", n=512)).then_inc(ld_b, 16)
            sp.dma_start(qkw[:, 0:1], qn_w.rearrange("(p a) -> p a", a=1)).then_inc(ld_b, 16)
            sp.dma_start(qkw[:, 1:2], kn_w.rearrange("(p a) -> p a", a=1)).then_inc(ld_b, 16)
            for i, (off, src) in enumerate(chunks):
                if i >= 2:
                    sp.wait_ge(w_split, i - 1)
                sp.dma_start(wraw[:, i % 2, :], src).then_inc(ld_w[i % 2], 16)
            sp.wait_ge(b_split, 3)
            for j in range(6):
                for part in range(2):
                    row = 32 * (j % 4) + part
                    sp.dma_start(bias_hl[row:row + 1, j // 4, :].bitcast(F32), bsp[part][j:j + 1, :].bitcast(F32)).then_inc(bias_placed, 16)
            sp.wait_ge(s1_ps, 1)
            sp.wait_ge(w_split, len(chunks))
            sp.wait_ge(bias_placed, 16 * 12)
            for i in range(2):
                sp.dma_start(wraw2[:, i, :].rearrange("p (h n) -> p h n", h=2), wo_chunks[i]).then_inc(ld_wo[i], 16)
            sp.dma_start(craw[:], ctx_in[0].rearrange("(k p) d -> p k d", p=P)).then_inc(ld_ctx, 16)
            sp.dma_start(msk[:], mask.rearrange("a (j p) e -> p (a j) e", p=P)).then_inc(ld_mask, 16)
            for b in range(B):
                if b:
                    sp.wait_ge(mrow, 64 * b)
                sp.wait_ge(mT_ready, b + 1)
                for jj in range(2):
                    for part in range(2):
                        row = jj * 16 + part * 8
                        to = 64 * jj + KS + part
                        sp.dma_start(qkT[to:to + 1, 0, :, b * T:(b + 1) * T].bitcast(F32), mT[row:row + 8, b % 2, :].bitcast(F32)).then_inc(mrow, 16)
            for b in range(1, B):
                sp.wait_ge(m_ps, side[("CT", b - 1, 1)] + 1)
                sp.dma_start(craw[:], ctx_in[b].rearrange("(k p) d -> p k d", p=P)).then_inc(ld_ctx, 16)
                if b == 1:
                    sp.wait_ge(zero_src, 1)
                    sp.dma_start(xg_dram.rearrange("(j p) d -> p j d", p=P),
                                 zeros[:].unsqueeze(1).to_broadcast([P, NSLOT, D])).then_inc(zeroed, 16)
            sp.wait_ge(v_split, B * KV)
            sp.dma_start(gw[:, :, 0:NE], gate_wT.rearrange("(c p) e -> p c e", p=P)).then_inc(ld_gate, 16)
            sp.wait_ge(x2_ready, B)
            sp.dma_start(w13[:, NE, :, :], w13T[NE].rearrange("(c p) n -> p c n", p=P)).then_inc(ld_shared, 16)
            sp.dma_start(w2s[:, NE, :, :], w2T[NE].rearrange("(c p) n -> p c n", p=IH)).then_inc(ld_shared, 16)
            for e in range(0, NE, 5):
                sp.dma_start(w13[:, e:e + 5].rearrange("p e c n -> p (e c) n"),
                             w13T[e:e + 5].rearrange("e (c p) n -> p (e c) n", p=P)).then_inc(ld_e, 16)
                sp.dma_start(w2s[:, e:e + 5].rearrange("p e c n -> p (e c) n"),
                             w2T[e:e + 5].rearrange("e (c p) n -> p (e c) n", p=IH)).then_inc(ld_e, 16)

            xg_rows = xg_dram.rearrange("(j p) d -> p j d", p=P)
            yg_rows = yg_dram.rearrange("(j p) d -> p j d", p=P)

            def load(j, buf):
                sp.dma_start(xg[:, buf:buf + 1, :], xg_rows[:, bass.ds(j, 1), :]).then_inc(xg_ld[buf], 16)

            def store(j, par):
                sp.wait_ge(y_read, j + LEAD + 1)
                sp.dma_start(yg_rows[:, bass.ds(j, 1), :], ys[:, par:par + 1, :]).then_inc(y_st[par], 16)

            sp.wait_ge(scattered, 16 * 2 * NT)
            for j in range(XG):
                load(j, j)
            with sp.Fori(0, NSLOT // XG - 1) as k:
                for i in range(XG):
                    sp.wait_ge(xg_ps, XG * k + i + 1)
                    load(XG * k + i + XG, i)
                    store(XG * k + i, i % 2)
            for j in range(XG * (NSLOT // XG - 1), NSLOT):
                if j + XG < NSLOT:
                    sp.wait_ge(xg_ps, j + 1)
                    load(j + XG, j % XG)
                store(j, j % 2)
            for t in range(NT):
                sp.wait_ge(done, t + 1)
                sp.dma_start(out_dram[:, t, :], xs[:, t, :]).then_inc(st_out, 16)
            sp.wait_ge(st_out, 16 * NT)

        @block.gpsimd
        def _(pool):
            n_self = 0

            def link(ins):
                nonlocal n_self
                n_self += 1
                ins.then_inc(pool_self, 1)
                pool.wait_ge(pool_self, n_self)

            link(pool.memset(ident[:], 0.0))
            pool.affine_select(out=ident[:], in_=ident[:], compare_op=ALU.not_equal, fill=1.0, base=0,
                               pattern=[[-1, P]], channel_multiplier=1).then_inc(consts, 1)
            link(pool.memset(qks[:].bitcast(F32), 0.0))
            pool.memset(qks[:, :, 1, :, KS:KM].bitcast(F32), 1.0).then_inc(consts, 1)
            link(pool.memset(va[:], 0.0))
            pool.memset(va[:, :, :, DH:DH + 1], 1.0).then_inc(consts, 1)
            pool.memset(ones2[:].bitcast(F32), 1.0).then_inc(consts, 1)
            pool.memset(zeros[:], 0.0).then_inc(zero_src, 1)
            pool.memset(onesf[:], 1.0).then_inc(pool_self, 1)
            link(pool.memset(upper[:], 1.0))
            n_self += 1
            pool.wait_ge(pool_self, n_self)
            pool.affine_select(out=upper[:], in_=upper[:], compare_op=ALU.is_gt, fill=0.0, base=0, pattern=[[1, P]],
                               channel_multiplier=-1).then_inc(consts, 1)
            pool.iota(iota_e[:], pattern=[[1, EW]], base=0, channel_multiplier=0,
                      allow_small_or_imprecise_dtypes=True).then_inc(consts, 1)
            pool.iota(iota_t[:], pattern=[[P, NT]], base=0, channel_multiplier=0,
                      allow_small_or_imprecise_dtypes=True).then_inc(consts, 1)
            pool.iota(iota_j[:], pattern=[[1, 32]], base=0, channel_multiplier=0,
                      allow_small_or_imprecise_dtypes=True).then_inc(consts, 1)
            pool.wait_ge(ld_b, 16 * 5)
            link(pool.tensor_tensor(wqk[:], qkw[:, 0:1], qkw[:, 1:2], ALU.mult))
            pool.tensor_scalar(wqk[:], wqk[:], XSCALE, None, ALU.mult).then_inc(b_split, 1)
            pool.tensor_copy(bsp[0][:], braw[:]).then_inc(b_split, 1)
            pool.wait_ge(b_split, 2)
            pool.tensor_tensor(bsp[1][:], braw[:], bsp[0][:].bitcast(F32), ALU.subtract).then_inc(b_split, 1)

            def split_weights(i):
                off, _ = chunks[i]
                pool.wait_ge(w_high, i + 1)
                pool.tensor_tensor(Wkvq[1][:, off:off + 512], wraw[:, i % 2, :], Wkvq[0][:, off:off + 512].bitcast(F32),
                                   ALU.subtract).then_inc(w_split, 1)

            for k in stage_slots():
                t = k - 3
                if 0 <= t < NT:
                    pool.wait_ge(hi_ready, t + 1)
                    pool.tensor_tensor(qks[:, t % 2, 0, :, 2 * DQ:KS], cat[:, t % 2, 0], qks[:, t % 2, 0, :, 0:DQ].bitcast(F32),
                                       ALU.subtract).then_inc(lo_ready, 1)
                    pool.tensor_tensor(qks[:, t % 2, 1, :, DQ:2 * DQ], cat[:, t % 2, 1], qks[:, t % 2, 1, :, 0:DQ].bitcast(F32),
                                       ALU.subtract).then_inc(lo_ready, 1)
                split_weights(k)

            def square(u, raw):
                pool.wait_ge(raw_ready, u + 1)
                if u >= 2:
                    pool.wait_ge(ss_ready, u - 1)
                pool.tensor_tensor(sq[:, u % 2, :], raw, raw, ALU.mult).then_inc(sq_ready, 1)

            def normalise_keys(g):
                v = kraw[:, :, g * HD:(g + 1) * HD]
                r = rK[:].rearrange("p (k g) -> p k g", g=KV)[:, :, g:g + 1]
                pool.tensor_tensor(v, v, r.to_broadcast([P, KT_, HD]), ALU.mult).then_inc(k_normed, 1)

            for i in range(len(wo_chunks)):
                pool.wait_ge(wo_high, i + 1)
                high, low = [w[:, 2 * i:2 * i + 2, :].rearrange("p h n -> p (h n)") for w in WoS]
                pool.tensor_tensor(low, wraw2[:, i % 2, :], high.bitcast(F32), ALU.subtract).then_inc(wo_split, 1)

            for s in range(FIRST, LAST):
                for kind, *a in products_of(s) + other_work(s):
                    if kind == "KP":
                        square(norm_unit[("K", *a)], kraw[:, a[1], :])
                    if kind == "QP":
                        square(norm_unit[("Q", *a)], qraw[:, a[1], :])
                    if kind == "NW":
                        pool.wait_ge(rk_ready, norm_chain[tuple(a)] + 1)
                        if a[0] == "K":
                            normalise_keys(0)
                        else:
                            v = qraw[:].rearrange("p k (g d) -> p (k g) d", d=HD)
                            pool.tensor_tensor(v, v, rQ[:].unsqueeze(2).to_broadcast([P, 4 * TB, HD]), ALU.mult).then_inc(q_normed, 1)
                            if a[1] % KV == 0:
                                for g in range(1, KV):
                                    normalise_keys(g)
                    if kind == "VS":
                        n, = a
                        pool.wait_ge(v_ready, 4 * (n // 4 + 1))
                        if n >= 2:
                            pool.wait_ge(pv_ps, 4 * (n - 1))
                        src = vraw[:, :, (n % 4) * HD:(n % 4 + 1) * HD]
                        link(pool.tensor_copy(vS[0][:, n % 2], src))
                        pool.tensor_tensor(vS[1][:, n % 2], src, vS[0][:, n % 2].bitcast(F32), ALU.subtract).then_inc(v_split, 1)

            pool.wait_ge(zeroed, 16)
            pool.wait_ge(xn3_ready, NT)
            pool.wait_ge(slots_ready, 1)
            for t in range(NT):
                for k in range(2):
                    pool.indirect_dma_start(out=xg_dram, out_offset=bass.IndirectOffsetOnAxis(sloti[:, k, t:t + 1], axis=0),
                                            in_=xn3[:, t, :], in_offset=None).then_inc(scattered, 16)
            for par in range(2):
                pool.wait_ge(y_st[par], 16 * (NSLOT // 2))
            for t in range(NT):
                for k in range(2):
                    pool.indirect_dma_start(out=yg[k][:, t, :], out_offset=None, in_=yg_dram,
                                            in_offset=bass.IndirectOffsetOnAxis(sloti[:, k, t:t + 1], axis=0)
                                            ).then_inc(gathered[t], 16)

        @block.scalar
        def _(act):
            n_self = 0

            def link(ins):
                nonlocal n_self
                n_self += 1
                ins.then_inc(act_self, 1)
                act.wait_ge(act_self, n_self)

            def rsqrt_guess(n, ready, at, done):
                act.wait_ge(ready, at)
                link(nc.scalar.activation(lnv[:, 0:n], ve[:, 0:n], ACT.Ln))
                nc.scalar.activation(r0[:, 0:n], lnv[:, 0:n], ACT.Exp, scale=-0.5).then_inc(done, 1)

            act.preload_act_table_set("natural_log_exp_and_others")
            rsqrt_guess(TB, var_ready, 1, r0_ready)
            act.dma_start(w2kv[:, 0:D], W_UK).then_inc(ld_small, 16)
            act.dma_start(w2kv[:, D:2 * D], W_UV).then_inc(ld_small, 16)
            act.dma_start(w2q[DC:P, 0:D], W_UQ).then_inc(ld_small, 16)
            act.dma_start(w2q[DC:P, D:D + DC], W_QR).then_inc(ld_small, 16)
            for off, v, n in ((0, b_UK, D), (D, b_UV, D), (2 * D, b_UQ, D), (3 * D, b_QR, DC)):
                act.dma_start(b2[:, off:off + n], v.rearrange("(a n) -> a n", a=1).to_broadcast([P, n])).then_inc(ld_small, 16)
            act.dma_start(cs[:], rope_cs).then_inc(ld_small, 16)
            for k in stage_slots():
                t = k - 2
                if 0 <= t < NT:
                    act.wait_ge(cT_ps, t + 1)
                    if t >= 2:
                        act.wait_ge(kvq_ps, t - 1)
                    act.copy(cT[:, t % 2, :], ps[0][:, D:D + P]).then_inc(cT_ready, 1)
                t = k
                if 0 <= t < NT:
                    act.wait_ge(xnT_ps, t + 1)
                    if t >= 2:
                        act.wait_ge(c_ps, t - 1)
                    act.copy(xnT[:, t % 2].rearrange("p c n -> p (c n)"), ps[0][:, 0:D]).then_inc(xnT_ready, 1)
                t = k - 3
                if 0 <= t < NT:
                    act.wait_ge(cat_ready, t + 1)
                    if t >= 2:
                        act.wait_ge(qk_ps, 4 * (t - 1))
                    src = cat[:, t % 2].rearrange("p a h d -> p (a h) d")
                    dst = qks[:, t % 2].rearrange("p a h d -> p (a h) d")
                    act.copy(dst[:, :, 0:DQ], src)
                    act.copy(dst[:, 0:NH, DQ:2 * DQ], src[:, 0:NH, :])
                    act.copy(dst[:, NH:2 * NH, 2 * DQ:KS], src[:, NH:2 * NH, :]).then_inc(hi_ready, 1)
                t = k - 4
                if 0 <= t < NT:
                    for g in range(2):
                        act.wait_ge(qk_ps, 4 * t + g + 1)
                        act.copy(qkT[:, 0, 4 * g:4 * g + 4, t * P:(t + 1) * P],
                                 ps[TURN_BANKS[g]][:].rearrange("p (a n) -> p a n", a=4)).then_inc(qkA, 1)
                off, _ = chunks[k]
                act.wait_ge(ld_w[k % 2], 16 * (k // 2 + 1))
                act.copy(Wkvq[0][:, off:off + 512], wraw[:, k % 2, :]).then_inc(w_high, 1)

                if k % TB == 0 and k // TB + 1 < LN1_SETS:
                    rsqrt_guess(TB, var_ready, k // TB + 2, r0_ready)

            for u in range(UNITS + P2_LAG + PV_LAG + 2):
                i = (u - P2_LAG) // 4
                if u % 4 == 0 and 0 <= i < len(wo_chunks):
                    if 1 <= i < len(wo_chunks) - 1:
                        act.wait_ge(wo_split, i)
                        act.dma_start(wraw2[:, (i + 1) % 2, :].rearrange("p (h n) -> p h n", h=2),
                                      wo_chunks[i + 1]).then_inc(ld_wo[(i + 1) % 2], 16)
                    act.wait_ge(ld_wo[i % 2], 16 * (i // 2 + 1))
                    act.copy(WoS[0][:, 2 * i:2 * i + 2, :].rearrange("p h n -> p (h n)"),
                             wraw2[:, i % 2, :]).then_inc(wo_high, 1)
                b = (u - M_LAG + 1) // NH
                if u >= M_LAG - 1 and (u - M_LAG + 1) % NH == 0 and b < B:
                    act.wait_ge(s1_max, NH * (b + 1))
                    if b:
                        act.wait_ge(mT_ps, b)
                    act.copy(msp[:, :, :, 0, :], mneg[:, b % 2].rearrange("p q (a j) -> p q j a", j=2)).then_inc(m_hi, 1)
                    act.wait_ge(mT_ps, b + 1)
                    if b >= 2:
                        act.wait_ge(mrow, 64 * (b - 1))
                    act.copy(mT[:, b % 2, :], ps[(17 * b + 16) % 2][0:32, 0:T]).then_inc(mT_ready, 1)
                v = u - P2_LAG
                if 0 <= v < UNITS:
                    act.wait_ge(sT_ps, v + 1)
                    if v >= 3:
                        act.wait_ge(o_ps, v - 2)
                    nc.scalar.activation(pTs[:, v % 3].rearrange("p k t -> p (k t)"), ps[2 + v % 2][:], ACT.Exp,
                                         scale=SA_SCALE).then_inc(pTs_ready, 1)
                v = u - P2_LAG - PV_LAG - 1
                if v >= 0 and v % 8 == 7:
                    g = v // 8
                    act.wait_ge(o_ps, v + 1)
                    if g >= 2:
                        act.wait_ge(o_rows, g - 1)
                    act.copy(oTs[:, g % 2, :], ps[4 + g % 2][:]).then_inc(oTs_ready, 1)

            for s in range(FIRST, LAST):
                if s >= 5 and s % 2 == 1 and (s - 5) // 2 < B * XH:
                    h = (s - 5) // 2
                    act.wait_ge(pv_ps, h + 1)
                    if h >= 1:
                        act.wait_ge(wo_ps, h)
                    act.copy(oT[0][:], ps[4][:, 0:T]).then_inc(o_hi, 1)
                for task in products_of(s):
                    kind, *a = task
                    if kind in EVACUATED:
                        act.wait_ge(m_ps, side[task] + 1)
                        bank = side_bank(task)
                    if kind == "CT":
                        b, c = a
                        if b:
                            act.wait_ge(m_ps, side[("VP", b - 1, KT_ - 1)] + 1)
                        act.copy(ctxT[0][:, c, :], bank[:]).then_inc(ctx_hi, 1)
                    if kind == "X3":
                        b, = a
                        act.copy(xn3T[:, :, b * T:(b + 1) * T], bank[:].rearrange("p (c n) -> p c n", c=C)).then_inc(x3_T, 1)
                    if kind == "XT":
                        b, = a
                        if b:
                            act.wait_ge(m_ps, side[("QP", 4 * b - 1, 1)] + 1)
                        act.copy(xT[0][:].rearrange("p c n -> p (c n)"), bank[:]).then_inc(xT_hi, 1)
                    if kind == "KP":
                        b, kt = a
                        if b:
                            act.wait_ge(m_ps, side[("KT", 4 * b - 1)] + 1)
                        act.copy(kraw[:, kt, :], bank[:]).then_inc(raw_ready, 1)
                    if kind == "QP":
                        n, qt = a
                        if n:
                            act.wait_ge(m_ps, side[("QT", n - 1, qt)] + 1)
                        act.copy(qraw[:, qt, :], bank[:]).then_inc(raw_ready, 1)
                    if kind == "VP":
                        b, kt = a
                        if b:
                            act.wait_ge(v_split, 4 * b)
                        act.copy(vraw[:, kt, :], bank[:]).then_inc(v_ready, 1)
                    if kind == "KT":
                        n, = a
                        if n >= 2:
                            act.wait_ge(S_ps, 8 * (n - 1))
                        nc.scalar.activation(kT[0][:, n % 2, :], bank[:], ACT.Copy, scale=wqk[:, 0:1]).then_inc(kT_hi, 1)
                    if kind == "QT":
                        n, qt = a
                        if n >= 2:
                            act.wait_ge(S_ps, 8 * (n - 1))
                        act.copy(qT[0][:, n % 2, qt, :], bank[:]).then_inc(qT_hi, 1)
                if 0 <= s - 2 < 8 * B * KV:
                    i = s - 2
                    act.wait_ge(pT_ps, i + 1)
                    if i // 2 >= 2:
                        act.wait_ge(pv_ps, i // 2 - 1)
                    act.copy(pT[0][:, (i // 2) % 2, :, (i % 2) * P:(i % 2 + 1) * P],
                             ps[2 + i % 2][:].rearrange("p (k n) -> p k n", k=KT_)).then_inc(pT_hi, 1)
                if 0 <= s < 8 * B * KV:
                    act.wait_ge(S_masked, s + 1)
                    nc.scalar.activation(pb[:, s % 3, :], pb[:, s % 3, :], ACT.Exp, bias=nmax[:, s % 3:s % 3 + 1], scale=-1.0,
                                         accum_out=psm[:, s % 3:s % 3 + 1]).then_inc(exp_done, 1)
                if 0 <= s - 1 < 8 * B * KV and (s - 1) % 2 == 0:
                    i = s - 1
                    act.wait_ge(rinv_ready, i + 1)
                    nc.scalar.activation(pb[:, i % 3, :], pb[:, i % 3, :], ACT.Copy, scale=rinv[:, i % 3:i % 3 + 1]).then_inc(p_normed[0], 1)
                for kind, *a in other_work(s - 1):
                    if kind in ("LNV", "L3V"):
                        rsqrt_guess(TB, var_ready, ln_set[(kind[:2], a[0])], r0_ready)
                for kind, *a in other_work(s):
                    if kind == "VE":
                        n = norm_chain[tuple(a)]
                        rsqrt_guess(16 if a[0] == "K" else 8, rk_var, n + 1, rk_r0)

            rsqrt_guess(TB, var_ready, LN_SETS, r0_ready)
            act.wait_ge(x3_ps, 1)
            act.copy(xn3T[:, :, (B - 1) * T:B * T], ps[0][:].rearrange("p (c n) -> p c n", c=C)).then_inc(x3_T, 1)
            act.wait_ge(lgm_ready, 1)
            nc.scalar.activation(lge[:], lg[:], ACT.Exp).then_inc(lge_ready, 1)

            def silu(i, par):
                act.wait_ge(up_ps, i + 1)
                nc.scalar.activation(sg[:, par, :], ps[2 + par][:, 0:INTER], ACT.Silu).then_inc(sg_ready, 1)

            def turn_rows(j, par):
                act.wait_ge(xg_ps, j + 1)
                act.copy(xgT[:, par].rearrange("p c n -> p (c n)"), ps[par][:, 0:D]).then_inc(xgT_ready, 1)

            for i in range(LEAD):
                if i >= 2:
                    act.wait_ge(hh_ready, i - 1)
                silu(i, i % 2)
            turn_rows(0, 0)
            act.wait_ge(hh_ready, LEAD - 1)
            silu(LEAD, 0)
            turn_rows(1, 1)
            with act.Fori(0, NSLOT // 2 - 1) as k:
                for par in range(2):
                    j = 2 * k + par + 1
                    act.wait_ge(hh_ready, j + (LEAD - 1))
                    silu(j + LEAD, 1 - par)
                    turn_rows(j + 1, par)
            act.wait_ge(hh_ready, LEAD + NSLOT - 2)
            silu(LEAD + NSLOT - 1, 1)
            for i in range(LEAD + NSLOT, NT + NSLOT):
                act.wait_ge(hh_ready, i - 1)
                silu(i, i % 2)

        @block.vector
        def _(dve):
            n_self = 0

            def link(ins):
                nonlocal n_self
                n_self += 1
                ins.then_inc(dve_self, 1)
                dve.wait_ge(dve_self, n_self)

            def polish(n, ready, at, r, done):
                dve.wait_ge(ready, at)
                link(dve.tensor_tensor(nwt[:, 0:n], r0[:, 0:n], r0[:, 0:n], ALU.mult))
                link(dve.tensor_tensor(nwt[:, 0:n], nwt[:, 0:n], ve[:, 0:n], ALU.mult))
                link(dve.tensor_scalar(nwt[:, 0:n], nwt[:, 0:n], -0.5, 1.5, ALU.mult, ALU.add))
                dve.tensor_tensor(r, r0[:, 0:n], nwt[:, 0:n], ALU.mult).then_inc(done, 1)

            def row_stats(tiles):
                for i, t in enumerate(tiles):
                    link(dve.bn_stats(stats[:, t % 2, :], xs[:, t, :]))
                    link(dve.bn_aggr(mv[:, t, :], stats[:, t % 2, :]))
                dve.tensor_scalar(ve[:, 0:len(tiles)], mv[:, tiles[0]:tiles[-1] + 1, 1], LN_EPS, None, ALU.add).then_inc(var_ready, 1)

            def mixture_rows(tiles):
                for t in tiles:
                    dve.tensor_scalar(xn3[:, t, :], xs[:, t, :], mv[:, t, 0:1], rln[:, t:t + 1], ALU.subtract,
                                      ALU.mult).then_inc(xn3_ready, 1)

            dve.wait_ge(ld_x[0], 16)
            row_stats(range(TB))
            polish(TB, r0_ready, 1, rln[:, 0:TB], rln_ready)
            for k in stage_slots():
                t = k
                if 0 <= t < NT:
                    dve.wait_ge(rln_ready, t // TB + 1)
                    if t >= 2:
                        dve.wait_ge(xnT_ps, t - 1)
                    dve.tensor_scalar(xn[:, t % 2, :], xs[:, t, :], mv[:, t, 0:1], rln[:, t:t + 1], ALU.subtract,
                                      ALU.mult).then_inc(xn_ready, 1)
                t = k - 3
                if 0 <= t < NT:
                    dve.wait_ge(kvq_ps, t + 1)
                    if t >= 2:
                        dve.wait_ge(lo_ready, 2 * (t - 1))
                        dve.wait_ge(hi_ready, t - 1)

                    def heads(a):
                        return a.rearrange("p (h d) -> p h d", h=NH)
                    dve.tensor_tensor(cat[:, t % 2, 1, :, 0:DH], heads(ps[3][:, 0:D]), heads(b2[:, 0:D]), ALU.add)
                    if t == 0:
                        dve.wait_ge(consts, 4)
                        dve.wait_ge(ld_small, 16 * 9)
                    dve.tensor_tensor(va[:, t, :, 0:DH], heads(ps[3][:, D:2 * D]), heads(b2[:, D:2 * D]), ALU.add)
                    dve.tensor_tensor(cat[:, t % 2, 0, :, 0:DH], heads(ps[4][:, 0:D]), heads(b2[:, 2 * D:3 * D]), ALU.add)
                    dve.tensor_tensor(rr[:, t % 3, 0, :], ps[4][:, D:D + DC], b2[:, 3 * D:3 * D + DC],
                                      ALU.add).then_inc(kvq_read, 1)
                    dve.wait_ge(kvq_read, t + 1)
                    dve.wait_ge(c_ready, t + 1)
                    rin = rr[:, t % 3].rearrange("p a (h d) -> p (a h) d", d=DR)
                    cos4 = cs[:, t % TB, 0:1, :].to_broadcast([P, 2 * NH, DR])
                    sin4 = cs[:, t % TB, 1:2, :].to_broadcast([P, 2 * NH, DR])
                    dve.tensor_tensor(rp1[:], rin, cos4, ALU.mult)
                    link(dve.tensor_tensor(rp2[:], rin, sin4, ALU.mult))
                    co = cat[:, t % 2].rearrange("p a h d -> p (a h) d")
                    dve.tensor_tensor(co[:, :, DH:DH + 2], rp1[:, :, 0:DR:2], rp1[:, :, 1:DR:2], ALU.subtract)
                    dve.tensor_tensor(co[:, :, DH + 2:DQ], rp2[:, :, 0:DR:2], rp2[:, :, 1:DR:2], ALU.add).then_inc(cat_ready, 1)
                t = k - 1
                if 0 <= t < NT:
                    if t == 0:
                        dve.wait_ge(ld_down, 16 * 6)
                    dve.wait_ge(c_ps, t + 1)
                    if t >= 2:
                        dve.wait_ge(cT_ps, t - 1)
                    dve.tensor_tensor(rr[:, t % 3, 1, :], ps[1][:, 128:192], b1[:, 128:192], ALU.add)
                    dve.tensor_tensor(c1[:, t % 2, :], ps[1][:, 0:128], b1[:, 0:128], ALU.add).then_inc(c_ready, 1)
                t = k - 4
                if 0 <= t < NT:
                    for g in range(2, 4):
                        dve.wait_ge(qk_ps, 4 * t + g + 1)
                        dve.tensor_copy(qkT[:, 1, 4 * (g - 2):4 * (g - 2) + 4, t * P:(t + 1) * P],
                                        ps[TURN_BANKS[g]][:].rearrange("p (a n) -> p a n", a=4)).then_inc(qkD, 1)

                if k % TB == 0 and k // TB + 1 < LN1_SETS:
                    if k == 0:
                        dve.wait_ge(ld_x[1], 16)
                    first = k + TB
                    row_stats(range(first, first + TB))
                    polish(TB, r0_ready, k // TB + 2, rln[:, first:first + TB], rln_ready)

            for u in range(UNITS + P2_LAG + PV_LAG + TURN_LAG + 1):
                if u < UNITS:
                    b, h = u // NH, u % NH
                    dve.wait_ge(s1_ps, u + 1)
                    if h == 0 and b >= 2:
                        dve.wait_ge(m_lo, b - 1)
                    dve.tensor_reduce(mneg[:, b % 2, :, h:h + 1], ps[(17 * b + h) % 2][:].rearrange("p (q k) -> p q k", q=TB),
                                      X, ALU.max, negate=True).then_inc(s1_max, 1)
                b = (u - M_LAG + 1) // NH
                if u >= M_LAG - 1 and (u - M_LAG + 1) % NH == 0 and b < B:
                    dve.wait_ge(m_hi, b + 1)
                    dve.tensor_tensor(msp[:, :, :, 1, :], mneg[:, b % 2].rearrange("p q (a j) -> p q j a", j=2),
                                      msp[:, :, :, 0, :].bitcast(F32), ALU.subtract).then_inc(m_lo, 1)
                v = u - P2_LAG - PV_LAG - TURN_LAG - 1
                if v >= 0 and v % NH == NH - 1:
                    b = v // NH
                    dve.wait_ge(o_rows, 2 * (b + 1))
                    for q in range(TB):
                        o = ps[6 + q][:].rearrange("p (h d) -> p h d", h=NH)
                        link(dve.reciprocal(rsv[:, q, :].unsqueeze(2), o[:, :, DH:DH + 1]))
                        link(dve.tensor_tensor(osa[:, q], o[:, :, 0:DH], rsv[:, q, :].unsqueeze(2).to_broadcast([P, NH, DH]), ALU.mult))
                    dve.tensor_tensor(xs[:, TB * b:TB * b + TB, :], xs[:, TB * b:TB * b + TB, :],
                                      osa[:].rearrange("p q h d -> p q (h d)"), ALU.add).then_inc(x1_ready, 1)

            dve.wait_ge(x1_ready, B)
            dve.wait_ge(w_split, len(chunks))
            dve.wait_ge(bias_placed, 16 * 12)
            for s in range(FIRST, LAST):
                if s >= 5 and s % 2 == 1 and (s - 5) // 2 < B * XH:
                    h = (s - 5) // 2
                    dve.wait_ge(o_hi, h + 1)
                    dve.tensor_tensor(oT[1][:], ps[4][:, 0:T], oT[0][:].bitcast(F32), ALU.subtract).then_inc(o_lo, 1)
                if 0 <= s < 8 * B * KV:
                    dve.wait_ge(S_ps, s + 1)
                    if s == 0:
                        dve.wait_ge(ld_mask, 16)
                    if s >= 3:
                        dve.wait_ge(pT_ps, s - 2)
                    dve.tensor_tensor_reduce(pb[:, s % 3, :], ps[s % 2][:], msk[:, s % 2, :], -1.0, 3.0e38, ALU.add, ALU.min,
                                             nmax[:, s % 3:s % 3 + 1]).then_inc(S_masked, 1)
                for task in products_of(s):
                    kind, *a = task
                    if task in side:
                        bank = side_bank(task)
                    if kind == "CT":
                        b, c = a
                        dve.wait_ge(ctx_hi, 2 * b + c + 1)
                        dve.tensor_tensor(ctxT[1][:, c, :], bank[:], ctxT[0][:, c, :].bitcast(F32), ALU.subtract).then_inc(ctx_lo, 1)
                    if kind == "XT":
                        b, = a
                        dve.wait_ge(xT_hi, b + 1)
                        dve.tensor_tensor(xT[1][:].rearrange("p c n -> p (c n)"), bank[:],
                                          xT[0][:].rearrange("p c n -> p (c n)").bitcast(F32), ALU.subtract).then_inc(xT_lo, 1)
                    if kind == "KT":
                        n, = a
                        dve.wait_ge(kT_hi, n + 1)
                        dve.scalar_tensor_tensor(kT[1][:, n % 2, :], bank[:], wqk[:, 0:1], kT[0][:, n % 2, :].bitcast(F32),
                                                 ALU.mult, ALU.subtract).then_inc(kT_lo, 1)
                    if kind == "QT":
                        n, qt = a
                        dve.wait_ge(qT_hi, 2 * n + qt + 1)
                        dve.tensor_tensor(qT[1][:, n % 2, qt, :], bank[:], qT[0][:, n % 2, qt, :].bitcast(F32),
                                          ALU.subtract).then_inc(qT_lo, 1)
                if 0 <= s - 1 < 8 * B * KV:
                    i = s - 1
                    dve.wait_ge(exp_done, i + 1)
                    dve.reciprocal(rinv[:, i % 3:i % 3 + 1], psm[:, i % 3:i % 3 + 1]).then_inc(rinv_ready, 1)
                    if i % 2 == 1:
                        dve.wait_ge(rinv_ready, i + 1)
                        dve.tensor_scalar(pb[:, i % 3, :], pb[:, i % 3, :], rinv[:, i % 3:i % 3 + 1], None,
                                          ALU.mult).then_inc(p_normed[1], 1)
                if 0 <= s - 2 < 8 * B * KV:
                    i = s - 2
                    dve.wait_ge(pT_hi, i + 1)
                    cols = slice((i % 2) * P, (i % 2 + 1) * P)
                    dve.tensor_tensor(pT[1][:, (i // 2) % 2, :, cols], ps[2 + i % 2][:].rearrange("p (k n) -> p k n", k=KT_),
                                      pT[0][:, (i // 2) % 2, :, cols].bitcast(F32), ALU.subtract).then_inc(pT_lo, 1)
                if s >= 6 and s % 2 == 0 and (s - 6) // 2 < B * XH and ((s - 6) // 2) % XH == XH - 1:
                    h = (s - 6) // 2
                    b = h // XH
                    dve.wait_ge(wo_ps, h + 1)
                    dve.tensor_tensor(xs[:, TB * b:TB * b + TB, :], ps[5][:].rearrange("p (q d) -> p q d", q=TB),
                                      xs[:, TB * b:TB * b + TB, :], ALU.add).then_inc(x2_ready, 1)
                for kind, *a in other_work(s):
                    if kind in ("LNV", "L3V"):
                        row_stats(range(TB * a[0], TB * a[0] + TB))
                    if kind == "L3W":
                        b, = a
                        polish(TB, r0_ready, ln_set[("L3", b)], rln[:, TB * b:TB * b + TB], rln_ready)
                        dve.wait_ge(rln_ready, ln_set[("L3", b)])
                        dve.wait_ge(m_ps, side[("VP", B - 1, KT_ - 1)] + 1)
                        mixture_rows(range(TB * b, TB * b + TB))
                    if kind == "LNW":
                        b, = a
                        polish(TB, r0_ready, ln_set[("LN", b)], rln[:, TB * b:TB * b + TB], rln_ready)
                        dve.wait_ge(rln_ready, ln_set[("LN", b)])
                        if b:
                            dve.wait_ge(m_ps, side[("XT", b - 1)] + 1)
                        for q in range(TB):
                            t = TB * b + q
                            dve.tensor_scalar(xnD[:, q, :], xs[:, t, :], mv[:, t, 0:1], rln[:, t:t + 1], ALU.subtract,
                                              ALU.mult).then_inc(xnD_ready, 1)
                    if kind == "SS":
                        which, i, t = a
                        u = norm_unit[(which, i, t)]
                        dve.wait_ge(sq_ready, u + 1)
                        to = (ssK if which == "K" else ssQ)[:, 4 * t:4 * t + 4]
                        dve.tensor_reduce(to, sq[:, u % 2, :].rearrange("p (g d) -> p g d", g=4), X, ALU.add).then_inc(ss_ready, 1)
                    if kind == "VE":
                        which, i = a
                        ss, n = (ssK, 16) if which == "K" else (ssQ, 8)
                        u = norm_unit[(which, i, n // 4 - 1)]
                        dve.wait_ge(ss_ready, u + 1)
                        dve.tensor_scalar(ve[:, 0:n], ss[:], 1.0 / HD, RMS_EPS, ALU.mult, ALU.add).then_inc(rk_var, 1)
                    if kind == "NW":
                        n = norm_chain[tuple(a)]
                        r = rK if a[0] == "K" else rQ
                        polish(16 if a[0] == "K" else 8, rk_r0, n + 1, r[:], rk_ready)

            dve.wait_ge(x2_ready, B)
            row_stats(range(NT - TB, NT))
            polish(TB, r0_ready, LN_SETS, rln[:, NT - TB:NT], rln_ready)
            dve.wait_ge(rln_ready, LN_SETS)
            mixture_rows(range(NT - TB, NT))

            def by_row(a):
                return a.unsqueeze(2).to_broadcast([P, NT, EW])
            experts = iota_e[:].unsqueeze(1).to_broadcast([P, NT, EW])

            def pick(k):
                link(dve.tensor_reduce(top[k][:], lg[:], X, ALU.max))
                link(dve.tensor_tensor(eq[:], lg[:], by_row(top[k][:]), ALU.is_equal))
                link(dve.scalar_tensor_tensor(eq[:], eq[:], -float(EW), experts, ALU.mult, ALU.add))
                link(dve.tensor_reduce(first_e[:], eq[:], X, ALU.min))
                link(dve.tensor_tensor(oh[k][:], eq[:], by_row(first_e[:]), ALU.is_equal))

            dve.wait_ge(consts, 8)
            for a in running:
                dve.memset(a[:, 0:NT // 2, :], 0.0)
            link(dve.memset(lg[:, :, NE:EW], FINITE_LOW))
            dve.wait_ge(gate_ps, 1)
            link(dve.tensor_copy(lg[:, :, 0:NE], ps[7][:, 0:NT * EW].rearrange("p (t e) -> p t e", t=NT)[:, :, 0:NE]))
            pick(0)
            dve.tensor_tensor(lg[:], lg[:], by_row(top[0][:]), ALU.subtract).then_inc(lgm_ready, 1)
            dve.wait_ge(lge_ready, 1)
            link(dve.scalar_tensor_tensor(lg[:], oh[0][:], FINITE_LOW, lg[:], ALU.mult, ALU.add))
            pick(1)
            dve.tensor_tensor(chosen[:], oh[0][:], oh[1][:], ALU.add).then_inc(chosen_ready, 1)
            link(dve.tensor_reduce(top[0][:], lge[:], X, ALU.add))
            link(dve.reciprocal(cw[0][:], top[0][:]))
            link(dve.tensor_tensor(lge[:], lge[:], oh[1][:], ALU.mult))
            link(dve.tensor_reduce(top[1][:], lge[:], X, ALU.add))
            link(dve.tensor_tensor(cw[1][:], top[1][:], cw[0][:], ALU.mult))

            dve.wait_ge(rank_ps, 1)
            per_tile = ps[0][:, P:2 * P].rearrange("p (t e) -> p t e", t=NT)
            zeros_ahead = NT // 2
            link(dve.tensor_copy(running[0][:, zeros_ahead:, :], per_tile))
            shift, at = 1, 0
            while shift < NT:
                a = running[at]
                link(dve.tensor_tensor(running[1 - at][:, zeros_ahead:, :], a[:, zeros_ahead:, :],
                                       a[:, zeros_ahead - shift:zeros_ahead - shift + NT, :], ALU.add))
                shift, at = 2 * shift, 1 - at
            before = running[at][:, zeros_ahead - 1:zeros_ahead - 1 + NT, :]
            count = running[at][:, zeros_ahead + NT - 1, :].unsqueeze(2).to_broadcast([P, EW, NT])
            link(dve.tensor_tensor(more[:], count, iota_t[:].unsqueeze(1).to_broadcast([P, EW, NT]), ALU.is_gt))
            link(dve.tensor_reduce(ntile[:], more[:], X, ALU.add))
            link(dve.tensor_tensor_scan(tend[:], onesf[:, 0:EW], ntile[:], 0.0, ALU.mult, ALU.add))
            link(dve.tensor_tensor(ntile[:], tend[:], ntile[:], ALU.subtract))
            rank = ps[0][:, 0:P].rearrange("p (t e) -> p t e", t=NT)
            link(dve.tensor_tensor(pos[:], rank, before, ALU.add))
            link(dve.scalar_tensor_tensor(pos[:], ntile[:].unsqueeze(1).to_broadcast([P, NT, EW]), float(P), pos[:],
                                          ALU.mult, ALU.add))
            for k in range(2):
                link(dve.tensor_tensor(eq[:], oh[k][:], pos[:], ALU.mult))
                link(dve.tensor_reduce(slotf[:, k, :], eq[:], X, ALU.add))
            dve.tensor_copy(sloti[:], slotf[:]).then_inc(slots_ready, 1)

            def product(i, par):
                dve.wait_ge(sg_ready, i + 1)
                dve.tensor_tensor(hh[:, par, :], ps[2 + par][:, INTER:2 * INTER], sg[:, par, :], ALU.mult).then_inc(hh_ready, 1)

            def turn_hidden(i, par):
                dve.wait_ge(h_ps, i + 1)
                dve.tensor_copy(hT[:, par].rearrange("p c n -> p (c n)"), ps[4 + par][0:IH, 0:2 * P]).then_inc(hT_ready, 1)

            def add_shared(i, t):
                dve.wait_ge(y_ps, i + 1)
                dve.tensor_tensor(xs[:, t, :], ps[6 + i % 2][:, 0:D], xs[:, t, :], ALU.add).then_inc(y_read, 1)

            def keep_result(j, par, stored):
                if stored is not None:
                    dve.wait_ge(y_st[par], stored)
                dve.wait_ge(y_ps, j + LEAD + 1)
                dve.tensor_copy(ys[:, par, :], ps[6 + par][:, 0:D]).then_inc(y_read, 1)

            for i in range(LEAD + 1):
                if i >= 2:
                    dve.wait_ge(h_ps, i - 1)
                product(i, i % 2)
                if i >= 1:
                    add_shared(i - 1, i - 1)
                turn_hidden(i, i % 2)
                if i == 1:
                    link(dve.tensor_tensor(isof[:], iota_j[:].unsqueeze(2).to_broadcast([P, 32, EW]),
                                           tend[:].unsqueeze(1).to_broadcast([P, 32, EW]), ALU.is_ge))
                    link(dve.tensor_reduce(expf[:], isof[:], X, ALU.add))
                    link(dve.tensor_scalar(expf[:], expf[:], float(NE - 1), None, ALU.min))
                    link(dve.tensor_copy(packf[:], expf[:, 0:32:XG]))
                    for i in range(1, XG + 2):
                        these = expf[:, i:32:XG]
                        words = packf[:, 0:these.shape[1]]
                        link(dve.scalar_tensor_tensor(words, these, float(EW ** i), words, ALU.mult, ALU.add))
                    dve.tensor_copy(expi[:], packf[:]).then_inc(slots_ready, 1)

            def two_tiles(k, stored):
                for par in range(2):
                    j = 2 * k + par + 1
                    dve.wait_ge(h_ps, j + (LEAD - 1))
                    product(j + LEAD, 1 - par)
                    keep_result(j - 1, par, stored)
                    turn_hidden(j + LEAD, 1 - par)

            two_tiles(0, None)
            with dve.Fori(1, NSLOT // 2 - 1) as k:
                two_tiles(k, 16 * k)
            last = NSLOT - 1
            dve.wait_ge(h_ps, last + LEAD - 1)
            product(last + LEAD, 1)
            keep_result(last - 1, 0, 16 * (last // 2))
            turn_hidden(last + LEAD, 1)
            for i in range(LEAD + NSLOT, NT + NSLOT):
                dve.wait_ge(h_ps, i - 1)
                product(i, i % 2)
                if i == LEAD + NSLOT:
                    keep_result(last, 1, 16 * (last // 2))
                else:
                    add_shared(i - 1, i - 1 - NSLOT)
                turn_hidden(i, i % 2)
            add_shared(NT + NSLOT - 1, NT - 1)
            dve.wait_ge(y_read, NT + NSLOT)
            for t in range(NT):
                dve.wait_ge(gathered[t], 32)
                link(dve.scalar_tensor_tensor(xs[:, t, :], yg[0][:, t, :], cw[0][:, t:t + 1], xs[:, t, :], ALU.mult, ALU.add))
                dve.scalar_tensor_tensor(xs[:, t, :], yg[1][:, t, :], cw[1][:, t:t + 1], xs[:, t, :], ALU.mult,
                                         ALU.add).then_inc(done, 1)

        @block.tensor
        def _(pe):
            def split_product(o, lhs, rhs, first, last):
                for i, (a, b) in enumerate(((0, 0), (0, 1), (1, 0))):
                    ins = pe.matmul(o, lhs[a], rhs[b], start=first and i == 0, stop=last and i == 2, skip_group_check=True)
                return ins

            def add_bias(bank, j):
                rows = slice(32 * (j % 4), 32 * (j % 4) + 2)
                return pe.matmul(bank[:], ones2[rows, :], bias_hl[rows, j // 4, :], start=False, stop=True, skip_group_check=True)

            pe.wait_ge(consts, 1)
            for k in stage_slots():
                t = k - 3
                if 0 <= t < NT:
                    pe.wait_ge(cT_ready, t + 1)
                    if t == 0:
                        pe.wait_ge(ld_small, 16 * 9)
                        pe.wait_ge(consts, 4)
                    if t:
                        pe.wait_ge(kvq_read, t)
                    pe.matmul(ps[3][:], cT[0:DC, t % 2, :], w2kv[:], start=True, stop=True)
                    pe.matmul(ps[4][:, 0:D + DC], cT[DC:P, t % 2, :], w2q[DC:P, :], start=True, stop=True).then_inc(kvq_ps, 1)
                t = k - 1
                if 0 <= t < NT:
                    pe.wait_ge(xnT_ready, t + 1)
                    if t == 0:
                        pe.wait_ge(ld_down, 16 * 6)
                    if t:
                        pe.wait_ge(c_ready, t)
                    for c in range(C):
                        ins = pe.matmul(ps[1][:, 0:192], xnT[:, t % 2, c, :], w1[:, c, :], start=c == 0, stop=c == C - 1)
                    ins.then_inc(c_ps, 1)
                t = k
                if 0 <= t < NT:
                    pe.wait_ge(xn_ready, t + 1)
                    if t:
                        pe.wait_ge(xnT_ready, t)
                    for c in range(C):
                        ins = pe.transpose(ps[0][:, c * P:(c + 1) * P], xn[:, t % 2, c * P:(c + 1) * P], ident[:])
                    ins.then_inc(xnT_ps, 1)
                t = k - 2
                if 0 <= t < NT:
                    pe.wait_ge(c_ready, t + 1)
                    if t:
                        pe.wait_ge(cT_ready, t)
                    pe.transpose(ps[0][:, D:D + P], c1[:, t % 2, :], ident[:]).then_inc(cT_ps, 1)
                t = k - 4
                if 0 <= t < NT:
                    pe.wait_ge(lo_ready, 2 * t + 2)
                    for g in range(4):
                        if t:
                            pe.wait_ge(qkA if g < 2 else qkD, 2 * (t - 1) + g % 2 + 1)
                        for i in range(4):
                            pair = 4 * (g % 2) + i
                            ins = pe.transpose(ps[TURN_BANKS[g]][:, i * P:(i + 1) * P],
                                               qks[:, t % 2, g // 2, 2 * pair:2 * pair + 2, :].rearrange("p h d -> p (h d)").bitcast(F32), ident[:])
                        ins.then_inc(qk_ps, 1)

            pe.wait_ge(qkA, 2 * NT)
            pe.wait_ge(qkD, 2 * NT)
            for u in range(UNITS + P2_LAG + PV_LAG + TURN_LAG):
                if u < UNITS:
                    b, h = u // NH, u % NH
                    unit = 17 * b + h
                    lo = HW * (h % 2)
                    if h == 1 and b:
                        pe.wait_ge(mT_ready, b)
                    elif u >= 2:
                        pe.wait_ge(s1_max, u if h == 0 else u - 1)
                    for q in range(TB):
                        t = TB * b + q
                        ins = pe.matmul(ps[unit % 2][:, q * T:(q + 1) * T], qkT[lo:lo + KS, 0, h // 2, t * P:(t + 1) * P],
                                        qkT[lo:lo + KS, 1, h // 2, b * T:(b + 1) * T], start=True, stop=True)
                    ins.then_inc(s1_ps, 1)
                b = (u - M_LAG + 1) // NH
                if u >= M_LAG - 1 and (u - M_LAG + 1) % NH == 0 and b < B:
                    pe.wait_ge(m_lo, b + 1)
                    for q in range(TB):
                        ins = pe.transpose(ps[(17 * b + 16) % 2][0:32, q * P:(q + 1) * P],
                                           msp[:, q].rearrange("p a b c -> p (a b c)").bitcast(F32), ident[:])
                    ins.then_inc(mT_ps, 1)
                v = u - P2_LAG
                if 0 <= v < UNITS:
                    b, h = v // NH, v % NH
                    lo = HW * (h % 2)
                    if h == 0:
                        pe.wait_ge(mrow, 64 * (b + 1))
                    if v >= 2:
                        pe.wait_ge(pTs_ready, v - 1)
                    for kc in range(TB):
                        t = TB * b + kc
                        ins = pe.matmul(ps[2 + v % 2][:, kc * T:(kc + 1) * T], qkT[lo:lo + KM, 1, h // 2, t * P:(t + 1) * P],
                                        qkT[lo:lo + KM, 0, h // 2, b * T:(b + 1) * T], start=True, stop=True)
                    ins.then_inc(sT_ps, 1)
                v = u - P2_LAG - PV_LAG
                if 0 <= v < UNITS:
                    b, h = v // NH, v % NH
                    pe.wait_ge(pTs_ready, v + 1)
                    if v % 8 == 0 and v >= 16:
                        pe.wait_ge(oTs_ready, v // 8 - 1)
                    row, col = VW * (v % 4), T * (v % 8 // 4)
                    for kc in range(TB):
                        ins = pe.matmul(ps[4 + v // 8 % 2][row:row + VW, col:col + T], va[:, TB * b + kc, h, :],
                                        pTs[:, v % 3, kc, :], start=kc == 0, stop=kc == TB - 1)
                    ins.then_inc(o_ps, 1)
                v -= TURN_LAG
                if v >= 0 and v % 8 == 7:
                    g = v // 8
                    pe.wait_ge(oTs_ready, g + 1)
                    if g % 2 == 0 and g:
                        pe.wait_ge(x1_ready, g // 2)
                    for q in range(TB):
                        for half in range(2):
                            col = (2 * (g % 2) + half) * P
                            ins = pe.transpose(ps[6 + q][:, col:col + P], oTs[:, g % 2, half * T + q * P:half * T + (q + 1) * P],
                                               ident[:])
                    ins.then_inc(o_rows, 1)

            def turn_mixture_rows(bank, b):
                pe.wait_ge(xn3_ready, TB * (b + 1))
                for c in range(C):
                    for q in range(TB):
                        ins = pe.transpose(bank[:, c * T + q * P:c * T + (q + 1) * P], xn3[:, TB * b + q, c * P:(c + 1) * P],
                                           ident[:])
                return ins

            pe.wait_ge(x1_ready, B)
            pe.wait_ge(w_split, len(chunks))
            pe.wait_ge(bias_placed, 16 * 12)
            STEPS = 8 * B * KV
            for s in range(FIRST, LAST):
                if 0 <= s < STEPS:
                    n, r, q = s // 8, (s % 8) // 2, s % 2
                    pe.wait_ge(kT_lo, n + 1)
                    pe.wait_ge(qT_lo, 2 * n + q + 1)
                    if s >= 2:
                        pe.wait_ge(S_masked, s - 1)
                    split_product(ps[s % 2][:], [z[:, n % 2, q, r * P:(r + 1) * P] for z in qT],
                                  [z[:, n % 2, :] for z in kT], True, True).then_inc(S_ps, 1)
                if 0 <= s - 2 < STEPS:
                    i = s - 2
                    pe.wait_ge(p_normed[i % 2], i // 2 + 1)
                    if i >= 2:
                        pe.wait_ge(pT_lo, i - 1)
                    for kt in range(KT_):
                        ins = pe.transpose(ps[2 + i % 2][:, kt * P:(kt + 1) * P], pb[:, i % 3, kt * P:(kt + 1) * P], ident[:])
                    ins.then_inc(pT_ps, 1)
                if s >= 4 and s % 2 == 0 and (s - 4) // 2 < B * XH:
                    h = (s - 4) // 2
                    n = h // GR
                    pe.wait_ge(pT_lo, 2 * h + 2)
                    pe.wait_ge(v_split, n + 1)
                    if h:
                        pe.wait_ge(o_lo, h)
                    for kt in range(KT_):
                        ins = split_product(ps[4][:, 0:T], [z[:, n % 2, kt, :] for z in vS], [z[:, h % 2, kt, :] for z in pT],
                                            kt == 0, kt == KT_ - 1)
                    ins.then_inc(pv_ps, 1)
                if s >= 5 and s % 2 == 1 and (s - 5) // 2 < B * XH:
                    h = (s - 5) // 2
                    b, hd = h // XH, h % XH
                    pe.wait_ge(o_lo, h + 1)
                    if hd == 0 and b:
                        pe.wait_ge(x2_ready, b)
                    if h == 0:
                        pe.wait_ge(wo_split, len(wo_chunks))
                    for q in range(TB):
                        ins = split_product(ps[5][:, q * D:(q + 1) * D], [z[:, q * P:(q + 1) * P] for z in oT],
                                            [z[:, hd, :] for z in WoS], hd == 0 and q == 0, hd == XH - 1)
                    ins.then_inc(wo_ps, 1)

                for task in tasks.get(s, ()):
                    kind, *a = task
                    if task not in side:
                        continue
                    m = side[task]
                    bank = side_bank(task)
                    if m >= 2:
                        pe.wait_ge(*released(side_order[m - 2]))
                    if kind == "CT":
                        b, c = a
                        pe.wait_ge(ld_ctx, 16 * (b + 1))
                        for kt in range(KT_):
                            ins = pe.transpose(bank[:, kt * P:(kt + 1) * P], craw[:, kt, c * P:(c + 1) * P], ident[:])
                    if kind == "XT":
                        b, = a
                        pe.wait_ge(xnD_ready, TB * (b + 1))
                        for c in range(C):
                            for q in range(TB):
                                ins = pe.transpose(bank[:, c * T + q * P:c * T + (q + 1) * P], xnD[:, q, c * P:(c + 1) * P], ident[:])
                    if kind == "X3":
                        ins = turn_mixture_rows(bank, *a)
                    if kind in ("KP", "VP"):
                        b, kt = a
                        pe.wait_ge(ctx_lo, 2 * (b + 1))
                        off, j = (OFF_K, 4) if kind == "KP" else (OFF_V, 5)
                        for c in range(C):
                            split_product(bank[:], [z[:, c, kt * P:(kt + 1) * P] for z in ctxT],
                                          [z[:, off + c * 512:off + (c + 1) * 512] for z in Wkvq], c == 0, False)
                        ins = add_bias(bank, j)
                    if kind == "QP":
                        n, qt = a
                        g = n % 4
                        pe.wait_ge(xT_lo, n // 4 + 1)
                        for c in range(C):
                            off = OFF_Q + c * 2048 + g * GW
                            split_product(bank[:], [z[:, c, qt * P:(qt + 1) * P] for z in xT],
                                          [z[:, off:off + GW] for z in Wkvq], c == 0, False)
                        ins = add_bias(bank, g)
                    if kind == "KT":
                        n, = a
                        pe.wait_ge(k_normed, n + 1)
                        for kt in range(KT_):
                            ins = pe.transpose(bank[:, kt * P:(kt + 1) * P], kraw[:, kt, (n % 4) * HD:(n % 4 + 1) * HD], ident[:])
                    if kind == "QT":
                        n, qt = a
                        pe.wait_ge(q_normed, n + 1)
                        for r in range(GR):
                            ins = pe.transpose(bank[:, r * P:(r + 1) * P], qraw[:, qt, r * P:(r + 1) * P], ident[:])
                    ins.then_inc(m_ps, 1)


            def gate(t):
                for c in range(C):
                    ins = pe.matmul(ps[7][:, t * EW:t * EW + NE], xn3T[:, c, t * P:(t + 1) * P], gw[:, c, 0:NE],
                                    start=c == 0, stop=c == C - 1)
                return ins

            pe.wait_ge(ld_gate, 16)
            pe.wait_ge(x3_T, B - 1)
            for t in range(NT - TB):
                gate(t)
            turn_mixture_rows(ps[0], B - 1).then_inc(x3_ps, 1)
            pe.wait_ge(x3_T, B)
            for t in range(NT - TB, NT):
                ins = gate(t)
            ins.then_inc(gate_ps, 1)
            pe.wait_ge(ld_shared, 32)

            def up(i, par, lhs, e):
                for c in range(C):
                    ins = pe.matmul(ps[2 + par][:, 0:2 * INTER], lhs[c], w13[:, e, c, :], start=c == 0, stop=c == C - 1)
                ins.then_inc(up_ps, 1)

            def turn_hidden(i, par):
                pe.wait_ge(hh_ready, i + 1)
                for c in range(2):
                    ins = pe.transpose(ps[4 + par][0:IH, c * P:(c + 1) * P], hh[:, par, c * IH:(c + 1) * IH], ident[:])
                ins.then_inc(h_ps, 1)

            def down(i, par, e):
                pe.wait_ge(hT_ready, i + 1)
                for c in range(2):
                    ins = pe.matmul(ps[6 + par][:, 0:D], hT[:, par, c, :], w2s[:, e, c, :], start=c == 0, stop=c == 1)
                ins.then_inc(y_ps, 1)

            def turn_rows(j, par, buf, ld):
                pe.wait_ge(xg_ld[buf], ld)
                for c in range(C):
                    ins = pe.transpose(ps[par][:, c * P:(c + 1) * P], xg[:, buf, c * P:(c + 1) * P], ident[:])
                ins.then_inc(xg_ps, 1)

            pe.wait_ge(chosen_ready, 1)
            flat = chosen[:].rearrange("p t e -> p (t e)")
            pe.matmul(ps[0][:, 0:P], upper[:], flat, start=True, stop=True)
            pe.matmul(ps[0][:, P:2 * P], onesf[:], flat, start=True, stop=True).then_inc(rank_ps, 1)
            for i in range(LEAD):
                if i >= 2:
                    pe.wait_ge(hh_ready, i - 1)
                up(i, i % 2, [xn3T[:, c, i * P:(i + 1) * P] for c in range(C)], NE)
                if i >= 1:
                    if i >= 3:
                        pe.wait_ge(y_read, i - 2)
                    down(i - 1, (i - 1) % 2, NE)
                turn_hidden(i, i % 2)

            pe.wait_ge(slots_ready, 2)
            pe.wait_ge(ld_e, 16 * 6)

            def experts_of(k):
                word = pe.value_load(expi[0:1, bass.ds(k, 1)], min_val=0, max_val=EW ** (XG + 2) - 1)
                return [word // EW ** i % EW for i in range(XG + 2)]

            def routed_up(j, par, e):
                pe.wait_ge(xgT_ready, j + 1)
                pe.wait_ge(hh_ready, j + (LEAD - 1))
                for c in range(C):
                    ins = pe.matmul(ps[2 + par][:, 0:2 * INTER], xgT[:, par, c, :],
                                    w13[:, bass.ds(e, 1), c, :].rearrange("p e n -> p (e n)"), start=c == 0, stop=c == C - 1)
                ins.then_inc(up_ps, 1)

            def routed_rest(j, par, e_before, buf, ld):
                if buf is not None:
                    turn_rows(j + 1, 1 - par, buf, ld)
                pe.wait_ge(y_read, j + (LEAD - 2))
                pe.wait_ge(hT_ready, j + LEAD)
                for c in range(2):
                    if e_before is None:
                        rhs = w2s[:, NE, c, :]
                    else:
                        rhs = w2s[:, bass.ds(e_before, 1), c, :].rearrange("p e n -> p (e n)")
                    ins = pe.matmul(ps[7 - par][:, 0:D], hT[:, 1 - par, c, :], rhs, start=c == 0, stop=c == 1)
                ins.then_inc(y_ps, 1)
                turn_hidden(j + LEAD, par)

            turn_rows(0, 0, 0, 16)
            e = experts_of(0)
            routed_up(0, 0, e[0])
            routed_rest(0, 0, None, 1, 16)
            routed_up(1, 1, e[1])
            with pe.Fori(0, NSLOT // XG) as k:
                e = experts_of(k)
                for i in range(1, XG + 1):
                    buf = (i + 1) % XG
                    routed_rest(XG * k + i, i % 2, e[i - 1], buf, 16 * (k + 1 + (i + 1) // XG))
                    routed_up(XG * k + i + 1, (i + 1) % 2, e[i + 1])
            last = NSLOT - 1
            e = experts_of(last // XG)
            routed_rest(last, 1, e[0], None, None)
            for i in range(LEAD + NSLOT, NT + NSLOT):
                t = i - NSLOT
                pe.wait_ge(hh_ready, i - 1)
                up(i, i % 2, [xn3T[:, c, t * P:(t + 1) * P] for c in range(C)], NE)
                pe.wait_ge(y_read, i - 2)
                if i == LEAD + NSLOT:
                    pe.wait_ge(hT_ready, i)
                    for c in range(2):
                        ins = pe.matmul(ps[7][:, 0:D], hT[:, 1, c, :], w2s[:, bass.ds(e[1], 1), c, :].rearrange("p e n -> p (e n)"),
                                        start=c == 0, stop=c == 1)
                    ins.then_inc(y_ps, 1)
                else:
                    down(i - 1, (i - 1) % 2, NE)
                turn_hidden(i, i % 2)
            pe.wait_ge(y_read, NT + NSLOT - 2)
            down(NT + NSLOT - 1, (NT + NSLOT - 1) % 2, NE)


_INS = ["x", "ctx_2048", "mask_1xSxS2_ff0"] + ["L0_attn_" + n for n in (
    "W_DKV", "b_DKV", "W_UK", "b_UK", "W_UV", "b_UV", "W_DQ", "b_DQ", "W_UQ", "b_UQ", "W_QR", "b_QR", "W_KR", "b_KR")] + [
    "L0_xattn_" + n for n in ("Wq", "bq", "Wk", "bk", "Wv", "bv", "Wo", "qn_w", "kn_w")]


def rope_table():
    f32 = np.float32
    freqs = f32(10000.0) ** (-(np.arange(0, DR, 2, dtype=f32) / f32(DR)))
    theta = np.arange(T, dtype=f32)[:, None] * freqs[None, :]
    cos, sin = np.cos(theta), np.sin(theta)
    rows = np.stack([np.stack([cos, sin], -1).reshape(T, DR), np.stack([sin, cos], -1).reshape(T, DR)], 1)
    return np.ascontiguousarray(rows.reshape(TB, P, 2, DR).transpose(1, 0, 2, 3).astype(f32))


def kernel(**inputs):
    import concourse.bacc as bacc
    from concourse.bass_utils import run_bass_kernel_spmd

    nc = bacc.Bacc("TRN2", target_bir_lowering=False, num_devices=1)
    arrays, args = {}, []

    def give(name, a):
        arrays[name] = a
        args.append(nc.dram_tensor(name, a.shape, mybir.dt.from_np(a.dtype), kind="ExternalInput").ap())

    for name in _INS:
        give(f"in_{name}", np.ascontiguousarray(inputs[name]))
    f = {n: inputs["L0_ffn_" + n] for n in ("gate_w", "w1", "w2", "w3", "sw1", "sw2", "sw3")}
    give("gate_wT", np.ascontiguousarray(f["gate_w"].T))
    w1, w3, w2 = (np.concatenate([f[n], f["s" + n][None]]) for n in ("w1", "w3", "w2"))
    give("w13T", np.ascontiguousarray(np.concatenate([w1, w3], 1).transpose(0, 2, 1)))
    give("w2T", np.ascontiguousarray(w2.transpose(0, 2, 1)))
    give("rope_cs", rope_table())
    args.append(nc.dram_tensor("out_0", (B, T, D), F32, kind="ExternalOutput").ap())
    layer(nc, *args)
    r = run_bass_kernel_spmd(nc, [arrays], core_ids=[0])
    return r.results[0]["out_0"]
```
